# Optimizing a Trainium2 kernel written in Bass

```python
import numpy as np
import jax
import jax.numpy as jnp

def _softmax(x, axis=-1):
    return jax.nn.softmax(x, axis=axis)

def _gelu(x):
    return jax.nn.gelu(x, approximate=True)

def _silu(x):
    return jax.nn.silu(x)

def _sigmoid(x):
    return jax.nn.sigmoid(x)

def _layernorm(x, axis=-1, eps=1e-05):
    m = jnp.mean(x, axis=axis, keepdims=True)
    v = jnp.var(x, axis=axis, keepdims=True)
    return (x - m) / jnp.sqrt(v + eps)

def _scatter_add(tgt, idx, src, axis=0):
    return tgt.at[idx].add(src)

def _segment_sum(src, seg, n):
    return jax.ops.segment_sum(src, seg, n)
kernel_name = 'mk_conv_attn_hybrid_d2_conv_nchw256_r2_dcbaa4'

def setup_inputs(seed: int=0):
    np.random.seed(seed)
    _w = jnp.asarray

    def _rec_inputs():
        import jax
        import jax.numpy as jnp
        _gk = jax.random.key(seed)
        x = -0.0002928 + 1 * jax.random.normal(jax.random.fold_in(_gk, 1), (4, 128, 32, 32), jnp.float32)
        return x
    x = _rec_inputs()

    def _L0_conv_setup():
        import jax, jax.numpy as jnp
        import numpy as np
        B, C, H, W = (4, 128, 32, 32)
        DQK = C // 8
        key = jax.random.key(seed)
        ks = jax.random.split(key, 8)
        std = 1.0 / np.sqrt(C)
        x = jax.random.normal(ks[0], (B, C, H, W), dtype=jnp.float32)
        Wq = jax.random.normal(ks[1], (DQK, C), dtype=jnp.float32) * std
        bq = jnp.zeros((DQK,), dtype=jnp.float32)
        Wk = jax.random.normal(ks[2], (DQK, C), dtype=jnp.float32) * std
        bk = jnp.zeros((DQK,), dtype=jnp.float32)
        Wv = jax.random.normal(ks[3], (C, C), dtype=jnp.float32) * std
        bv = jnp.zeros((C,), dtype=jnp.float32)
        gamma = jax.random.normal(ks[4], (1,), dtype=jnp.float32) * 0.1
        return {'x': x, 'Wq': Wq, 'bq': bq, 'Wk': Wk, 'bk': bk, 'Wv': Wv, 'bv': bv, 'gamma': gamma}
    _L0_conv_all = _L0_conv_setup()
    _L0_conv_in = {k: v for k, v in _L0_conv_all.items() if k in ('Wq', 'bq', 'Wk', 'bk', 'Wv', 'bv', 'gamma')}
    del _L0_conv_all

    def _L1_attn_setup():
        import jax, jax.numpy as jnp
        import numpy as np
        B, N, DIM, H, R = (8, 2048, 128, 8, 32)
        key = jax.random.key(seed)
        k0, k1, k2, k3 = jax.random.split(key, 4)
        x = jax.random.normal(k0, (B, N, DIM), jnp.float32)
        qkv_w = jax.random.normal(k1, (DIM, 2 * H * DIM), jnp.float32) * 0.02
        qkv_b = jnp.zeros((2 * H * DIM,), jnp.float32)
        lunchbox = jax.random.normal(k2, (DIM, R), jnp.float32) * (1.0 / np.sqrt(DIM))
        proj_w = jax.random.normal(k3, (H * DIM, DIM), jnp.float32) * 0.02
        proj_b = jnp.zeros((DIM,), jnp.float32)
        return dict(x=x, qkv_w=qkv_w, qkv_b=qkv_b, lunchbox=lunchbox, proj_w=proj_w, proj_b=proj_b)
    _L1_attn_all = _L1_attn_setup()
    _L1_attn_in = {k: v for k, v in _L1_attn_all.items() if k in ('qkv_w', 'qkv_b', 'lunchbox', 'proj_w', 'proj_b')}
    del _L1_attn_all

    def _L1_ffn_setup():
        import jax, jax.numpy as jnp
        import numpy as np
        N_EXPERTS = 8
        TOP_K = 2
        key = jax.random.key(seed)
        ks = jax.random.split(key, 5)
        B, T, C, E, H = (8, 1024, 128, 8, 341)
        scale = 1.0 / np.sqrt(C)
        return {'x': jax.random.normal(ks[0], (B, T, C), dtype=jnp.float32), 'router_w': jax.random.normal(ks[1], (E, C), dtype=jnp.float32) * scale, 'w1': jax.random.normal(ks[2], (E, H, C), dtype=jnp.float32) * scale, 'w2': jax.random.normal(ks[3], (E, C, H), dtype=jnp.float32) * (1.0 / np.sqrt(H)), 'w3': jax.random.normal(ks[4], (E, H, C), dtype=jnp.float32) * scale}
    _L1_ffn_all = _L1_ffn_setup()
    _L1_ffn_in = {k: v for k, v in _L1_ffn_all.items() if k in ('router_w', 'w1', 'w2', 'w3')}
    del _L1_ffn_all
    return {'x': x, 'L0_conv_Wq': _L0_conv_in['Wq'], 'L0_conv_bq': _L0_conv_in['bq'], 'L0_conv_Wk': _L0_conv_in['Wk'], 'L0_conv_bk': _L0_conv_in['bk'], 'L0_conv_Wv': _L0_conv_in['Wv'], 'L0_conv_bv': _L0_conv_in['bv'], 'L0_conv_gamma': _L0_conv_in['gamma'], 'L1_attn_qkv_w': _L1_attn_in['qkv_w'], 'L1_attn_qkv_b': _L1_attn_in['qkv_b'], 'L1_attn_lunchbox': _L1_attn_in['lunchbox'], 'L1_attn_proj_w': _L1_attn_in['proj_w'], 'L1_attn_proj_b': _L1_attn_in['proj_b'], 'L1_ffn_router_w': _L1_ffn_in['router_w'], 'L1_ffn_w1': _L1_ffn_in['w1'], 'L1_ffn_w2': _L1_ffn_in['w2'], 'L1_ffn_w3': _L1_ffn_in['w3']}

def reference(x, L0_conv_Wq, L0_conv_bq, L0_conv_Wk, L0_conv_bk, L0_conv_Wv, L0_conv_bv, L0_conv_gamma, L1_attn_qkv_w, L1_attn_qkv_b, L1_attn_lunchbox, L1_attn_proj_w, L1_attn_proj_b, L1_ffn_router_w, L1_ffn_w1, L1_ffn_w2, L1_ffn_w3):
    import jax
    import jax.numpy as jnp

    def _L0_conv_ref(x, Wq, bq, Wk, bk, Wv, bv, gamma):
        import jax, jax.numpy as jnp
        import numpy as np
        B, C, H, W = (4, 128, 32, 32)
        DQK = C // 8
        b, c, h, w = x.shape
        n = h * w
        xf = x.reshape(b, c, n)
        q = jnp.einsum('oc,bcn->bno', Wq, xf) + bq
        k = jnp.einsum('oc,bcn->bon', Wk, xf) + bk[:, None]
        v = jnp.einsum('oc,bcn->bon', Wv, xf) + bv[:, None]
        scale = jnp.sqrt(jnp.asarray(DQK, dtype=x.dtype))
        attn = jax.nn.softmax(jnp.einsum('bnd,bdm->bnm', q, k) / scale, axis=-1)
        out = jnp.einsum('bcm,bnm->bcn', v, attn)
        out = out.reshape(b, c, h, w)
        return gamma[0] * out + x

    def _L1_attn_ref(x, qkv_w, qkv_b, lunchbox, proj_w, proj_b):
        import jax, jax.numpy as jnp
        import numpy as np
        B, N, DIM, H, R = (8, 2048, 128, 8, 32)
        Bsz, Nseq, C = x.shape
        D, Rr = lunchbox.shape
        Hh = qkv_w.shape[1] // (2 * D)
        scale = max(D, Rr) ** (-0.5)
        h = x @ qkv_w + qkv_b
        h = jnp.transpose(h, (0, 2, 1)).reshape(Bsz, 2, Hh, D, Nseq)
        q, v = (h[:, 0], h[:, 1])
        attn = jnp.einsum('bhdn,dr->bhrd', q, lunchbox) * scale
        res = jnp.einsum('bhrd,bhdn->bhnd', attn, v)
        out = res.reshape(Bsz, Nseq, Hh * D) @ proj_w + proj_b
        return out

    def _L1_ffn_ref(x, router_w, w1, w2, w3):
        import jax, jax.numpy as jnp
        import numpy as np
        N_EXPERTS = 8
        TOP_K = 2
        B, T, C = x.shape
        flat = x.reshape(-1, C)
        logits = flat @ router_w.T
        probs = jax.nn.softmax(logits, axis=-1)
        topk_probs, topk_idx = jax.lax.top_k(probs, TOP_K)
        topk_probs = topk_probs / (jnp.sum(topk_probs, axis=-1, keepdims=True) + 1e-09)
        onehot = jax.nn.one_hot(topk_idx, N_EXPERTS, dtype=flat.dtype)
        gates = jnp.einsum('nk,nke->ne', topk_probs, onehot)
        h1 = jnp.einsum('nc,ehc->neh', flat, w1)
        h3 = jnp.einsum('nc,ehc->neh', flat, w3)
        h = jax.nn.silu(h1) * h3
        y = jnp.einsum('neh,ech->nec', h, w2)
        out = jnp.einsum('ne,nec->nc', gates, y)
        return out.reshape(B, T, C)

    def _gn(v, G=32, eps=1e-05):
        B_, C_, H_, W_ = v.shape
        g = v.reshape(B_, G, C_ // G, H_, W_)
        m = jnp.mean(g, axis=(2, 3, 4), keepdims=True)
        s = jnp.var(g, axis=(2, 3, 4), keepdims=True)
        return ((g - m) / jnp.sqrt(s + eps)).reshape(v.shape)

    def _ln_c(v, eps=1e-06):
        m = jnp.mean(v, axis=1, keepdims=True)
        s = jnp.var(v, axis=1, keepdims=True)
        return (v - m) / jnp.sqrt(s + eps)

    def _ln_t(v, eps=1e-05):
        m = jnp.mean(v, axis=-1, keepdims=True)
        s = jnp.var(v, axis=-1, keepdims=True)
        return (v - m) / jnp.sqrt(s + eps)

    def _to_tokens(v):
        B_, C_, H_, W_ = v.shape
        return v.reshape(B_, C_, H_ * W_).transpose(0, 2, 1)

    def _from_tokens(t, like):
        B_, C_, H_, W_ = like.shape
        return t.transpose(0, 2, 1).reshape(B_, C_, H_, W_)
    x = _L0_conv_ref(x, L0_conv_Wq, L0_conv_bq, L0_conv_Wk, L0_conv_bk, L0_conv_Wv, L0_conv_bv, L0_conv_gamma)
    t = _to_tokens(x)
    t = t + _L1_attn_ref(_ln_t(t), L1_attn_qkv_w, L1_attn_qkv_b, L1_attn_lunchbox, L1_attn_proj_w, L1_attn_proj_b)
    t = t + _L1_ffn_ref(_ln_t(t), L1_ffn_router_w, L1_ffn_w1, L1_ffn_w2, L1_ffn_w3)
    x = _from_tokens(t, x)
    return x

_drawn_inputs = setup_inputs


def setup_inputs(seed=0):
    import zlib

    import numpy as np

    out = dict(_drawn_inputs(seed))
    spreads = {'L0_conv_bq': (0.0, 1.247),
     'L0_conv_bk': (0.0, 2.0),
     'L0_conv_bv': (0.0, 0.1),
     'L1_attn_qkv_b': (0.0, 0.1),
     'L1_attn_proj_b': (0.0, 0.1)}
    factors = {}
    for name, (base, spread) in spreads.items():
        noise = np.random.default_rng([zlib.crc32(name.encode()), seed]).standard_normal(out[name].shape)
        drawn = base * np.exp(spread * noise) if base else spread * noise
        out[name] = jnp.asarray(drawn.astype(out[name].dtype))
    for name, factor in factors.items():
        out[name] = (out[name] * factor).astype(out[name].dtype)
    return out
```

```python
from contextlib import ExitStack

import concourse.bass as bass
from concourse import mybir

ALU = mybir.AluOpType
ACT = mybir.ActivationFunctionType
AX_X = mybir.AxisListType.X
F32 = mybir.dt.float32
F32R = mybir.dt.float32r
BF16 = mybir.dt.bfloat16
I32 = mybir.dt.int32

P = 128

C_IDENT = 0
C_LOW = 128
C_RANK = 129
C_BASE = 137
C_TILE = 145
FFN_MAX = 72
C_ROW = C_TILE + FFN_MAX
C_DIGIT = C_ROW + 1
C_COLS = C_DIGIT + FFN_MAX


class Uses:

    def __init__(self, filled, drained, total, **first):
        self.filled, self.drained, self.total, self.first = filled, drained, total, first

    def before(self, i, use, n=0):
        return i * self.total + (self.first[use] + n + 1)

    def after(self, i, use, n=0):
        return i * self.total + (self.first[use] + n + 2)

    def full(self, i, use, n=0):
        return i * self.total + (self.first[use] + n + 1)


def conv_attn_moe_kernel(nc, x, cst, tri, tokid, pad_ids, wqk, bqk, wvT, bvB, gammaB, wq, bq, lunch, wvD, bvD, wp, bpB,
                         routerT, w13, w2T, out):
    IMAGES, C, N = x.shape
    TILES = N // P
    TOKENS = IMAGES * N
    DQK = 16
    STACK = 4 * DQK
    HEADS = wp.shape[1]
    EXPERTS = routerT.shape[1]
    HID2 = w13.shape[2]
    HID = HID2 // 2
    CHUNK = -(-HID // 3)
    REGION = TOKENS
    FFN_TILES = 2 * TOKENS // P + EXPERTS
    assert FFN_TILES == FFN_MAX
    RESULTS = 2 * TOKENS + 2 * EXPERTS * P
    SLOTS8 = 8
    GROUPS = FFN_TILES // SLOTS8
    AHEAD = 6
    H13 = 170
    W_A = HID2 // 2 + 1
    SLOTS = pad_ids.shape[0] * pad_ids.shape[1]
    PAIRS = IMAGES // 2
    HALF = N // 2
    VCOLS = C + 1

    ids_dram = nc.dram_tensor("ids_dram", [SLOTS, 1], I32, kind="Internal").ap()
    ln2_dram = nc.dram_tensor("ln2_dram", [TOKENS, C], F32, kind="Internal").ap()

    y_dram = nc.dram_tensor("y_dram", [RESULTS, C], F32, kind="Internal").ap()

    with ExitStack() as ctx:
        def sb(name, shape, dt=F32):
            return ctx.enter_context(nc.sbuf_tensor(name + "_sb", shape, dt))

        def psum(name, shape):
            return ctx.enter_context(nc.psum_tensor(name, shape, F32))

        def sem(name):
            return ctx.enter_context(nc.semaphore(name))

        cst_s = sb("cst_s", [P, C_COLS])
        tri_s = sb("tri_s", [P, 2 * P], BF16)
        wqk_s = sb("wqk_s", [P, P])
        wvT_s = sb("wvT_s", [P, C])
        vec_s = sb("vec_s", [P, 2])
        bvB_s = sb("bvB_s", [P, C])
        wq_s = sb("wq_s", [P, HEADS * P])
        bq_s = sb("bq_s", [P, HEADS])
        lunch_s = sb("lunch_s", [P, lunch.shape[1]])
        wvD_s = sb("wvD_s", [P, HEADS, C])
        bvD_s = sb("bvD_s", [P, HEADS])
        wp_s = sb("wp_s", [P, HEADS, C])
        bpB_s = sb("bpB_s", [P, C])
        routerT_s = sb("routerT_s", [P, EXPERTS])
        w13_hi = sb("w13_hi", [P, EXPERTS, HID2], F32R)
        w13_lo = sb("w13_lo", [P, EXPERTS, HID2], F32R)
        w2_s = sb("w2_s", [CHUNK, 3, EXPERTS, C])

        xc = [sb(f"xc{b}", [P, N]) for b in range(2)]
        qk_sum = sb("qk_sum", [P, N])
        qk_hi = sb("qk_hi", [P, N], F32R)
        q_stack = [sb(f"q_stack{b}", [STACK + 2, N], F32R) for b in range(2)]
        k_stack = [sb(f"k_stack{b}", [STACK + 2, N], F32R) for b in range(2)]
        gbv = sb("gbv", [P, C])
        v_ext = [sb(f"v_ext{b}", [P, TILES, VCOLS]) for b in range(2)]
        xt = [sb(f"xt{b}", [P, TILES, C]) for b in range(2)]
        row_max2 = sb("row_max2", [P, TILES, 2])
        neg_max = sb("neg_max", [P, TILES])
        neg_max_hi = sb("neg_max_hi", [P, TILES], F32R)
        max_cols = sb("max_cols", [P, TILES, STACK + 2])
        probs = sb("probs", [P, TILES, N])
        rden = sb("rden", [P, TILES])
        t1 = sb("t1", [P, TILES, C])
        stats = sb("stats", [P, TILES, 6])
        mean_var = sb("mean_var", [P, TILES, 2])
        var_eps = sb("var_eps", [P, TILES])
        minus_half = sb("minus_half", [P, TILES])
        rstd = sb("rstd", [P, TILES])
        ln1 = sb("ln1", [P, TILES, C])
        lnT = sb("lnT", [P, N])
        ln1_sum = sb("ln1_sum", [P, 2])
        nbq = sb("nbq", [P, HEADS])
        lunch_sum = sb("lunch_sum", [P, 1])
        qsum = sb("qsum", [P, HEADS])
        g_head = sb("g_head", [P, HEADS])
        g_wv = sb("g_wv", [P, HEADS, C])
        g_bv = sb("g_bv", [P, HEADS])
        wp_sum = sb("wp_sum", [P, C])
        t2 = sb("t2", [P, IMAGES * TILES, C])
        w13_raw = t2[:].rearrange("p n c -> p (n c)")[:, (IMAGES * TILES - 11) * C:(IMAGES * TILES - 11) * C + 2 * HID2].rearrange("p (b h) -> p b h", b=2)
        ln2 = [sb(f"ln2_{b}", [P, TILES, C]) for b in range(2)]
        small = sb("small", [P, 8, TILES])
        logit = sb("logit", [P, TILES, EXPERTS])
        prob = sb("prob", [P, TILES, EXPERTS])
        tie = sb("tie", [P, TILES, EXPERTS])
        pick = sb("pick", [P, 2, TILES, EXPERTS])
        both = sb("both", [P, TILES, EXPERTS], BF16)
        gates = sb("gates", [P, 2, IMAGES * TILES])
        base = sb("base", [P, EXPERTS])
        slots = [sb(f"slots{b}", [P, 2 * TILES], I32) for b in range(2)]
        tok = [sb(f"tok{b}", [P, 2 * TILES], I32) for b in range(2)]

        counts = sb("counts", [P, EXPERTS])
        counts_i = sb("counts_i", [P, EXPERTS], I32)
        n_tiles = sb("n_tiles", [P, EXPERTS])
        ends = sb("ends", [P, EXPERTS])
        past = sb("past", [1, FFN_TILES, EXPERTS])
        ended = sb("ended", [P, EXPERTS])
        tile_at = sb("tile_at", [P, 3])
        tile_row = sb("tile_row", [P, 1], I32)
        expert_f = sb("expert_f", [1, FFN_TILES])
        word_f = sb("word_f", [1, GROUPS])
        table = sb("table", [1, 1 + GROUPS], I32)
        ids_rows = sb("ids_rows", [FFN_TILES, P], I32)
        ids_rows_f = sb("ids_rows_f", [FFN_TILES, P])
        ids = sb("ids", [P, FFN_TILES], I32)
        id_slot = sb("id_slot", [P, SLOTS8], I32)
        tok_slot = sb("tok_slot", [P, SLOTS8], I32)
        x_hi = [sb(f"x_hi{b}", [P, P], F32R) for b in range(2)]
        x_lo = [sb(f"x_lo{b}", [P, P], F32R) for b in range(2)]
        spare, used = probs[:].rearrange("p m n -> p (m n)"), [0]

        def place(cols):
            used[0] += cols
            assert used[0] <= TILES * N
            return spare[:, used[0] - cols:used[0]]

        x_rows = [place(C) for _ in range(SLOTS8)]
        y_rows = [place(C) for _ in range(SLOTS8)]
        silu1 = [place(HID) for _ in range(2)]
        hidden = [place(3 * CHUNK) for _ in range(2)]
        hiddenT = [place(3 * P).rearrange("p (k n) -> p k n", n=P) for _ in range(2)]
        y_in = [[place(4 * C).rearrange("p (n c) -> p n c", c=C) for _ in range(2)] for _ in range(2)]
        y_out = [place(4 * P) for _ in range(2)]
        mixed = [spare[:, 4 * C * b:4 * C * (b + 1)].rearrange("p (n c) -> p n c", c=C) for b in range(2)]

        bank_a = [psum(f"bank_a{h}", [P, 512]) for h in range(2)]
        bank_s = [psum(f"bank_s{h}", [P, N]) for h in range(2)]
        bank_c = [psum(f"bank_c{h}", [P, 512]) for h in range(2)]

        loaded = {n: sem(f"{n}_loaded") for n in ("cst", "wqk", "wv", "attn", "router", "w2", "tok")}
        x_loaded, w13_loaded = [sem(f"x_loaded{b}") for b in range(2)], [sem(f"w13_loaded{b}") for b in range(2)]
        w13_split = sem("w13_split")
        ids_cleared = sem("ids_cleared")
        consts_made, pool_made = sem("consts_made"), sem("pool_made")
        A = [Uses(sem(f"a_filled{h}"), sem(f"a_drained{h}"), 4 + TILES,
                  qk=0, v=1, xt=2, scores=3, rows=3 + TILES) for h in range(2)]
        S = [Uses(sem(f"s_filled{h}"), sem(f"s_drained{h}"), TILES // 2 + HEADS // 2,
                  scores=0, weff=TILES // 2) for h in range(2)]
        K = TILES // 2
        Cb = [Uses(sem("c_filled0"), sem("c_drained0"), K + 5,
                   pv=0, ln1=K, qsum=K + 1, attn=K + 2, ln2=K + 3, route=K + 4),
              Uses(sem("c_filled1"), sem("c_drained1"), K + 4,
                   pv=0, ln1=K, attn=K + 1, ln2=K + 2, rank=K + 3)]
        stack_step, max_step = sem("stack_step"), sem("max_step")
        norm_step, gate_step = sem("norm_step"), sem("gate_step")
        rstd_ready, exp_ready = sem("rstd_ready"), sem("exp_ready")
        ln2_stored = [sem(f"ln2_stored{b}") for b in range(2)]
        ids_stored = [sem(f"ids_stored{b}") for b in range(2)]
        STACK_STEPS, MAX_STEPS, NORM_STEPS, GATE_STEPS = 3, 4, 11, 25
        LN1_STEP, WPG_STEP, BOTH_STEP = 4, 7, 21
        setup, den_ready, tok_step, bias_added = sem("setup"), sem("den_ready"), sem("tok_step"), sem("bias_added")
        weff = probs[:].rearrange("p k (h c) -> p k h c", c=C)

        table_ready, table_step = sem("table_ready"), sem("table_step")
        rows_ready, ids_loaded, ids_exact, ids_turned = sem("rows_ready"), sem("ids_loaded"), sem("ids_exact"), sem("ids_turned")
        ids_ready = sem("ids_ready")
        slot_ready = sem("slot_ready")
        gathered = [sem(f"gathered{k}") for k in range(SLOTS8)]
        scattered = [sem(f"scattered{k}") for k in range(SLOTS8)]
        x_turned, x_hi_ready, x_lo_ready = sem("x_turned"), sem("x_hi_ready"), sem("x_lo_ready")
        h13_ready, silu_ready, hidden_ready = sem("h13_ready"), sem("silu_ready"), sem("hidden_ready")
        hidden_turned, hiddenT_ready = sem("hidden_turned"), sem("hiddenT_ready")
        y_ready, y_kept, hidden_pad = sem("y_ready"), sem("y_kept"), sem("hidden_pad")
        y_loaded, y_mixed = [sem(f"y_loaded{b}") for b in range(2)], [sem(f"y_mixed{b}") for b in range(2)]
        mix_step, waits_passed = sem("mix_step"), sem("waits_passed")
        mix_turned, out_kept = [sem(f"mix_turned{b}") for b in range(2)], [sem(f"out_kept{b}") for b in range(2)]
        out_stored = [sem(f"out_stored{b}") for b in range(2)]

        def experts_loop(eng, tile, begin=lambda g: None):
            begin(0)
            for t in range(SLOTS8):
                tile(t, t)
            with eng.Fori(1, GROUPS - 1) as g:
                begin(g)
                for k in range(SLOTS8):
                    tile(g * SLOTS8 + k, k)
            begin(GROUPS - 1)
            for k in range(SLOTS8):
                tile((GROUPS - 1) * SLOTS8 + k, k)

        def wait_apart(eng, s, value):
            eng.wait_ge(s, value)
            eng.sem_inc(waits_passed, 1)

        def at_least(eng, s, value):
            if not isinstance(value, int) or value > 0:
                eng.wait_ge(s, value)

        def gathered_value(t, k):
            return (t - k) * (16 // SLOTS8) + 16

        scattered_value = gathered_value

        ident = cst_s[:, C_IDENT:C_IDENT + P]

        block = ctx.enter_context(nc.Block())

        @block.sync
        def _(sp):
            for b in range(2):
                sp.dma_start(xc[b][:], x[b]).then_inc(x_loaded[b], 16)
                if b == 0:
                    sp.dma_start(wqk_s[:], wqk).then_inc(loaded["wqk"], 16)
                    sp.dma_start(vec_s[:, 0:1], bqk).then_inc(loaded["wqk"], 16)
                    sp.dma_start(vec_s[:, 1:2], gammaB).then_inc(loaded["wqk"], 16)
                    sp.dma_start(cst_s[:], cst).then_inc(loaded["cst"], 16)
                    sp.dma_start(tri_s[:], tri).then_inc(loaded["cst"], 16)
                    sp.dma_start(wvT_s[:], wvT).then_inc(loaded["wv"], 16)
                    sp.dma_start(bvB_s[:], bvB).then_inc(loaded["wv"], 16)
            for dst, src in ((wq_s, wq), (bq_s, bq), (lunch_s, lunch), (wvD_s, wvD), (bvD_s, bvD), (wp_s, wp), (bpB_s, bpB)):
                sp.dma_start(dst[:], src).then_inc(loaded["attn"], 16)
            sp.dma_start(routerT_s[:], routerT).then_inc(loaded["router"], 16)
            for b in range(2):
                sp.dma_start(tok[b][:], tokid[b]).then_inc(loaded["tok"], 16)
            sp.dma_start(ids_dram.rearrange("(a b) c -> a (b c)", b=pad_ids.shape[1]), pad_ids).then_inc(ids_cleared, 16)
            for e in range(EXPERTS):
                if e >= 2:
                    sp.wait_ge(w13_split, 2 * (e - 1))
                sp.dma_start(w13_raw[:, e % 2], w13[:, e]).then_inc(w13_loaded[e % 2], 16)
            sp.dma_start(w2_s[:], w2T).then_inc(loaded["w2"], 16)

            def store_ln2(i, b):
                sp.wait_ge(norm_step, i * NORM_STEPS + NORM_STEPS)
                sp.dma_start(ln2_dram[bass.ds(i * N, N), :].rearrange("(n p) c -> p n c", p=P), ln2[b][:]).then_inc(ln2_stored[b], 16)

            def load_x(i, b):
                sp.wait_ge(A[1].filled, A[1].full(i - 2, "xt"))
                sp.dma_start(xc[b][:], x[bass.ds(i, 1)].rearrange("i c n -> c (i n)")).then_inc(x_loaded[b], 16)

            for b in range(2):
                load_x(2 + b, b)
            with sp.Fori(0, PAIRS) as pair:
                for b in range(2):
                    store_ln2(2 * pair + b, b)
            for b in range(2):
                sp.wait_ge(ln2_stored[b], 16 * PAIRS + 16)
            for k in range(SLOTS8):
                sp.wait_ge(scattered[k], 16 * GROUPS)
            with sp.Fori(0, IMAGES) as i:
                for b in range(2):
                    sp.wait_ge(y_mixed[b], i + 1)
                    for k in range(2):
                        rows = y_dram[bass.ds(i * N + (k * TOKENS + b * HALF), HALF), :]
                        sp.dma_start(y_in[b][k], rows.rearrange("(n p) c -> p n c", p=P)).then_inc(y_loaded[b], 16)
            for b in range(2):
                sp.wait_ge(out_stored[b], 16 * (IMAGES + 1))

        @block.tensor
        def _(pe):
            def mm(bank, lhsT, rhs, start=True, stop=True):
                return nc.tensor.matmul(bank, lhsT, rhs, start=start, stop=stop)

            def project(i, b):
                pe.wait_ge(x_loaded[b], i * 8 + (16 - 8 * b))
                for h in range(2):
                    pe.wait_ge(A[h].drained, A[h].before(i, "qk"))
                    mm(bank_a[h][:, :], wqk_s[:], xc[b][:, h * HALF:(h + 1) * HALF]).then_inc(A[h].filled, 1)
                for h in range(2):
                    pe.wait_ge(A[h].drained, A[h].before(i, "v"))
                    for j in range(4):
                        n = 4 * h + j
                        last = mm(bank_a[h][:, j * C:(j + 1) * C], xc[b][:, n * P:(n + 1) * P], wvT_s[:])
                    last.then_inc(A[h].filled, 1)
                for h in range(2):
                    pe.wait_ge(A[h].drained, A[h].before(i, "xt"))
                    for j in range(4):
                        n = 4 * h + j
                        last = nc.tensor.transpose(bank_a[h][:, j * C:(j + 1) * C], xc[b][:, n * P:(n + 1) * P], ident)
                    last.then_inc(A[h].filled, 1)

            def scores_by_query(i, b, n):
                if n == 0:
                    pe.wait_ge(stack_step, i * STACK_STEPS + (STACK_STEPS + 1))
                for h in range(2):
                    pe.wait_ge(A[h].drained, A[h].before(i, "scores", n))
                    mm(bank_a[h][:, :], q_stack[b][0:STACK, n * P:(n + 1) * P],
                       k_stack[b][0:STACK, h * HALF:(h + 1) * HALF]).then_inc(A[h].filled, 1)

            def max_rows(i, b):
                pe.wait_ge(max_step, i * MAX_STEPS + MAX_STEPS)
                for h in range(2):
                    pe.wait_ge(A[h].drained, A[h].before(i, "rows"))
                    for j in range(4):
                        last = nc.tensor.transpose(bank_a[h][0:STACK + 2, j * P:(j + 1) * P], max_cols[:, 4 * h + j, :], ident)
                    last.then_inc(A[h].filled, 1)

            def scores_by_key(i, b, m):
                if m == 0:
                    for h in range(2):
                        pe.wait_ge(A[h].drained, A[h].after(i, "rows"))
                s = S[m % 2]
                pe.wait_ge(s.drained, s.before(i, "scores", m // 2))
                for h in range(2):
                    last = mm(bank_s[m % 2][:, h * HALF:(h + 1) * HALF], k_stack[b][:, m * P:(m + 1) * P],
                              q_stack[b][:, h * HALF:(h + 1) * HALF])
                last.then_inc(s.filled, 1)

            def weigh_values(i, b, n):
                if n == 0:
                    for s in S:
                        pe.wait_ge(s.drained, s.after(i, "scores", TILES // 2 - 1))
                c = Cb[n % 2]
                pe.wait_ge(c.drained, c.before(i, "pv", n // 2))
                for m in range(TILES):
                    last = mm(bank_c[n % 2][:, 0:VCOLS], probs[:, m, n * P:(n + 1) * P], v_ext[b][:, m, :],
                              start=(m == 0), stop=(m == TILES - 1))
                last.then_inc(c.filled, 1)

            def turn(i, src, use):
                for h in range(2):
                    pe.wait_ge(Cb[h].drained, Cb[h].before(i, use))
                    for j in range(4):
                        last = nc.tensor.transpose(bank_c[h][:, j * C:(j + 1) * C], src[:, 4 * h + j, :], ident)
                    last.then_inc(Cb[h].filled, 1)

            def linear_attention(i, b):
                pe.wait_ge(norm_step, i * NORM_STEPS + LN1_STEP)
                turn(i, ln1, "ln1")
                for h in range(2):
                    pe.wait_ge(Cb[h].drained, Cb[h].after(i, "ln1"))
                for hd in range(HEADS):
                    last = mm(bank_c[0][:, 2 * hd:2 * hd + 2], wq_s[:, hd * P:(hd + 1) * P], ln1_sum[:, :])
                last.then_inc(Cb[0].filled, 1)
                pe.wait_ge(norm_step, i * NORM_STEPS + WPG_STEP)
                for hd in range(HEADS):
                    s = S[hd % 2]
                    pe.wait_ge(s.drained, s.before(i, "weff", hd // 2))
                    for h in range(2):
                        last = mm(bank_s[hd % 2][:, h * HALF:(h + 1) * HALF], g_wv[:, hd, :],
                                  wp_s[:, 4 * h:4 * h + 4, :].rearrange("p k c -> p (k c)"))
                    last.then_inc(s.filled, 1)
                for h in range(2):
                    pe.wait_ge(Cb[h].drained, Cb[h].before(i, "attn"))
                    for hd in range(4):
                        mm(bank_c[h][:, hd * C:(hd + 1) * C], g_bv[:, 4 * h + hd:4 * h + hd + 1].broadcast_to([P, P]),
                           wp_sum[:], start=(hd == 0), stop=False)
                for s in S:
                    pe.wait_ge(s.drained, s.after(i, "weff", HEADS // 2 - 1))
                for h in range(2):
                    for k in range(HEADS):
                        last = mm(bank_c[h][:, :], lnT[:, k:N:HEADS],
                                  weff[:, k, 4 * h:4 * h + 4, :].rearrange("p h c -> p (h c)"), start=False, stop=(k == HEADS - 1))
                    last.then_inc(Cb[h].filled, 1)

            def route(i, b):
                pe.wait_ge(norm_step, i * NORM_STEPS + NORM_STEPS)
                turn(i, ln2[b], "ln2")
                for h in range(2):
                    pe.wait_ge(Cb[h].drained, Cb[h].after(i, "ln2"))
                for n in range(TILES):
                    last = mm(bank_c[0][:, n * EXPERTS:(n + 1) * EXPERTS], lnT[:, n * P:(n + 1) * P], routerT_s[:])
                last.then_inc(Cb[0].filled, 1)

            def rank(i):
                pe.wait_ge(gate_step, i * GATE_STEPS + BOTH_STEP)
                pe.wait_ge(Cb[1].drained, Cb[1].before(i, "rank"))
                W = TILES * EXPERTS
                flat = both[:].rearrange("p n e -> p (n e)")
                mm(bank_c[1][:, 0:W], tri_s[:, 0:P], flat, stop=False)
                for n in range(1, TILES):
                    mm(bank_c[1][:, n * EXPERTS:W], tri_s[:, P:2 * P], flat[:, 0:W - n * EXPERTS], start=False, stop=False)
                for n in range(TILES):
                    last = mm(bank_c[1][:, W:W + EXPERTS], tri_s[:, P:2 * P], both[:, n, :], start=False, stop=(n == TILES - 1))
                last.then_inc(Cb[1].filled, 1)

            pe.wait_ge(loaded["wqk"], 48)
            pe.wait_ge(loaded["wv"], 32)
            pe.wait_ge(loaded["cst"], 32)
            pe.wait_ge(loaded["attn"], 16 * 7)
            pe.wait_ge(loaded["router"], 16)
            pe.wait_ge(consts_made, 7)
            pe.wait_ge(pool_made, 1)
            with pe.Fori(0, PAIRS) as pair:
                for b in range(2):
                    i = 2 * pair + b
                    project(i, b)
                    for n in range(TILES):
                        scores_by_query(i, b, n)
                    max_rows(i, b)
                    for m in range(TILES):
                        scores_by_key(i, b, m)
                    for n in range(TILES):
                        weigh_values(i, b, n)
                    linear_attention(i, b)
                    route(i, b)
                    rank(i)

            def turn_x(t, k):
                at_least(pe, x_lo_ready, t - 1)
                pe.wait_ge(gathered[k], gathered_value(t, k))
                nc.tensor.transpose(bank_a[k % 2][:, 0:P], x_rows[k], ident).then_inc(x_turned, 1)

            def hidden13(t, k, e):
                pe.wait_ge(x_lo_ready, t + 1)
                at_least(pe, hidden_ready, t - 1)
                hi, lo = x_hi[k % 2], x_lo[k % 2]
                for h, cols in enumerate((slice(0, W_A), slice(W_A, HID2))):
                    dst = bank_s[k % 2][:, H13 + cols.start:H13 + cols.stop]
                    for n, (x_part, w_part) in enumerate(((hi, w13_hi), (hi, w13_lo), (lo, w13_hi))):
                        last = mm(dst, x_part[:], w_part[:, bass.ds(e, 1), cols].rearrange("p a h -> p (a h)"), start=(n == 0), stop=(n == 2))
                last.then_inc(h13_ready, 1)

            def turn_hidden(t, k):
                pe.wait_ge(hidden_ready, t + 1)
                at_least(pe, hiddenT_ready, t)
                for c in range(3):
                    last = nc.tensor.transpose(bank_c[0][0:CHUNK, c * P:(c + 1) * P], hidden[k % 2][:, c * CHUNK:(c + 1) * CHUNK], ident)
                last.then_inc(hidden_turned, 1)

            def result(t, k, e):
                pe.wait_ge(hiddenT_ready, t + 1)
                at_least(pe, y_kept, t)
                for c in range(3):
                    rows = min(CHUNK, HID - c * CHUNK)
                    last = mm(bank_c[1][:, 0:C], hiddenT[k % 2][0:rows, c, :],
                              w2_s[0:rows, c, bass.ds(e, 1), :].rearrange("p a c -> p (a c)"), start=(c == 0), stop=(c == 2))
                last.then_inc(y_ready, 1)

            def tile(t, k):
                hidden13(t, k, experts[k + 2])
                if not isinstance(t, int) or t + 2 < FFN_TILES:
                    turn_x(t + 2, (k + 2) % SLOTS8)
                if not isinstance(t, int) or t >= 1:
                    turn_hidden(t - 1, (k - 1) % SLOTS8)
                if not isinstance(t, int) or t >= 2:
                    result(t - 2, (k - 2) % SLOTS8, experts[k])

            experts = []

            def load_experts(g):
                bits = (EXPERTS - 1).bit_length()
                words = nc.values_load_multi_w_load_instructions(table[0:1, bass.ds(g, 2)], engines=[mybir.EngineType.PE],
                                                                 min_val=0, max_val=EXPERTS ** SLOTS8 - 1)[1]
                digits = [(0, SLOTS8 - 2), (0, SLOTS8 - 1)] + [(1, j) for j in range(SLOTS8)]
                experts[:] = [(words[w] >> (bits * j)) & (EXPERTS - 1) for w, j in digits]

            pe.wait_ge(ids_exact, 1)
            nc.tensor.transpose(bank_c[1][:, 0:FFN_TILES], ids_rows_f[:], cst_s[0:FFN_TILES, C_IDENT:C_IDENT + FFN_TILES]).then_inc(ids_turned, 1)
            pe.wait_ge(table_ready, 1)
            pe.wait_ge(w13_split, 2 * EXPERTS)
            pe.wait_ge(loaded["w2"], 16)
            turn_x(0, 0)
            turn_x(1, 1)
            experts_loop(pe, tile, load_experts)
            turn_hidden(FFN_TILES - 1, SLOTS8 - 1)
            for t in (FFN_TILES - 2, FFN_TILES - 1):
                result(t, t % SLOTS8, experts[t - FFN_TILES])

            with pe.Fori(0, IMAGES) as i:
                for b in range(2):
                    pe.wait_ge(y_mixed[b], i + 2)
                    pe.wait_ge(out_kept[b], i + 1)
                    for j in range(4):
                        last = nc.tensor.transpose(bank_a[b][:, j * P:(j + 1) * P], mixed[b][:, j, :], ident)
                    last.then_inc(mix_turned[b], 1)

        @block.scalar
        def _(act):
            def stack_sums(i, b):
                for h in range(2):
                    act.wait_ge(A[h].filled, A[h].full(i, "qk"))
                    act.wait_ge(stack_step, i * STACK_STEPS + 1)
                    nc.scalar.activation(qk_sum[:, h * HALF:(h + 1) * HALF], bank_a[h][:, :], ACT.Identity,
                                         bias=vec_s[:, 0:1]).then_inc(A[h].drained, 1)

            def keep_xt(i, b):
                for h in range(2):
                    act.wait_ge(A[h].filled, A[h].full(i, "xt"))
                    nc.scalar.copy(xt[b][:, 4 * h:4 * h + 4, :], bank_a[h][:, :].rearrange("p (n c) -> p n c", c=C)).then_inc(A[h].drained, 1)

            def max_rows(i, b):
                for h in range(2):
                    act.wait_ge(A[h].filled, A[h].full(i, "rows"))
                    nc.scalar.copy(q_stack[b][STACK:STACK + 2, h * HALF:(h + 1) * HALF],
                                   bank_a[h][STACK:STACK + 2, :]).then_inc(A[h].drained, 1)

            def exps(i, b, m):
                s = S[m % 2]
                act.wait_ge(s.filled, s.full(i, "scores", m // 2))
                nc.scalar.activation(probs[:, m, :], bank_s[m % 2][:, :], ACT.Exp, scale=DQK ** -0.5).then_inc(s.drained, 1)

            def keep_ln1T(i):
                for h in range(2):
                    act.wait_ge(Cb[h].filled, Cb[h].full(i, "ln1"))
                    nc.scalar.activation(lnT[:, h * HALF:(h + 1) * HALF], bank_c[h][:, :], ACT.Identity,
                                         accum_out=ln1_sum[:, h:h + 1]).then_inc(Cb[h].drained, 1)

            def keep_weff(i):
                for hd in range(HEADS):
                    s = S[hd % 2]
                    act.wait_ge(s.filled, s.full(i, "weff", hd // 2))
                    nc.scalar.copy(weff[:, :, hd, :], bank_s[hd % 2][:, :].rearrange("p (k c) -> p k c", c=C)).then_inc(s.drained, 1)

            def keep_ln2T(i):
                for h in range(2):
                    act.wait_ge(Cb[h].filled, Cb[h].full(i, "ln2"))
                    nc.scalar.copy(lnT[:, h * HALF:(h + 1) * HALF], bank_c[h][:, :]).then_inc(Cb[h].drained, 1)

            def gate_exp(i):
                act.wait_ge(Cb[0].drained, Cb[0].after(i, "route"))
                nc.scalar.activation(prob[:].rearrange("p n e -> p (n e)"), logit[:].rearrange("p n e -> p (n e)"),
                                     ACT.Exp).then_inc(exp_ready, 1)

            act.wait_ge(loaded["wqk"], 48)
            with act.Fori(0, PAIRS) as pair:
                for b in range(2):
                    i = 2 * pair + b
                    stack_sums(i, b)
                    keep_xt(i, b)
                    max_rows(i, b)
                    for m in range(TILES):
                        exps(i, b, m)
                    keep_ln1T(i)
                    keep_weff(i)
                    keep_ln2T(i)
                    gate_exp(i)

            def silu(t, k):
                act.wait_ge(h13_ready, t + 1)
                at_least(act, hidden_ready, t - 1)
                nc.scalar.activation(silu1[k % 2], bank_s[k % 2][:, H13:H13 + HID], ACT.Silu).then_inc(silu_ready, 1)

            def high_part(t, k):
                act.wait_ge(x_turned, t + 1)
                at_least(act, h13_ready, t - 1)
                nc.scalar.copy(x_hi[k % 2][:], bank_a[k % 2][:, 0:P]).then_inc(x_hi_ready, 1)

            def keep_y(t, k):
                act.wait_ge(y_ready, t + 1)
                if not isinstance(t, int) or t >= SLOTS8:
                    act.wait_ge(scattered[k], scattered_value(t, k) - 16)
                nc.scalar.copy(y_rows[k], bank_c[1][:, 0:C]).then_inc(y_kept, 1)

            def tile(t, k):
                silu(t, k)
                if not isinstance(t, int) or t + 2 < FFN_TILES:
                    high_part(t + 2, (k + 2) % SLOTS8)
                if not isinstance(t, int) or t >= 2:
                    keep_y(t - 2, (k - 2) % SLOTS8)

            high_part(0, 0)
            high_part(1, 1)
            experts_loop(act, tile)
            for t in (FFN_TILES - 2, FFN_TILES - 1):
                keep_y(t, t % SLOTS8)

            with act.Fori(0, IMAGES) as i:
                for b in range(2):
                    act.wait_ge(mix_turned[b], i + 2)
                    act.wait_ge(out_stored[b], i * 16 + 16)
                    nc.scalar.copy(y_out[b], bank_a[b][:, :]).then_inc(out_kept[b], 1)
                    act.wait_ge(out_kept[b], i + 2)
                    act.dma_start(out[bass.ds(i, 1), :, b * HALF:(b + 1) * HALF].rearrange("i c n -> c (i n)"), y_out[b]).then_inc(out_stored[b], 16)

        @block.vector
        def _(dve):
            V = nc.vector

            def step(ins, s, start, n):
                ins.then_inc(s, 1)
                dve.wait_ge(s, start + n)

            def bcast_e(ap):
                return ap.unsqueeze(2).broadcast_to([P, TILES, EXPERTS])

            def make_stacks(i, b):
                s0 = i * STACK_STEPS + 1
                for h in range(2):
                    dve.wait_ge(A[h].drained, A[h].after(i, "qk"))
                step(V.tensor_copy(qk_hi[:], qk_sum[:]), stack_step, s0, 1)
                for k, (dst, lo) in enumerate(((q_stack[b], 0), (k_stack[b], STACK))):
                    rows = slice(lo, lo + STACK)
                    V.scalar_tensor_tensor(out=dst[0:STACK, :], in0=qk_hi[rows, :].bitcast(F32), scalar=cst_s[rows, C_LOW:C_LOW + 1],
                                           in1=qk_sum[rows, :], op0=ALU.mult, op1=ALU.add).then_inc(stack_step, 1)

            def keep_v(i, b):
                for h in range(2):
                    dve.wait_ge(A[h].filled, A[h].full(i, "v"))
                    for j in range(4):
                        last = V.scalar_tensor_tensor(out=v_ext[b][:, 4 * h + j, 0:C], in0=bank_a[h][:, j * C:(j + 1) * C],
                                                      scalar=vec_s[:, 1:2], in1=gbv[:], op0=ALU.mult, op1=ALU.add)
                    last.then_inc(A[h].drained, 1)

            def row_max(i, n):
                for h in range(2):
                    dve.wait_ge(A[h].filled, A[h].full(i, "scores", n))
                    V.reduce_max(row_max2[:, n, h:h + 1], bank_a[h][:, :], AX_X).then_inc(A[h].drained, 1)

            def negate_max(i):
                s0 = i * MAX_STEPS
                for h in range(2):
                    dve.wait_ge(A[h].drained, A[h].after(i, "scores", TILES - 1))
                step(V.tensor_reduce(neg_max[:], row_max2[:], AX_X, ALU.max, negate=True), max_step, s0, 1)
                step(V.tensor_copy(neg_max_hi[:], neg_max[:]), max_step, s0, 2)
                V.tensor_copy(max_cols[:, :, STACK], neg_max_hi[:].bitcast(F32)).then_inc(max_step, 1)
                V.tensor_tensor(max_cols[:, :, STACK + 1], neg_max[:], neg_max_hi[:].bitcast(F32), ALU.subtract).then_inc(max_step, 1)

            def attended(i, b, n):
                c = Cb[n % 2]
                dve.wait_ge(c.filled, c.full(i, "pv", n // 2))
                s0 = (i * TILES) + n
                V.reciprocal(rden[:, n:n + 1], bank_c[n % 2][:, C:VCOLS]).then_inc(den_ready, 1)
                dve.wait_ge(den_ready, s0 + 1)
                V.scalar_tensor_tensor(out=t1[:, n, :], in0=bank_c[n % 2][:, 0:C], scalar=rden[:, n:n + 1],
                                       in1=xt[b][:, n, :], op0=ALU.mult, op1=ALU.add).then_inc(c.drained, 1)

            def norm(i, src, dst, first, which, eps):
                s0 = i * NORM_STEPS
                for n in range(TILES):
                    last = V.bn_stats(stats[:, n, :], src(n))
                last.then_inc(norm_step, 1)
                wait_apart(dve, norm_step, s0 + (first + 1))
                for n in range(TILES):
                    last = V.bn_aggr(mean_var[:, n, :], stats[:, n, :])
                step(last, norm_step, s0, first + 2)
                V.tensor_scalar(var_eps[:], mean_var[:, :, 1], eps, None, ALU.add).then_inc(norm_step, 1)
                dve.wait_ge(rstd_ready, i * 2 + (which + 1))
                for n in range(TILES):
                    last = V.tensor_scalar(dst[:, n, :], src(n), mean_var[:, n, 0:1], rstd[:, n:n + 1], ALU.subtract, ALU.mult)
                last.then_inc(norm_step, 1)

            def head_weights(i):
                s0 = i * NORM_STEPS
                dve.wait_ge(Cb[0].filled, Cb[0].full(i, "qsum"))
                V.tensor_reduce(qsum[:], bank_c[0][:, 0:2 * HEADS].rearrange("p (h t) -> p h t", t=2), AX_X, ALU.add).then_inc(Cb[0].drained, 1)
                dve.wait_ge(Cb[0].drained, Cb[0].after(i, "qsum"))
                step(V.tensor_tensor(qsum[:], qsum[:], nbq[:], ALU.add), norm_step, s0, 5)
                step(V.tensor_scalar(g_head[:], qsum[:], lunch_sum[:, 0:1], None, ALU.mult), norm_step, s0, 6)
                V.tensor_tensor(g_bv[:], g_head[:], bvD_s[:], ALU.mult)
                V.tensor_tensor(g_wv[:], wvD_s[:], g_head[:].unsqueeze(2).broadcast_to([P, HEADS, C]), ALU.mult).then_inc(norm_step, 1)

            def linear_attended(i):
                dve.wait_ge(bias_added, i + 1)
                for h in range(2):
                    dve.wait_ge(Cb[h].filled, Cb[h].full(i, "attn"))
                    V.tensor_tensor(t2[:, bass.ds(i * TILES + 4 * h, 4), :], bank_c[h][:, :].rearrange("p (n c) -> p n c", c=C),
                                    t1[:, 4 * h:4 * h + 4, :], ALU.add).then_inc(Cb[h].drained, 1)
                dve.wait_ge(loaded["cst"], 32)
                for h in range(2):
                    dve.wait_ge(Cb[h].drained, Cb[h].after(i, "attn"))

            def choose(i, b):
                s0 = i * GATE_STEPS
                flat = "p n e -> p (n e)"
                psl = bank_c[0][:, 0:TILES * EXPERTS].rearrange("p (n e) -> p n e", e=EXPERTS)
                mx, z, first, wmax, m2, den = (small[:, k, :] for k in range(6))
                rev = cst_s[:, C_RANK:C_RANK + EXPERTS].unsqueeze(1).broadcast_to([P, TILES, EXPERTS])
                g = [gates[:, k, bass.ds(i * TILES, TILES)] for k in range(2)]
                done = [0]

                def at(ins):
                    done[0] += 1
                    step(ins, gate_step, s0, done[0])

                dve.wait_ge(Cb[0].filled, Cb[0].full(i, "route"))
                at(V.tensor_reduce(mx, psl, AX_X, ALU.max))
                V.tensor_tensor(logit[:], psl, bcast_e(mx), ALU.subtract).then_inc(Cb[0].drained, 1)
                dve.wait_ge(exp_ready, i + 1)
                at(V.tensor_reduce(z, prob[:], AX_X, ALU.add))
                at(V.reciprocal(z, z))
                at(V.tensor_tensor(prob[:], prob[:], bcast_e(z), ALU.mult))
                for k, top in enumerate((first, m2)):
                    at(V.tensor_reduce(top, prob[:], AX_X, ALU.max))
                    at(V.tensor_tensor(tie[:], prob[:], bcast_e(top), ALU.is_equal))
                    at(V.tensor_tensor(tie[:], tie[:], rev, ALU.mult))
                    at(V.tensor_reduce(wmax, tie[:], AX_X, ALU.max))
                    at(V.tensor_tensor(pick[:, k], tie[:], bcast_e(wmax), ALU.is_equal))
                    if k == 0:
                        at(V.scalar_tensor_tensor(out=prob[:].rearrange(flat), in0=pick[:, 0].rearrange(flat), scalar=-2.0,
                                                  in1=prob[:].rearrange(flat), op0=ALU.mult, op1=ALU.add))
                at(V.tensor_tensor(den, first, m2, ALU.add))
                at(V.tensor_scalar(den, den, 1e-9, None, ALU.add))
                at(V.reciprocal(den, den))
                at(V.tensor_tensor(g[0], first, den, ALU.mult))
                at(V.tensor_tensor(g[1], m2, den, ALU.mult))
                at(V.tensor_tensor(both[:], pick[:, 0], pick[:, 1], ALU.add))
                assert done[0] == BOTH_STEP
                W = TILES * EXPERTS
                dve.wait_ge(Cb[1].filled, Cb[1].full(i, "rank"))
                at(V.tensor_tensor(logit[:], bank_c[1][:, 0:W].rearrange("p (n e) -> p n e", e=EXPERTS),
                                   base[:].unsqueeze(1).broadcast_to([P, TILES, EXPERTS]), ALU.add))
                V.tensor_tensor(base[:], bank_c[1][:, W:W + EXPERTS], base[:], ALU.add).then_inc(Cb[1].drained, 1)
                at(V.tensor_tensor(pick[:], pick[:], logit[:].unsqueeze(1).broadcast_to([P, 2, TILES, EXPERTS]), ALU.mult))
                slot_f = small[:, 6:8, :].rearrange("p k n -> p (k n)")
                at(V.tensor_reduce(slot_f, pick[:].rearrange("p k n e -> p (k n) e"), AX_X, ALU.add))
                at(V.tensor_copy(slots[b][:], slot_f))
                assert done[0] == GATE_STEPS

            V.memset(max_cols[:], 0.0).then_inc(consts_made, 1)
            for b in range(2):
                V.memset(v_ext[b][:, :, C:VCOLS], 1.0).then_inc(consts_made, 1)
                V.memset(k_stack[b][STACK:STACK + 2, :].bitcast(F32), 1.0).then_inc(consts_made, 1)
            for bank in (*A, *S, *Cb):
                dve.sem_inc(bank.drained, 1)
            dve.sem_inc(stack_step, 1)
            for b in range(2):
                for s, by in ((ln2_stored[b], 16), (y_mixed[b], 1), (mix_turned[b], 1), (out_kept[b], 1), (out_stored[b], 16)):
                    dve.sem_inc(s, by)
            dve.wait_ge(loaded["wqk"], 48)
            dve.wait_ge(loaded["cst"], 32)
            dve.wait_ge(loaded["wv"], 32)
            V.tensor_scalar(gbv[:], bvB_s[:], vec_s[:, 1:2], None, ALU.mult).then_inc(consts_made, 1)
            dve.wait_ge(loaded["attn"], 16 * 7)
            V.tensor_scalar(nbq[:], bq_s[:], float(N), None, ALU.mult).then_inc(setup, 1)
            V.tensor_reduce(lunch_sum[:], lunch_s[:], AX_X, ALU.add).then_inc(setup, 1)
            V.tensor_reduce(wp_sum[:], wp_s[:].rearrange("p k c -> p c k"), AX_X, ALU.add).then_inc(consts_made, 1)
            V.tensor_copy(base[:], cst_s[:, C_BASE:C_BASE + EXPERTS]).then_inc(setup, 1)
            dve.wait_ge(setup, 3)
            V.tensor_scalar(lunch_sum[:], lunch_sum[:], float(max(P, lunch.shape[1])) ** -0.5, None, ALU.mult).then_inc(setup, 1)
            dve.wait_ge(setup, 4)
            dve.wait_ge(consts_made, 7)
            with dve.Fori(0, PAIRS) as pair:
                for b in range(2):
                    i = 2 * pair + b
                    make_stacks(i, b)
                    keep_v(i, b)
                    for n in range(TILES):
                        row_max(i, n)
                    negate_max(i)
                    for n in range(TILES):
                        attended(i, b, n)
                    dve.wait_ge(loaded["cst"], 32)
                    for h in range(2):
                        dve.wait_ge(Cb[h].drained, Cb[h].after(i, "pv", K - 1))
                    norm(i, lambda n: t1[:, n, :], ln1, 0, 0, 1e-5)
                    head_weights(i)
                    linear_attended(i)
                    wait_apart(dve, ln2_stored[b], 16 * pair + 16)
                    norm(i, lambda n: t2[:, bass.ds(i * TILES + n, 1), :], ln2[b], 7, 1, 1e-5)
                    choose(i, b)

            marks = [0]

            def then(ins):
                marks[0] += 1
                step(ins, table_step, 0, marks[0])

            then(V.tensor_tensor(counts[:], base[:], cst_s[:, C_BASE:C_BASE + EXPERTS], ALU.subtract))
            then(V.tensor_scalar(counts_i[:], counts[:], float(P - 1), None, ALU.add))
            then(V.tensor_scalar(counts_i[:], counts_i[:], P.bit_length() - 1, None, ALU.arith_shift_right))
            then(V.tensor_copy(n_tiles[:], counts_i[:]))
            then(V.tensor_copy(ends[:], n_tiles[:]))
            for e in range(1, EXPERTS):
                then(V.tensor_tensor(ends[:, e:e + 1], ends[:, e - 1:e], ends[:, e:e + 1], ALU.add))
            at_row = cst_s[:, C_ROW:C_ROW + 1]
            expert, before, row = (tile_at[:, k:k + 1] for k in range(3))
            then(V.tensor_scalar(ended[:], ends[:], at_row, None, ALU.is_le))
            then(V.tensor_reduce(expert, ended[:], AX_X, ALU.add))
            then(V.tensor_tensor(ended[:], ended[:], n_tiles[:], ALU.mult))
            then(V.tensor_reduce(before, ended[:], AX_X, ALU.add))
            then(V.tensor_tensor(row, at_row, before, ALU.subtract))
            then(V.scalar_tensor_tensor(out=row, in0=expert, scalar=float(REGION // P), in1=row, op0=ALU.mult, op1=ALU.add))
            V.tensor_copy(tile_row[:], row).then_inc(rows_ready, 1)
            tiles = cst_s[0:1, C_TILE:C_TILE + FFN_TILES]
            wide = [1, FFN_TILES, EXPERTS]
            then(V.tensor_tensor(past[:], tiles.unsqueeze(2).broadcast_to(wide), ends[0:1, :].unsqueeze(1).broadcast_to(wide), ALU.is_ge))
            then(V.tensor_reduce(expert_f[:], past[:], AX_X, ALU.add))
            then(V.scalar_tensor_tensor(out=expert_f[:], in0=expert_f[:], scalar=float(EXPERTS - 1), in1=cst_s[0:1, C_DIGIT:C_DIGIT + FFN_TILES],
                                        op0=ALU.min, op1=ALU.mult))
            then(V.memset(table[:, 0:1], 0))
            then(V.tensor_reduce(word_f[:], expert_f[:].rearrange("p (g k) -> p g k", k=SLOTS8), AX_X, ALU.add))
            then(V.tensor_copy(table[:, 1:1 + GROUPS], word_f[:]))
            V.memset(hidden[0][:, HID:3 * CHUNK], 0.0).then_inc(hidden_pad, 1)
            V.memset(hidden[1][:, HID:3 * CHUNK], 0.0).then_inc(table_ready, 1)

            def ready_token(t, k):
                V.tensor_scalar(tok_slot[:, k:k + 1], ids[:, bass.ds(t, 1)], TOKENS - 1, None, ALU.bitwise_and).then_inc(slot_ready, 1)

            def ready_result(t, k):
                if not isinstance(t, int) or t >= SLOTS8:
                    dve.wait_ge(scattered[k], scattered_value(t, k) - 16)
                V.tensor_scalar(id_slot[:, k:k + 1], ids[:, bass.ds(t, 1)], 0, None, ALU.bitwise_or)

            def low_part(t, k):
                dve.wait_ge(x_hi_ready, t + 1)
                V.tensor_tensor(x_lo[k % 2][:], bank_a[k % 2][:, 0:P], x_hi[k % 2][:].bitcast(F32), ALU.subtract).then_inc(x_lo_ready, 1)

            def multiply(t, k):
                dve.wait_ge(silu_ready, t + 1)
                at_least(dve, hidden_turned, t - 1)
                V.tensor_tensor(hidden[k % 2][:, 0:HID], silu1[k % 2], bank_s[k % 2][:, H13 + HID:H13 + HID2], ALU.mult).then_inc(hidden_ready, 1)

            def keep_hiddenT(t, k):
                dve.wait_ge(hidden_turned, t + 1)
                at_least(dve, y_ready, t - 1)
                V.tensor_copy(hiddenT[k % 2][0:CHUNK], bank_c[0][0:CHUNK, 0:3 * P].rearrange("p (k n) -> p k n", n=P)).then_inc(hiddenT_ready, 1)

            def tile(t, k):
                multiply(t, k)
                if not isinstance(t, int) or t + 2 < FFN_TILES:
                    low_part(t + 2, (k + 2) % SLOTS8)
                if not isinstance(t, int) or t >= 1:
                    keep_hiddenT(t - 1, (k - 1) % SLOTS8)
                if not isinstance(t, int) or t + AHEAD + 1 < FFN_TILES:
                    ready_token(t + AHEAD + 1, (k + AHEAD + 1) % SLOTS8)
                if not isinstance(t, int) or t + 1 < FFN_TILES:
                    ready_result(t + 1, (k + 1) % SLOTS8)

            dve.wait_ge(ids_loaded, 16)
            V.tensor_copy(ids_rows_f[:], ids_rows[:]).then_inc(ids_exact, 1)
            dve.wait_ge(ids_turned, 1)
            V.tensor_copy(ids[:], bank_c[1][:, 0:FFN_TILES]).then_inc(ids_ready, 1)
            dve.wait_ge(ids_ready, 1)
            for t in range(AHEAD + 1):
                ready_token(t, t)
            ready_result(0, 0)
            low_part(0, 0)
            low_part(1, 1)
            experts_loop(dve, tile)
            keep_hiddenT(FFN_TILES - 1, SLOTS8 - 1)

            with dve.Fori(0, IMAGES) as i:
                for b in range(2):
                    dve.wait_ge(y_loaded[b], i * 32 + 32)
                    for j in range(4):
                        n = i * TILES + (4 * b + j)
                        last = V.scalar_tensor_tensor(out=t2[:, bass.ds(n, 1), :], in0=y_in[b][0][:, j, :], scalar=gates[:, 0, bass.ds(n, 1)],
                                                      in1=t2[:, bass.ds(n, 1), :], op0=ALU.mult, op1=ALU.add)
                    last.then_inc(mix_step, 1)
                    dve.wait_ge(mix_step, i * 2 + (b + 1))
                    dve.wait_ge(mix_turned[b], i + 1)
                    for j in range(4):
                        n = i * TILES + (4 * b + j)
                        last = V.scalar_tensor_tensor(out=mixed[b][:, j, :], in0=y_in[b][1][:, j, :], scalar=gates[:, 1, bass.ds(n, 1)],
                                                      in1=t2[:, bass.ds(n, 1), :], op0=ALU.mult, op1=ALU.add)
                    last.then_inc(y_mixed[b], 1)

        @block.gpsimd
        def _(pool):
            G = nc.gpsimd
            G.memset(minus_half[:], -0.5).then_inc(pool_made, 1)
            pool.wait_ge(pool_made, 1)
            for e in range(EXPERTS):
                pool.wait_ge(w13_loaded[e % 2], 16 * (e // 2 + 1))
                G.tensor_copy(w13_hi[:, e], w13_raw[:, e % 2]).then_inc(w13_split, 1)
                pool.wait_ge(w13_split, 2 * e + 1)
                G.tensor_tensor(w13_lo[:, e], w13_raw[:, e % 2], w13_hi[:, e].bitcast(F32), ALU.subtract).then_inc(w13_split, 1)

            def rstds(i, which):
                pool.wait_ge(norm_step, i * NORM_STEPS + (3 + 7 * which))
                G.tensor_tensor(rstd[:], var_eps[:], minus_half[:], ALU.pow).then_inc(rstd_ready, 1)

            def scatter_ids(i, b):
                wait_apart(pool, gate_step, i * GATE_STEPS + GATE_STEPS)
                for k in range(2 * TILES):
                    G.indirect_dma_start(ids_dram, bass.IndirectOffsetOnAxis(ap=slots[b][:, k:k + 1], axis=0),
                                         tok[b][:, k:k + 1], None).then_inc(ids_stored[b], 16)

            pool.wait_ge(ids_cleared, 16)
            pool.wait_ge(loaded["attn"], 16 * 7)
            pool.wait_ge(loaded["tok"], 32)
            with pool.Fori(0, PAIRS) as pair:
                for b in range(2):
                    i = 2 * pair + b
                    rstds(i, 0)
                    pool.wait_ge(norm_step, i * NORM_STEPS + LN1_STEP)
                    G.tensor_tensor(t1[:], t1[:], bpB_s[:].unsqueeze(1).broadcast_to([P, TILES, C]), ALU.add).then_inc(bias_added, 1)
                    rstds(i, 1)
                    scatter_ids(i, b)
                    wait_apart(pool, ids_stored[b], 16 * 2 * TILES * (pair + 1))
                    G.tensor_scalar(tok[b][:], tok[b][:], float(2 * N), None, ALU.add).then_inc(tok_step, 1)
                    pool.wait_ge(tok_step, i + 1)

            def gather(t, k):
                if not isinstance(t, int) or t >= SLOTS8:
                    pool.wait_ge(x_turned, t - (SLOTS8 - 1))
                wait_apart(pool, slot_ready, t + 1)
                G.indirect_dma_start(x_rows[k], None, ln2_dram, bass.IndirectOffsetOnAxis(ap=tok_slot[:, k:k + 1], axis=0)).then_inc(gathered[k], 16)

            def scatter(t, k):
                wait_apart(pool, y_kept, t + 1)
                G.indirect_dma_start(y_dram, bass.IndirectOffsetOnAxis(ap=id_slot[:, k:k + 1], axis=0), y_rows[k], None).then_inc(scattered[k], 16)

            def tile(t, k):
                if not isinstance(t, int) or t + AHEAD < FFN_TILES:
                    gather(t + AHEAD, (k + AHEAD) % SLOTS8)
                scatter(t, k)

            for b in range(2):
                pool.wait_ge(ids_stored[b], 16 * 2 * TILES * PAIRS)
                pool.wait_ge(ln2_stored[b], 16 * PAIRS + 16)
            pool.wait_ge(rows_ready, 1)
            G.indirect_dma_start(ids_rows[:], None, ids_dram.rearrange("(a b) c -> a (b c)", b=P),
                                 bass.IndirectOffsetOnAxis(ap=tile_row[0:FFN_TILES, :], axis=0)).then_inc(ids_loaded, 16)
            for t in range(AHEAD):
                gather(t, t)
            experts_loop(pool, tile)

def host_layout(np, ml, d):
    f = {k: np.ascontiguousarray(np.asarray(v)) for k, v in d.items()}
    images, c, hh, ww = f["x"].shape
    n = hh * ww
    tiles = n // P
    tokens = images * n
    dim, r = f["L1_attn_lunchbox"].shape
    heads = f["L1_attn_proj_w"].shape[0] // dim
    experts, hid, _ = f["L1_ffn_w1"].shape
    chunk = -(-hid // 3)
    ident = np.eye(P, dtype=np.float32)
    dqk = f["L0_conv_Wq"].shape[0]
    low = np.zeros((P, 1), np.float32)
    for k in (2, 3, 5, 7):
        low[k * dqk:(k + 1) * dqk] = -1.0
    e = np.arange(experts, dtype=np.float32)
    cst = np.concatenate([ident, low, np.tile(experts - e, (P, 1)), np.tile(e * tokens, (P, 1)), np.tile(np.arange(FFN_MAX), (P, 1)),
                          np.arange(P)[:, None], np.tile(float(experts) ** (np.arange(FFN_MAX) % 8), (P, 1))], 1).astype(np.float32)
    tri = np.concatenate([np.triu(np.ones((P, P)), 1), np.ones((P, P))], 1).astype(ml.bfloat16)
    tok = np.arange(2)[:, None, None] * tokens + np.arange(tiles)[None, :, None] * P + np.arange(P)[None, None, :]
    tok = np.stack([tok.reshape(2 * tiles, P).T + b * n for b in range(2)]).astype(np.int32)
    rows = np.arange(P)
    pad = [np.tile(2 * tokens + P * k + rows, tokens // P) for k in range(experts)]
    pad += [2 * tokens + P * (experts + k) + rows for k in range(experts)]
    pad = np.concatenate(pad).astype(np.int32).reshape(-1, (experts * (tokens + P)) // P)
    w = f["L1_attn_qkv_w"]
    bq, bv = f["L1_attn_qkv_b"][:heads * dim], f["L1_attn_qkv_b"][heads * dim:]
    w2 = np.transpose(f["L1_ffn_w2"], (2, 0, 1))
    w2p = np.zeros((3 * chunk, experts, c), np.float32)
    w2p[:hid] = w2
    return {
        "x": f["x"].reshape(images, c, n), "cst": cst, "tri": tri, "tokid": tok, "pad_ids": pad,
        "wqk": np.concatenate([f["L0_conv_Wq"].T] * 4 + [f["L0_conv_Wk"].T] * 4, 1),
        "bqk": np.concatenate([f["L0_conv_bq"]] * 4 + [f["L0_conv_bk"]] * 4)[:, None],
        "wvT": f["L0_conv_Wv"].T, "bvB": np.tile(f["L0_conv_bv"], (P, 1)), "gammaB": np.tile(f["L0_conv_gamma"], (P, 1)),
        "wq": w[:, :heads * dim], "bq": bq.reshape(heads, dim).T, "lunch": f["L1_attn_lunchbox"],
        "wvD": w[:, heads * dim:].T.reshape(heads, dim, c).transpose(1, 0, 2),
        "bvD": bv.reshape(heads, dim).T,
        "wp": f["L1_attn_proj_w"].reshape(heads, dim, c).transpose(1, 0, 2),
        "bpB": np.tile(f["L1_attn_proj_b"], (P, 1)), "routerT": f["L1_ffn_router_w"].T,
        "w13": np.concatenate([f["L1_ffn_w1"], f["L1_ffn_w3"]], 1).transpose(2, 0, 1),
        "w2T": w2p.reshape(3, chunk, experts, c).transpose(1, 0, 2, 3),
    }


_ORDER = ["x", "cst", "tri", "tokid", "pad_ids", "wqk", "bqk", "wvT", "bvB", "gammaB", "wq", "bq", "lunch", "wvD", "bvD", "wp",
          "bpB", "routerT", "w13", "w2T"]


def kernel(**inputs):
    import ml_dtypes
    import numpy as np
    import concourse.bacc as bacc
    from concourse.bass_utils import run_bass_kernel_spmd

    nc = bacc.Bacc("TRN2", target_bir_lowering=False, num_devices=1)
    layout = host_layout(np, ml_dtypes, inputs)
    arrays, args = {}, []
    for name in _ORDER:
        a = np.ascontiguousarray(layout[name])
        arrays[f"in_{name}_dram"] = a
        args.append(nc.dram_tensor(f"in_{name}_dram", a.shape, mybir.dt.from_np(a.dtype), kind="ExternalInput").ap())
    shape = inputs["x"].shape
    flat = (shape[0], shape[1], shape[2] * shape[3])
    args.append(nc.dram_tensor("out_0_dram", flat, F32, kind="ExternalOutput").ap())
    conv_attn_moe_kernel(nc, *args)
    r = run_bass_kernel_spmd(nc, [arrays], core_ids=[0])
    return r.results[0]["out_0_dram"].reshape(shape)
```

```python
from contextlib import ExitStack

import concourse.bass as bass
from concourse import mybir

ALU = mybir.AluOpType
ACT = mybir.ActivationFunctionType
AX_X = mybir.AxisListType.X
F32 = mybir.dt.float32
F32R = mybir.dt.float32r
BF16 = mybir.dt.bfloat16
I32 = mybir.dt.int32

P = 128

C_IDENT = 0
C_LOW = 128
C_RANK = 129
C_BASE = 137
C_TILE = 145
FFN_MAX = 72
C_ROW = C_TILE + FFN_MAX
C_DIGIT = C_ROW + 1
C_COLS = C_DIGIT + FFN_MAX


class Uses:

    def __init__(self, filled, drained, total, **first):
        self.filled, self.drained, self.total, self.first = filled, drained, total, first

    def before(self, i, use, n=0):
        return i * self.total + (self.first[use] + n + 1)

    def after(self, i, use, n=0):
        return i * self.total + (self.first[use] + n + 2)

    def full(self, i, use, n=0):
        return i * self.total + (self.first[use] + n + 1)


def conv_attn_moe_kernel(nc, x, cst, tri, tokid, pad_ids, wqk, bqk, wvT, bvB, gammaB, wq, bq, lunch, wvD, bvD, wp, bpB,
                         routerT, w13, w2T, out):
    IMAGES, C, N = x.shape
    TILES = N // P
    TOKENS = IMAGES * N
    DQK = 16
    STACK = 4 * DQK
    HEADS = wp.shape[1]
    EXPERTS = routerT.shape[1]
    HID2 = w13.shape[2]
    HID = HID2 // 2
    CHUNK = -(-HID // 3)
    REGION = TOKENS
    FFN_TILES = 2 * TOKENS // P + EXPERTS
    assert FFN_TILES == FFN_MAX
    RESULTS = 2 * TOKENS + 2 * EXPERTS * P
    SLOTS8 = 8
    GROUPS = FFN_TILES // SLOTS8
    RANK_AFTER = 5
    AHEAD = 6
    H13 = 170
    W_A = HID2 // 2 + 1
    SLOTS = pad_ids.shape[0] * pad_ids.shape[1]
    HALF = N // 2
    VCOLS = C + 1

    ids_dram = nc.dram_tensor("ids_dram", [SLOTS, 1], I32, kind="Internal").ap()
    ln2_dram = nc.dram_tensor("ln2_dram", [TOKENS, C], F32, kind="Internal").ap()

    y_dram = nc.dram_tensor("y_dram", [RESULTS, C], F32, kind="Internal").ap()

    with ExitStack() as ctx:
        def sb(name, shape, dt=F32):
            return ctx.enter_context(nc.sbuf_tensor(name + "_sb", shape, dt))

        def psum(name, shape):
            return ctx.enter_context(nc.psum_tensor(name, shape, F32))

        def sem(name):
            return ctx.enter_context(nc.semaphore(name))

        cst_s = sb("cst_s", [P, C_COLS])
        tri_s = sb("tri_s", [P, 2 * P], BF16)
        wqk_s = sb("wqk_s", [P, P])
        wvT_s = sb("wvT_s", [P, C])
        vec_s = sb("vec_s", [P, 2])
        bvB_s = sb("bvB_s", [P, C])
        wq_s = sb("wq_s", [P, HEADS * P])
        bq_s = sb("bq_s", [P, HEADS])
        lunch_s = sb("lunch_s", [P, lunch.shape[1]])
        wvD_s = sb("wvD_s", [P, HEADS, C])
        bvD_s = sb("bvD_s", [P, HEADS])
        wp_s = sb("wp_s", [P, HEADS, C])
        bpB_s = sb("bpB_s", [P, C])
        routerT_s = sb("routerT_s", [P, EXPERTS])
        w13_hi = sb("w13_hi", [P, EXPERTS, HID2], F32R)
        w13_lo = sb("w13_lo", [P, EXPERTS, HID2], F32R)
        w2_s = sb("w2_s", [CHUNK, 3, EXPERTS, C])

        xc = sb("xc", [P, N])
        qk_sum = sb("qk_sum", [P, N])
        qk_hi = sb("qk_hi", [P, N], F32R)
        q_stack = sb("q_stack", [STACK + 2, N], F32R)
        k_stack = sb("k_stack", [STACK + 2, N], F32R)
        gbv = sb("gbv", [P, C])
        v_ext = sb("v_ext", [P, TILES, VCOLS])
        xt = sb("xt", [P, TILES, C])
        row_max2 = sb("row_max2", [P, TILES, 2])
        neg_max = sb("neg_max", [P, TILES])
        neg_max_hi = sb("neg_max_hi", [P, TILES], F32R)
        max_cols = sb("max_cols", [P, TILES, STACK + 2])
        probs = sb("probs", [P, TILES, N])
        rden = sb("rden", [P, TILES])
        t1 = sb("t1", [P, TILES, C])
        stats = sb("stats", [P, TILES, 6])
        mean_var = sb("mean_var", [P, TILES, 2])
        var_eps = sb("var_eps", [P, TILES])
        minus_half = sb("minus_half", [P, TILES])
        rstd = sb("rstd", [P, TILES])
        ln1 = sb("ln1", [P, TILES, C])
        lnT = sb("lnT", [P, N])
        ln1_sum = sb("ln1_sum", [P, 2])
        nbq = sb("nbq", [P, HEADS])
        lunch_sum = sb("lunch_sum", [P, 1])
        qsum = sb("qsum", [P, HEADS])
        g_head = sb("g_head", [P, HEADS])
        g_wv = sb("g_wv", [P, HEADS, C])
        g_bv = sb("g_bv", [P, HEADS])
        wp_sum = sb("wp_sum", [P, C])
        t2 = sb("t2", [P, IMAGES * TILES, C])
        w13_raw = t2[:].rearrange("p n c -> p (n c)")[:, (IMAGES * TILES - 11) * C:(IMAGES * TILES - 11) * C + 2 * HID2].rearrange("p (b h) -> p b h", b=2)
        ln2 = sb("ln2", [P, TILES, C])
        small = sb("small", [P, 8, TILES])
        logit = sb("logit", [P, TILES, EXPERTS])
        prob = sb("prob", [P, TILES, EXPERTS])
        tie = sb("tie", [P, TILES, EXPERTS])
        pick = sb("pick", [P, 2, TILES, EXPERTS])
        both = sb("both", [P, TILES, EXPERTS], BF16)
        gates = sb("gates", [P, 2, IMAGES * TILES])
        base = sb("base", [P, EXPERTS])
        slots = sb("slots", [P, 2 * TILES], I32)
        tok = sb("tok", [P, 2 * TILES], I32)

        counts = sb("counts", [P, EXPERTS])
        counts_i = sb("counts_i", [P, EXPERTS], I32)
        n_tiles = sb("n_tiles", [P, EXPERTS])
        ends = sb("ends", [P, EXPERTS])
        past = sb("past", [1, FFN_TILES, EXPERTS])
        ended = sb("ended", [P, EXPERTS])
        tile_at = sb("tile_at", [P, 3])
        tile_row = sb("tile_row", [P, 1], I32)
        expert_f = sb("expert_f", [1, FFN_TILES])
        word_f = sb("word_f", [1, GROUPS])
        table = sb("table", [1, 1 + GROUPS], I32)
        ids_rows = sb("ids_rows", [FFN_TILES, P], I32)
        ids_rows_f = sb("ids_rows_f", [FFN_TILES, P])
        ids = sb("ids", [P, FFN_TILES], I32)
        id_slot = sb("id_slot", [P, SLOTS8], I32)
        tok_slot = sb("tok_slot", [P, SLOTS8], I32)
        x_hi = [sb(f"x_hi{b}", [P, P], F32R) for b in range(2)]
        x_lo = [sb(f"x_lo{b}", [P, P], F32R) for b in range(2)]
        spare, used = probs[:].rearrange("p m n -> p (m n)"), [0]

        def place(cols):
            used[0] += cols
            assert used[0] <= TILES * N
            return spare[:, used[0] - cols:used[0]]

        x_rows = [place(C) for _ in range(SLOTS8)]
        y_rows = [place(C) for _ in range(SLOTS8)]
        silu1 = [place(HID) for _ in range(2)]
        hidden = [place(3 * CHUNK) for _ in range(2)]
        hiddenT = [place(3 * P).rearrange("p (k n) -> p k n", n=P) for _ in range(2)]
        y_in = [[place(4 * C).rearrange("p (n c) -> p n c", c=C) for _ in range(2)] for _ in range(2)]
        y_out = [place(4 * P) for _ in range(2)]
        mixed = [spare[:, 4 * C * b:4 * C * (b + 1)].rearrange("p (n c) -> p n c", c=C) for b in range(2)]

        bank_a = [psum(f"bank_a{h}", [P, 512]) for h in range(2)]
        bank_s = [psum(f"bank_s{h}", [P, N]) for h in range(2)]
        bank_c = [psum(f"bank_c{h}", [P, 512]) for h in range(2)]

        loaded = {n: sem(f"{n}_loaded") for n in ("cst", "wqk", "wv", "attn", "router", "w2", "tok")}
        x_loaded, w13_loaded = sem("x_loaded"), [sem(f"w13_loaded{b}") for b in range(2)]
        w13_split = sem("w13_split")
        ids_cleared = sem("ids_cleared")
        consts_made, pool_made = sem("consts_made"), sem("pool_made")
        K = TILES // 2
        A = [Uses(sem(f"a_filled{h}"), sem(f"a_drained{h}"), 4 + TILES,
                  qk=0, xt=1, v=2, scores=3, rows=3 + TILES) for h in range(2)]
        S = [Uses(sem("s_filled0"), sem("s_drained0"), K + 1 + HEADS // 2, scores=0, rank=K, weff=K + 1),
             Uses(sem("s_filled1"), sem("s_drained1"), K + HEADS // 2, scores=0, weff=K)]
        Cb = [Uses(sem("c_filled0"), sem("c_drained0"), K + 5, pv=0, ln1=K, qsum=K + 1, attn=K + 2, ln2=K + 3, route=K + 4),
              Uses(sem("c_filled1"), sem("c_drained1"), K + 3, pv=0, ln1=K, attn=K + 1, ln2=K + 2)]

        def rank_use(i):
            return "scores" if isinstance(i, int) and i == IMAGES - 1 else "rank"

        stack_step, max_step = sem("stack_step"), sem("max_step")
        norm_step, gate_step = sem("norm_step"), sem("gate_step")
        rstd_ready, exp_ready = sem("rstd_ready"), sem("exp_ready")
        ln2_stored, ids_stored = sem("ln2_stored"), sem("ids_stored")
        STACK_STEPS, MAX_STEPS, NORM_STEPS, GATE_STEPS = 3, 4, 11, 25
        LN1_STEP, WPG_STEP, BOTH_STEP = 4, 7, 16
        setup, den_ready, tok_step, bias_added = sem("setup"), sem("den_ready"), sem("tok_step"), sem("bias_added")
        weff = probs[:].rearrange("p k (h c) -> p k h c", c=C)

        table_ready, table_step = sem("table_ready"), sem("table_step")
        rows_ready, ids_loaded, ids_exact, ids_turned = sem("rows_ready"), sem("ids_loaded"), sem("ids_exact"), sem("ids_turned")
        ids_ready = sem("ids_ready")
        slot_ready = sem("slot_ready")
        gathered = [sem(f"gathered{k}") for k in range(SLOTS8)]
        scattered = [sem(f"scattered{k}") for k in range(SLOTS8)]
        x_turned, x_hi_ready, x_lo_ready = sem("x_turned"), sem("x_hi_ready"), sem("x_lo_ready")
        h13_ready, silu_ready, hidden_ready = sem("h13_ready"), sem("silu_ready"), sem("hidden_ready")
        hidden_turned, hiddenT_ready = sem("hidden_turned"), sem("hiddenT_ready")
        y_ready, y_kept, hidden_pad = sem("y_ready"), sem("y_kept"), sem("hidden_pad")
        y_loaded, y_mixed = [sem(f"y_loaded{b}") for b in range(2)], [sem(f"y_mixed{b}") for b in range(2)]
        mix_step, waits_passed = sem("mix_step"), sem("waits_passed")
        mix_turned, out_kept = [sem(f"mix_turned{b}") for b in range(2)], [sem(f"out_kept{b}") for b in range(2)]
        out_stored = [sem(f"out_stored{b}") for b in range(2)]

        def experts_loop(eng, tile, begin=lambda g: None):
            begin(0)
            for t in range(SLOTS8):
                tile(t, t)
            with eng.Fori(1, GROUPS - 1) as g:
                begin(g)
                for k in range(SLOTS8):
                    tile(g * SLOTS8 + k, k)
            begin(GROUPS - 1)
            for k in range(SLOTS8):
                tile((GROUPS - 1) * SLOTS8 + k, k)

        def wait_apart(eng, s, value):
            eng.wait_ge(s, value)
            eng.sem_inc(waits_passed, 1)

        def at_least(eng, s, value):
            if not isinstance(value, int) or value > 0:
                eng.wait_ge(s, value)

        def gathered_value(t, k):
            return (t - k) * (16 // SLOTS8) + 16

        scattered_value = gathered_value

        ident = cst_s[:, C_IDENT:C_IDENT + P]

        block = ctx.enter_context(nc.Block())

        @block.sync
        def _(sp):
            sp.dma_start(xc[:], x[0]).then_inc(x_loaded, 16)
            sp.dma_start(wqk_s[:], wqk).then_inc(loaded["wqk"], 16)
            sp.dma_start(vec_s[:, 0:1], bqk).then_inc(loaded["wqk"], 16)
            sp.dma_start(vec_s[:, 1:2], gammaB).then_inc(loaded["wqk"], 16)
            sp.dma_start(cst_s[:], cst).then_inc(loaded["cst"], 16)
            sp.dma_start(tri_s[:], tri).then_inc(loaded["cst"], 16)
            sp.dma_start(wvT_s[:], wvT).then_inc(loaded["wv"], 16)
            sp.dma_start(bvB_s[:], bvB).then_inc(loaded["wv"], 16)
            for dst, src in ((wq_s, wq), (bq_s, bq), (lunch_s, lunch), (wvD_s, wvD), (bvD_s, bvD), (wp_s, wp), (bpB_s, bpB)):
                sp.dma_start(dst[:], src).then_inc(loaded["attn"], 16)
            sp.dma_start(routerT_s[:], routerT).then_inc(loaded["router"], 16)
            sp.dma_start(tok[:], tokid).then_inc(loaded["tok"], 16)
            sp.dma_start(ids_dram.rearrange("(a b) c -> a (b c)", b=pad_ids.shape[1]), pad_ids).then_inc(ids_cleared, 16)
            for e in range(EXPERTS):
                if e >= 2:
                    sp.wait_ge(w13_split, 2 * (e - 1))
                sp.dma_start(w13_raw[:, e % 2], w13[:, e]).then_inc(w13_loaded[e % 2], 16)
            sp.dma_start(w2_s[:], w2T).then_inc(loaded["w2"], 16)

            def store_ln2(i):
                sp.wait_ge(norm_step, i * NORM_STEPS + NORM_STEPS)
                sp.dma_start(ln2_dram[bass.ds(i * N, N), :].rearrange("(n p) c -> p n c", p=P), ln2[:]).then_inc(ln2_stored, 16)

            def load_x(i):
                sp.wait_ge(A[1].filled, A[1].full(i - 1, "v"))
                sp.dma_start(xc[:], x[bass.ds(i, 1)].rearrange("i c n -> c (i n)")).then_inc(x_loaded, 16)

            load_x(1)
            with sp.Fori(0, IMAGES - 2) as i:
                store_ln2(i)
                load_x(i + 2)
            for i in (IMAGES - 2, IMAGES - 1):
                store_ln2(i)
            sp.wait_ge(ln2_stored, 16 * IMAGES + 16)
            for k in range(SLOTS8):
                sp.wait_ge(scattered[k], 16 * GROUPS)
            with sp.Fori(0, IMAGES) as i:
                for b in range(2):
                    sp.wait_ge(y_mixed[b], i + 1)
                    for k in range(2):
                        rows = y_dram[bass.ds(i * N + (k * TOKENS + b * HALF), HALF), :]
                        sp.dma_start(y_in[b][k], rows.rearrange("(n p) c -> p n c", p=P)).then_inc(y_loaded[b], 16)
            for b in range(2):
                sp.wait_ge(out_stored[b], 16 * (IMAGES + 1))

        @block.tensor
        def _(pe):
            def mm(bank, lhsT, rhs, start=True, stop=True):
                return nc.tensor.matmul(bank, lhsT, rhs, start=start, stop=stop)

            def project(i):
                pe.wait_ge(x_loaded, i * 16 + 16)
                for h in range(2):
                    pe.wait_ge(A[h].drained, A[h].before(i, "qk"))
                    mm(bank_a[h][:, :], wqk_s[:], xc[:, h * HALF:(h + 1) * HALF]).then_inc(A[h].filled, 1)
                for h in range(2):
                    pe.wait_ge(A[h].drained, A[h].before(i, "xt"))
                    for j in range(4):
                        n = 4 * h + j
                        last = nc.tensor.transpose(bank_a[h][:, j * C:(j + 1) * C], xc[:, n * P:(n + 1) * P], ident)
                    last.then_inc(A[h].filled, 1)
                for h in range(2):
                    pe.wait_ge(A[h].drained, A[h].before(i, "v"))
                    for j in range(4):
                        n = 4 * h + j
                        last = mm(bank_a[h][:, j * C:(j + 1) * C], xc[:, n * P:(n + 1) * P], wvT_s[:])
                    last.then_inc(A[h].filled, 1)

            def scores_by_query(i, n):
                if n == 0:
                    pe.wait_ge(stack_step, i * STACK_STEPS + (STACK_STEPS + 1))
                for h in range(2):
                    pe.wait_ge(A[h].drained, A[h].before(i, "scores", n))
                    mm(bank_a[h][:, :], q_stack[0:STACK, n * P:(n + 1) * P],
                       k_stack[0:STACK, h * HALF:(h + 1) * HALF]).then_inc(A[h].filled, 1)

            def max_rows(i):
                pe.wait_ge(max_step, i * MAX_STEPS + MAX_STEPS)
                for h in range(2):
                    pe.wait_ge(A[h].drained, A[h].before(i, "rows"))
                    for j in range(4):
                        last = nc.tensor.transpose(bank_a[h][0:STACK + 2, j * P:(j + 1) * P], max_cols[:, 4 * h + j, :], ident)
                    last.then_inc(A[h].filled, 1)

            def scores_by_key(i, m):
                if m == 0:
                    for h in range(2):
                        pe.wait_ge(A[h].drained, A[h].after(i, "rows"))
                s = S[m % 2]
                pe.wait_ge(s.drained, s.before(i, "scores", m // 2))
                for h in range(2):
                    last = mm(bank_s[m % 2][:, h * HALF:(h + 1) * HALF], k_stack[:, m * P:(m + 1) * P],
                              q_stack[:, h * HALF:(h + 1) * HALF])
                last.then_inc(s.filled, 1)

            def weigh_values(i, n):
                if n == 0:
                    for s in S:
                        pe.wait_ge(s.drained, s.after(i, "scores", TILES // 2 - 1))
                c = Cb[n % 2]
                pe.wait_ge(c.drained, c.before(i, "pv", n // 2))
                for m in range(TILES):
                    last = mm(bank_c[n % 2][:, 0:VCOLS], probs[:, m, n * P:(n + 1) * P], v_ext[:, m, :],
                              start=(m == 0), stop=(m == TILES - 1))
                last.then_inc(c.filled, 1)

            def turn(i, src, use):
                for h in range(2):
                    pe.wait_ge(Cb[h].drained, Cb[h].before(i, use))
                    for j in range(4):
                        last = nc.tensor.transpose(bank_c[h][:, j * C:(j + 1) * C], src[:, 4 * h + j, :], ident)
                    last.then_inc(Cb[h].filled, 1)

            def head_sums(i):
                pe.wait_ge(norm_step, i * NORM_STEPS + LN1_STEP)
                turn(i, ln1, "ln1")
                for h in range(2):
                    pe.wait_ge(Cb[h].drained, Cb[h].after(i, "ln1"))
                for hd in range(HEADS):
                    last = mm(bank_c[0][:, 2 * hd:2 * hd + 2], wq_s[:, hd * P:(hd + 1) * P], ln1_sum[:, :])
                last.then_inc(Cb[0].filled, 1)

            def head_weight(i, hd):
                if hd == 0:
                    pe.wait_ge(norm_step, i * NORM_STEPS + WPG_STEP)
                s = S[hd % 2]
                pe.wait_ge(s.drained, s.before(i, "weff", hd // 2))
                for h in range(2):
                    last = mm(bank_s[hd % 2][:, h * HALF:(h + 1) * HALF], g_wv[:, hd, :],
                              wp_s[:, 4 * h:4 * h + 4, :].rearrange("p k c -> p (k c)"))
                last.then_inc(s.filled, 1)

            def linear_attention(i):
                for h in range(2):
                    pe.wait_ge(Cb[h].drained, Cb[h].before(i, "attn"))
                    for hd in range(4):
                        mm(bank_c[h][:, hd * C:(hd + 1) * C], g_bv[:, 4 * h + hd:4 * h + hd + 1].broadcast_to([P, P]),
                           wp_sum[:], start=(hd == 0), stop=False)
                for s in S:
                    pe.wait_ge(s.drained, s.after(i, "weff", HEADS // 2 - 1))
                for h in range(2):
                    for k in range(HEADS):
                        last = mm(bank_c[h][:, :], lnT[:, k:N:HEADS],
                                  weff[:, k, 4 * h:4 * h + 4, :].rearrange("p h c -> p (h c)"), start=False, stop=(k == HEADS - 1))
                    last.then_inc(Cb[h].filled, 1)

            def route(i):
                pe.wait_ge(norm_step, i * NORM_STEPS + NORM_STEPS)
                turn(i, ln2, "ln2")
                for h in range(2):
                    pe.wait_ge(Cb[h].drained, Cb[h].after(i, "ln2"))
                for n in range(TILES):
                    last = mm(bank_c[0][:, n * EXPERTS:(n + 1) * EXPERTS], lnT[:, n * P:(n + 1) * P], routerT_s[:])
                last.then_inc(Cb[0].filled, 1)

            def rank(i):
                pe.wait_ge(gate_step, i * GATE_STEPS + BOTH_STEP)
                pe.wait_ge(S[0].drained, S[0].before(i + 1, rank_use(i)))
                W = TILES * EXPERTS
                flat = both[:].rearrange("p n e -> p (n e)")
                mm(bank_s[0][:, 0:W], tri_s[:, 0:P], flat, stop=False)
                for n in range(1, TILES):
                    mm(bank_s[0][:, n * EXPERTS:W], tri_s[:, P:2 * P], flat[:, 0:W - n * EXPERTS], start=False, stop=False)
                for n in range(TILES):
                    last = mm(bank_s[0][:, W:W + EXPERTS], tri_s[:, P:2 * P], both[:, n, :], start=False, stop=(n == TILES - 1))
                last.then_inc(S[0].filled, 1)

            def image(i, first=False, last=False):
                for m in range(TILES):
                    scores_by_key(i, m)
                if not first:
                    route(i - 1)
                for n in range(RANK_AFTER):
                    weigh_values(i, n)
                if first:
                    pe.sem_inc(S[0].filled, 1)
                    pe.sem_inc(S[0].drained, 1)
                else:
                    rank(i - 1)
                for n in range(RANK_AFTER, TILES):
                    weigh_values(i, n)
                if not last:
                    project(i + 1)
                head_sums(i)
                for hd in range(HEADS):
                    head_weight(i, hd)
                    if not last:
                        scores_by_query(i + 1, hd)
                if not last:
                    max_rows(i + 1)
                linear_attention(i)

            pe.wait_ge(loaded["wqk"], 48)
            pe.wait_ge(loaded["wv"], 32)
            pe.wait_ge(loaded["cst"], 32)
            pe.wait_ge(loaded["attn"], 16 * 7)
            pe.wait_ge(loaded["router"], 16)
            pe.wait_ge(consts_made, 5)
            pe.wait_ge(pool_made, 1)
            project(0)
            for n in range(TILES):
                scores_by_query(0, n)
            max_rows(0)
            image(0, first=True)
            with pe.Fori(1, IMAGES - 1) as i:
                image(i)
            image(IMAGES - 1, last=True)
            route(IMAGES - 1)
            rank(IMAGES - 1)

            def turn_x(t, k):
                at_least(pe, x_lo_ready, t - 1)
                pe.wait_ge(gathered[k], gathered_value(t, k))
                nc.tensor.transpose(bank_a[k % 2][:, 0:P], x_rows[k], ident).then_inc(x_turned, 1)

            def hidden13(t, k, e):
                pe.wait_ge(x_lo_ready, t + 1)
                at_least(pe, hidden_ready, t - 1)
                hi, lo = x_hi[k % 2], x_lo[k % 2]
                for h, cols in enumerate((slice(0, W_A), slice(W_A, HID2))):
                    dst = bank_s[k % 2][:, H13 + cols.start:H13 + cols.stop]
                    for n, (x_part, w_part) in enumerate(((hi, w13_hi), (hi, w13_lo), (lo, w13_hi))):
                        last = mm(dst, x_part[:], w_part[:, bass.ds(e, 1), cols].rearrange("p a h -> p (a h)"), start=(n == 0), stop=(n == 2))
                last.then_inc(h13_ready, 1)

            def turn_hidden(t, k):
                pe.wait_ge(hidden_ready, t + 1)
                at_least(pe, hiddenT_ready, t)
                for c in range(3):
                    last = nc.tensor.transpose(bank_c[0][0:CHUNK, c * P:(c + 1) * P], hidden[k % 2][:, c * CHUNK:(c + 1) * CHUNK], ident)
                last.then_inc(hidden_turned, 1)

            def result(t, k, e):
                pe.wait_ge(hiddenT_ready, t + 1)
                at_least(pe, y_kept, t)
                for c in range(3):
                    rows = min(CHUNK, HID - c * CHUNK)
                    last = mm(bank_c[1][:, 0:C], hiddenT[k % 2][0:rows, c, :],
                              w2_s[0:rows, c, bass.ds(e, 1), :].rearrange("p a c -> p (a c)"), start=(c == 0), stop=(c == 2))
                last.then_inc(y_ready, 1)

            def tile(t, k):
                hidden13(t, k, experts[k + 2])
                if not isinstance(t, int) or t + 2 < FFN_TILES:
                    turn_x(t + 2, (k + 2) % SLOTS8)
                if not isinstance(t, int) or t >= 1:
                    turn_hidden(t - 1, (k - 1) % SLOTS8)
                if not isinstance(t, int) or t >= 2:
                    result(t - 2, (k - 2) % SLOTS8, experts[k])

            experts = []

            def load_experts(g):
                bits = (EXPERTS - 1).bit_length()
                words = nc.values_load_multi_w_load_instructions(table[0:1, bass.ds(g, 2)], engines=[mybir.EngineType.PE],
                                                                 min_val=0, max_val=EXPERTS ** SLOTS8 - 1)[1]
                digits = [(0, SLOTS8 - 2), (0, SLOTS8 - 1)] + [(1, j) for j in range(SLOTS8)]
                experts[:] = [(words[w] >> (bits * j)) & (EXPERTS - 1) for w, j in digits]

            pe.wait_ge(ids_exact, 1)
            nc.tensor.transpose(bank_c[1][:, 0:FFN_TILES], ids_rows_f[:], cst_s[0:FFN_TILES, C_IDENT:C_IDENT + FFN_TILES]).then_inc(ids_turned, 1)
            pe.wait_ge(table_ready, 1)
            pe.wait_ge(w13_split, 2 * EXPERTS)
            pe.wait_ge(loaded["w2"], 16)
            turn_x(0, 0)
            turn_x(1, 1)
            experts_loop(pe, tile, load_experts)
            turn_hidden(FFN_TILES - 1, SLOTS8 - 1)
            for t in (FFN_TILES - 2, FFN_TILES - 1):
                result(t, t % SLOTS8, experts[t - FFN_TILES])

            with pe.Fori(0, IMAGES) as i:
                for b in range(2):
                    pe.wait_ge(y_mixed[b], i + 2)
                    pe.wait_ge(out_kept[b], i + 1)
                    for j in range(4):
                        last = nc.tensor.transpose(bank_a[b][:, j * P:(j + 1) * P], mixed[b][:, j, :], ident)
                    last.then_inc(mix_turned[b], 1)

        @block.scalar
        def _(act):
            def stack_sums(i):
                for h in range(2):
                    act.wait_ge(A[h].filled, A[h].full(i, "qk"))
                    act.wait_ge(stack_step, i * STACK_STEPS + 1)
                    nc.scalar.activation(qk_sum[:, h * HALF:(h + 1) * HALF], bank_a[h][:, :], ACT.Identity,
                                         bias=vec_s[:, 0:1]).then_inc(A[h].drained, 1)

            def keep_xt(i):
                for h in range(2):
                    if not isinstance(i, int) or i > 0:
                        act.wait_ge(Cb[h].drained, Cb[h].after(i - 1, "pv", K - 1))
                    act.wait_ge(A[h].filled, A[h].full(i, "xt"))
                    nc.scalar.copy(xt[:, 4 * h:4 * h + 4, :], bank_a[h][:, :].rearrange("p (n c) -> p n c", c=C)).then_inc(A[h].drained, 1)

            def max_rows(i):
                for h in range(2):
                    act.wait_ge(A[h].filled, A[h].full(i, "rows"))
                    nc.scalar.copy(q_stack[STACK:STACK + 2, h * HALF:(h + 1) * HALF],
                                   bank_a[h][STACK:STACK + 2, :]).then_inc(A[h].drained, 1)

            def exps(i, m):
                s = S[m % 2]
                act.wait_ge(s.filled, s.full(i, "scores", m // 2))
                nc.scalar.activation(probs[:, m, :], bank_s[m % 2][:, :], ACT.Exp, scale=DQK ** -0.5).then_inc(s.drained, 1)

            def keep_ln1T(i):
                for h in range(2):
                    act.wait_ge(Cb[h].filled, Cb[h].full(i, "ln1"))
                    nc.scalar.activation(lnT[:, h * HALF:(h + 1) * HALF], bank_c[h][:, :], ACT.Identity,
                                         accum_out=ln1_sum[:, h:h + 1]).then_inc(Cb[h].drained, 1)

            def keep_weff(i):
                for hd in range(HEADS):
                    s = S[hd % 2]
                    act.wait_ge(s.filled, s.full(i, "weff", hd // 2))
                    nc.scalar.copy(weff[:, :, hd, :], bank_s[hd % 2][:, :].rearrange("p (k c) -> p k c", c=C)).then_inc(s.drained, 1)

            def keep_ln2T(i):
                for h in range(2):
                    act.wait_ge(Cb[h].filled, Cb[h].full(i, "ln2"))
                    nc.scalar.copy(lnT[:, h * HALF:(h + 1) * HALF], bank_c[h][:, :]).then_inc(Cb[h].drained, 1)

            def gate_exp(i):
                act.wait_ge(Cb[0].drained, Cb[0].after(i, "route"))
                nc.scalar.activation(prob[:].rearrange("p n e -> p (n e)"), logit[:].rearrange("p n e -> p (n e)"),
                                     ACT.Exp).then_inc(exp_ready, 1)

            act.wait_ge(loaded["wqk"], 48)
            def image(i, first=False, last=False):
                for m in range(TILES):
                    exps(i, m)
                if not first:
                    keep_ln2T(i - 1)
                    gate_exp(i - 1)
                if not last:
                    stack_sums(i + 1)
                    keep_xt(i + 1)
                keep_ln1T(i)
                keep_weff(i)
                if not last:
                    max_rows(i + 1)

            stack_sums(0)
            keep_xt(0)
            max_rows(0)
            image(0, first=True)
            with act.Fori(1, IMAGES - 1) as i:
                image(i)
            image(IMAGES - 1, last=True)
            keep_ln2T(IMAGES - 1)
            gate_exp(IMAGES - 1)

            def silu(t, k):
                act.wait_ge(h13_ready, t + 1)
                at_least(act, hidden_ready, t - 1)
                nc.scalar.activation(silu1[k % 2], bank_s[k % 2][:, H13:H13 + HID], ACT.Silu).then_inc(silu_ready, 1)

            def high_part(t, k):
                act.wait_ge(x_turned, t + 1)
                at_least(act, h13_ready, t - 1)
                nc.scalar.copy(x_hi[k % 2][:], bank_a[k % 2][:, 0:P]).then_inc(x_hi_ready, 1)

            def keep_y(t, k):
                act.wait_ge(y_ready, t + 1)
                if not isinstance(t, int) or t >= SLOTS8:
                    act.wait_ge(scattered[k], scattered_value(t, k) - 16)
                nc.scalar.copy(y_rows[k], bank_c[1][:, 0:C]).then_inc(y_kept, 1)

            def tile(t, k):
                silu(t, k)
                if not isinstance(t, int) or t + 2 < FFN_TILES:
                    high_part(t + 2, (k + 2) % SLOTS8)
                if not isinstance(t, int) or t >= 2:
                    keep_y(t - 2, (k - 2) % SLOTS8)

            high_part(0, 0)
            high_part(1, 1)
            experts_loop(act, tile)
            for t in (FFN_TILES - 2, FFN_TILES - 1):
                keep_y(t, t % SLOTS8)

            with act.Fori(0, IMAGES) as i:
                for b in range(2):
                    act.wait_ge(mix_turned[b], i + 2)
                    act.wait_ge(out_stored[b], i * 16 + 16)
                    nc.scalar.copy(y_out[b], bank_a[b][:, :]).then_inc(out_kept[b], 1)
                    act.wait_ge(out_kept[b], i + 2)
                    act.dma_start(out[bass.ds(i, 1), :, b * HALF:(b + 1) * HALF].rearrange("i c n -> c (i n)"), y_out[b]).then_inc(out_stored[b], 16)

        @block.vector
        def _(dve):
            V = nc.vector

            def step(ins, s, start, n):
                ins.then_inc(s, 1)
                dve.wait_ge(s, start + n)

            def bcast_e(ap):
                return ap.unsqueeze(2).broadcast_to([P, TILES, EXPERTS])

            def make_stacks(i):
                s0 = i * STACK_STEPS + 1
                for h in range(2):
                    dve.wait_ge(A[h].drained, A[h].after(i, "qk"))
                step(V.tensor_copy(qk_hi[:], qk_sum[:]), stack_step, s0, 1)
                for k, (dst, lo) in enumerate(((q_stack, 0), (k_stack, STACK))):
                    rows = slice(lo, lo + STACK)
                    V.scalar_tensor_tensor(out=dst[0:STACK, :], in0=qk_hi[rows, :].bitcast(F32), scalar=cst_s[rows, C_LOW:C_LOW + 1],
                                           in1=qk_sum[rows, :], op0=ALU.mult, op1=ALU.add).then_inc(stack_step, 1)

            def keep_v(i):
                for h in range(2):
                    dve.wait_ge(A[h].filled, A[h].full(i, "v"))
                    for j in range(4):
                        last = V.scalar_tensor_tensor(out=v_ext[:, 4 * h + j, 0:C], in0=bank_a[h][:, j * C:(j + 1) * C],
                                                      scalar=vec_s[:, 1:2], in1=gbv[:], op0=ALU.mult, op1=ALU.add)
                    last.then_inc(A[h].drained, 1)

            def row_max(i, n):
                for h in range(2):
                    dve.wait_ge(A[h].filled, A[h].full(i, "scores", n))
                    V.reduce_max(row_max2[:, n, h:h + 1], bank_a[h][:, :], AX_X).then_inc(A[h].drained, 1)

            def negate_max(i):
                s0 = i * MAX_STEPS
                for h in range(2):
                    dve.wait_ge(A[h].drained, A[h].after(i, "scores", TILES - 1))
                step(V.tensor_reduce(neg_max[:], row_max2[:], AX_X, ALU.max, negate=True), max_step, s0, 1)
                step(V.tensor_copy(neg_max_hi[:], neg_max[:]), max_step, s0, 2)
                V.tensor_copy(max_cols[:, :, STACK], neg_max_hi[:].bitcast(F32)).then_inc(max_step, 1)
                V.tensor_tensor(max_cols[:, :, STACK + 1], neg_max[:], neg_max_hi[:].bitcast(F32), ALU.subtract).then_inc(max_step, 1)

            def attended(i, n):
                c = Cb[n % 2]
                dve.wait_ge(c.filled, c.full(i, "pv", n // 2))
                s0 = (i * TILES) + n
                V.reciprocal(rden[:, n:n + 1], bank_c[n % 2][:, C:VCOLS]).then_inc(den_ready, 1)
                dve.wait_ge(den_ready, s0 + 1)
                V.scalar_tensor_tensor(out=t1[:, n, :], in0=bank_c[n % 2][:, 0:C], scalar=rden[:, n:n + 1],
                                       in1=xt[:, n, :], op0=ALU.mult, op1=ALU.add).then_inc(c.drained, 1)

            def norm(i, src, dst, first, which, eps, stats_made=0):
                s0 = i * NORM_STEPS
                for n in range(stats_made, TILES):
                    last = V.bn_stats(stats[:, n, :], src(n))
                last.then_inc(norm_step, 1)
                wait_apart(dve, norm_step, s0 + (first + 1))
                for n in range(TILES):
                    last = V.bn_aggr(mean_var[:, n, :], stats[:, n, :])
                step(last, norm_step, s0, first + 2)
                V.tensor_scalar(var_eps[:], mean_var[:, :, 1], eps, None, ALU.add).then_inc(norm_step, 1)
                dve.wait_ge(rstd_ready, i * 2 + (which + 1))
                for n in range(TILES):
                    last = V.tensor_scalar(dst[:, n, :], src(n), mean_var[:, n, 0:1], rstd[:, n:n + 1], ALU.subtract, ALU.mult)
                last.then_inc(norm_step, 1)

            def head_weights(i):
                s0 = i * NORM_STEPS
                dve.wait_ge(Cb[0].filled, Cb[0].full(i, "qsum"))
                V.tensor_reduce(qsum[:], bank_c[0][:, 0:2 * HEADS].rearrange("p (h t) -> p h t", t=2), AX_X, ALU.add).then_inc(Cb[0].drained, 1)
                dve.wait_ge(Cb[0].drained, Cb[0].after(i, "qsum"))
                step(V.tensor_tensor(qsum[:], qsum[:], nbq[:], ALU.add), norm_step, s0, 5)
                step(V.tensor_scalar(g_head[:], qsum[:], lunch_sum[:, 0:1], None, ALU.mult), norm_step, s0, 6)
                V.tensor_tensor(g_bv[:], g_head[:], bvD_s[:], ALU.mult)
                V.tensor_tensor(g_wv[:], wvD_s[:], g_head[:].unsqueeze(2).broadcast_to([P, HEADS, C]), ALU.mult).then_inc(norm_step, 1)

            def linear_attended(i):
                dve.wait_ge(bias_added, i + 1)
                for h in range(2):
                    dve.wait_ge(Cb[h].filled, Cb[h].full(i, "attn"))
                    V.tensor_tensor(t2[:, bass.ds(i * TILES + 4 * h, 4), :], bank_c[h][:, :].rearrange("p (n c) -> p n c", c=C),
                                    t1[:, 4 * h:4 * h + 4, :], ALU.add).then_inc(Cb[h].drained, 1)
                dve.wait_ge(loaded["cst"], 32)
                for h in range(2):
                    dve.wait_ge(Cb[h].drained, Cb[h].after(i, "attn"))

            mx, z, first, wmax, m2, den = (small[:, k, :] for k in range(6))
            rev = cst_s[:, C_RANK:C_RANK + EXPERTS].unsqueeze(1).broadcast_to([P, TILES, EXPERTS])
            flat = "p n e -> p (n e)"

            def gate_chain(i, from_step):
                done = [from_step]

                def at(ins):
                    done[0] += 1
                    step(ins, gate_step, i * GATE_STEPS, done[0])

                return at

            def gate_probs(i):
                at = gate_chain(i, 0)
                psl = bank_c[0][:, 0:TILES * EXPERTS].rearrange("p (n e) -> p n e", e=EXPERTS)
                dve.wait_ge(Cb[0].filled, Cb[0].full(i, "route"))
                at(V.tensor_reduce(mx, psl, AX_X, ALU.max))
                V.tensor_tensor(logit[:], psl, bcast_e(mx), ALU.subtract).then_inc(Cb[0].drained, 1)

            def pick_top(i, k):
                at = gate_chain(i, 4 if k == 0 else 10)
                top = (first, m2)[k]
                if k == 0:
                    at = gate_chain(i, 1)
                    dve.wait_ge(exp_ready, i + 1)
                    at(V.tensor_reduce(z, prob[:], AX_X, ALU.add))
                    at(V.reciprocal(z, z))
                    at(V.tensor_tensor(prob[:], prob[:], bcast_e(z), ALU.mult))
                at(V.tensor_reduce(top, prob[:], AX_X, ALU.max))
                at(V.tensor_tensor(tie[:], prob[:], bcast_e(top), ALU.is_equal))
                at(V.tensor_tensor(tie[:], tie[:], rev, ALU.mult))
                at(V.tensor_reduce(wmax, tie[:], AX_X, ALU.max))
                at(V.tensor_tensor(pick[:, k], tie[:], bcast_e(wmax), ALU.is_equal))
                if k == 0:
                    at(V.scalar_tensor_tensor(out=prob[:].rearrange(flat), in0=pick[:, 0].rearrange(flat), scalar=-2.0,
                                              in1=prob[:].rearrange(flat), op0=ALU.mult, op1=ALU.add))

            def set_gates(i):
                at = gate_chain(i, 15)
                g = [gates[:, k, bass.ds(i * TILES, TILES)] for k in range(2)]
                at(V.tensor_tensor(both[:], pick[:, 0], pick[:, 1], ALU.add))
                at(V.tensor_tensor(den, first, m2, ALU.add))
                at(V.tensor_scalar(den, den, 1e-9, None, ALU.add))
                at(V.reciprocal(den, den))
                at(V.tensor_tensor(g[0], first, den, ALU.mult))
                at(V.tensor_tensor(g[1], m2, den, ALU.mult))

            def set_slots(i):
                at = gate_chain(i, 21)
                W = TILES * EXPERTS
                dve.wait_ge(S[0].filled, S[0].full(i + 1, rank_use(i)))
                at(V.tensor_tensor(logit[:], bank_s[0][:, 0:W].rearrange("p (n e) -> p n e", e=EXPERTS),
                                   base[:].unsqueeze(1).broadcast_to([P, TILES, EXPERTS]), ALU.add))
                V.tensor_tensor(base[:], bank_s[0][:, W:W + EXPERTS], base[:], ALU.add).then_inc(S[0].drained, 1)
                at(V.tensor_tensor(pick[:], pick[:], logit[:].unsqueeze(1).broadcast_to([P, 2, TILES, EXPERTS]), ALU.mult))
                slot_f = small[:, 6:8, :].rearrange("p k n -> p (k n)")
                at(V.tensor_reduce(slot_f, pick[:].rearrange("p k n e -> p (k n) e"), AX_X, ALU.add))
                dve.wait_ge(tok_step, i + 1)
                at(V.tensor_copy(slots[:], slot_f))

            def norm2(i):
                wait_apart(dve, ln2_stored, 16 * i + 16)
                norm(i, lambda n: t2[:, bass.ds(i * TILES + n, 1), :], ln2, 7, 1, 1e-5)

            def image(i, first=False, last=False):
                if not first:
                    norm2(i - 1)
                    gate_probs(i - 1)
                for n in range(TILES):
                    attended(i, n)
                    if not first:
                        if n < 2:
                            pick_top(i - 1, n)
                        if n == 2:
                            set_gates(i - 1)
                        if n == RANK_AFTER:
                            set_slots(i - 1)
                dve.wait_ge(loaded["cst"], 32)
                for h in range(2):
                    dve.wait_ge(Cb[h].drained, Cb[h].after(i, "pv", K - 1))
                norm(i, lambda n: t1[:, n, :], ln1, 0, 0, 1e-5)
                if not last:
                    make_stacks(i + 1)
                    keep_v(i + 1)
                head_weights(i)
                if not last:
                    for n in range(TILES):
                        row_max(i + 1, n)
                    negate_max(i + 1)
                linear_attended(i)

            V.memset(max_cols[:], 0.0).then_inc(consts_made, 1)
            V.memset(v_ext[:, :, C:VCOLS], 1.0).then_inc(consts_made, 1)
            V.memset(k_stack[STACK:STACK + 2, :].bitcast(F32), 1.0).then_inc(consts_made, 1)
            for bank in (*A, *S, *Cb):
                dve.sem_inc(bank.drained, 1)
            for s, by in ((stack_step, 1), (tok_step, 1), (ln2_stored, 16)):
                dve.sem_inc(s, by)
            for b in range(2):
                for s, by in ((y_mixed[b], 1), (mix_turned[b], 1), (out_kept[b], 1), (out_stored[b], 16)):
                    dve.sem_inc(s, by)
            dve.wait_ge(loaded["wqk"], 48)
            dve.wait_ge(loaded["cst"], 32)
            dve.wait_ge(loaded["wv"], 32)
            V.tensor_scalar(gbv[:], bvB_s[:], vec_s[:, 1:2], None, ALU.mult).then_inc(consts_made, 1)
            dve.wait_ge(loaded["attn"], 16 * 7)
            V.tensor_scalar(nbq[:], bq_s[:], float(N), None, ALU.mult).then_inc(setup, 1)
            V.tensor_reduce(lunch_sum[:], lunch_s[:], AX_X, ALU.add).then_inc(setup, 1)
            V.tensor_reduce(wp_sum[:], wp_s[:].rearrange("p k c -> p c k"), AX_X, ALU.add).then_inc(consts_made, 1)
            V.tensor_copy(base[:], cst_s[:, C_BASE:C_BASE + EXPERTS]).then_inc(setup, 1)
            dve.wait_ge(setup, 3)
            V.tensor_scalar(lunch_sum[:], lunch_sum[:], float(max(P, lunch.shape[1])) ** -0.5, None, ALU.mult).then_inc(setup, 1)
            dve.wait_ge(setup, 4)
            dve.wait_ge(consts_made, 5)
            make_stacks(0)
            keep_v(0)
            for n in range(TILES):
                row_max(0, n)
            negate_max(0)
            image(0, first=True)
            with dve.Fori(1, IMAGES - 1) as i:
                image(i)
            image(IMAGES - 1, last=True)
            norm2(IMAGES - 1)
            gate_probs(IMAGES - 1)
            for k in range(2):
                pick_top(IMAGES - 1, k)
            set_gates(IMAGES - 1)
            set_slots(IMAGES - 1)

            marks = [0]

            def then(ins):
                marks[0] += 1
                step(ins, table_step, 0, marks[0])

            then(V.tensor_tensor(counts[:], base[:], cst_s[:, C_BASE:C_BASE + EXPERTS], ALU.subtract))
            then(V.tensor_scalar(counts_i[:], counts[:], float(P - 1), None, ALU.add))
            then(V.tensor_scalar(counts_i[:], counts_i[:], P.bit_length() - 1, None, ALU.arith_shift_right))
            then(V.tensor_copy(n_tiles[:], counts_i[:]))
            then(V.tensor_copy(ends[:], n_tiles[:]))
            for e in range(1, EXPERTS):
                then(V.tensor_tensor(ends[:, e:e + 1], ends[:, e - 1:e], ends[:, e:e + 1], ALU.add))
            at_row = cst_s[:, C_ROW:C_ROW + 1]
            expert, before, row = (tile_at[:, k:k + 1] for k in range(3))
            then(V.tensor_scalar(ended[:], ends[:], at_row, None, ALU.is_le))
            then(V.tensor_reduce(expert, ended[:], AX_X, ALU.add))
            then(V.tensor_tensor(ended[:], ended[:], n_tiles[:], ALU.mult))
            then(V.tensor_reduce(before, ended[:], AX_X, ALU.add))
            then(V.tensor_tensor(row, at_row, before, ALU.subtract))
            then(V.scalar_tensor_tensor(out=row, in0=expert, scalar=float(REGION // P), in1=row, op0=ALU.mult, op1=ALU.add))
            V.tensor_copy(tile_row[:], row).then_inc(rows_ready, 1)
            tiles = cst_s[0:1, C_TILE:C_TILE + FFN_TILES]
            wide = [1, FFN_TILES, EXPERTS]
            then(V.tensor_tensor(past[:], tiles.unsqueeze(2).broadcast_to(wide), ends[0:1, :].unsqueeze(1).broadcast_to(wide), ALU.is_ge))
            then(V.tensor_reduce(expert_f[:], past[:], AX_X, ALU.add))
            then(V.scalar_tensor_tensor(out=expert_f[:], in0=expert_f[:], scalar=float(EXPERTS - 1), in1=cst_s[0:1, C_DIGIT:C_DIGIT + FFN_TILES],
                                        op0=ALU.min, op1=ALU.mult))
            then(V.memset(table[:, 0:1], 0))
            then(V.tensor_reduce(word_f[:], expert_f[:].rearrange("p (g k) -> p g k", k=SLOTS8), AX_X, ALU.add))
            then(V.tensor_copy(table[:, 1:1 + GROUPS], word_f[:]))
            V.memset(hidden[0][:, HID:3 * CHUNK], 0.0).then_inc(hidden_pad, 1)
            V.memset(hidden[1][:, HID:3 * CHUNK], 0.0).then_inc(table_ready, 1)

            def ready_token(t, k):
                V.tensor_scalar(tok_slot[:, k:k + 1], ids[:, bass.ds(t, 1)], TOKENS - 1, None, ALU.bitwise_and).then_inc(slot_ready, 1)

            def ready_result(t, k):
                if not isinstance(t, int) or t >= SLOTS8:
                    dve.wait_ge(scattered[k], scattered_value(t, k) - 16)
                V.tensor_scalar(id_slot[:, k:k + 1], ids[:, bass.ds(t, 1)], 0, None, ALU.bitwise_or)

            def low_part(t, k):
                dve.wait_ge(x_hi_ready, t + 1)
                V.tensor_tensor(x_lo[k % 2][:], bank_a[k % 2][:, 0:P], x_hi[k % 2][:].bitcast(F32), ALU.subtract).then_inc(x_lo_ready, 1)

            def multiply(t, k):
                dve.wait_ge(silu_ready, t + 1)
                at_least(dve, hidden_turned, t - 1)
                V.tensor_tensor(hidden[k % 2][:, 0:HID], silu1[k % 2], bank_s[k % 2][:, H13 + HID:H13 + HID2], ALU.mult).then_inc(hidden_ready, 1)

            def keep_hiddenT(t, k):
                dve.wait_ge(hidden_turned, t + 1)
                at_least(dve, y_ready, t - 1)
                V.tensor_copy(hiddenT[k % 2][0:CHUNK], bank_c[0][0:CHUNK, 0:3 * P].rearrange("p (k n) -> p k n", n=P)).then_inc(hiddenT_ready, 1)

            def tile(t, k):
                multiply(t, k)
                if not isinstance(t, int) or t + 2 < FFN_TILES:
                    low_part(t + 2, (k + 2) % SLOTS8)
                if not isinstance(t, int) or t >= 1:
                    keep_hiddenT(t - 1, (k - 1) % SLOTS8)
                if not isinstance(t, int) or t + AHEAD + 1 < FFN_TILES:
                    ready_token(t + AHEAD + 1, (k + AHEAD + 1) % SLOTS8)
                if not isinstance(t, int) or t + 1 < FFN_TILES:
                    ready_result(t + 1, (k + 1) % SLOTS8)

            dve.wait_ge(ids_loaded, 16)
            V.tensor_copy(ids_rows_f[:], ids_rows[:]).then_inc(ids_exact, 1)
            dve.wait_ge(ids_turned, 1)
            V.tensor_copy(ids[:], bank_c[1][:, 0:FFN_TILES]).then_inc(ids_ready, 1)
            dve.wait_ge(ids_ready, 1)
            for t in range(AHEAD + 1):
                ready_token(t, t)
            ready_result(0, 0)
            low_part(0, 0)
            low_part(1, 1)
            experts_loop(dve, tile)
            keep_hiddenT(FFN_TILES - 1, SLOTS8 - 1)

            with dve.Fori(0, IMAGES) as i:
                for b in range(2):
                    dve.wait_ge(y_loaded[b], i * 32 + 32)
                    for j in range(4):
                        n = i * TILES + (4 * b + j)
                        last = V.scalar_tensor_tensor(out=t2[:, bass.ds(n, 1), :], in0=y_in[b][0][:, j, :], scalar=gates[:, 0, bass.ds(n, 1)],
                                                      in1=t2[:, bass.ds(n, 1), :], op0=ALU.mult, op1=ALU.add)
                    last.then_inc(mix_step, 1)
                    dve.wait_ge(mix_step, i * 2 + (b + 1))
                    dve.wait_ge(mix_turned[b], i + 1)
                    for j in range(4):
                        n = i * TILES + (4 * b + j)
                        last = V.scalar_tensor_tensor(out=mixed[b][:, j, :], in0=y_in[b][1][:, j, :], scalar=gates[:, 1, bass.ds(n, 1)],
                                                      in1=t2[:, bass.ds(n, 1), :], op0=ALU.mult, op1=ALU.add)
                    last.then_inc(y_mixed[b], 1)

        @block.gpsimd
        def _(pool):
            G = nc.gpsimd
            G.memset(minus_half[:], -0.5).then_inc(pool_made, 1)
            pool.wait_ge(pool_made, 1)
            for e in range(EXPERTS):
                pool.wait_ge(w13_loaded[e % 2], 16 * (e // 2 + 1))
                G.tensor_copy(w13_hi[:, e], w13_raw[:, e % 2]).then_inc(w13_split, 1)
                pool.wait_ge(w13_split, 2 * e + 1)
                G.tensor_tensor(w13_lo[:, e], w13_raw[:, e % 2], w13_hi[:, e].bitcast(F32), ALU.subtract).then_inc(w13_split, 1)

            def rstds(i, which):
                pool.wait_ge(norm_step, i * NORM_STEPS + (3 + 7 * which))
                G.tensor_tensor(rstd[:], var_eps[:], minus_half[:], ALU.pow).then_inc(rstd_ready, 1)

            def scatter_ids(i):
                wait_apart(pool, gate_step, i * GATE_STEPS + GATE_STEPS)
                for k in range(2 * TILES):
                    G.indirect_dma_start(ids_dram, bass.IndirectOffsetOnAxis(ap=slots[:, k:k + 1], axis=0),
                                         tok[:, k:k + 1], None).then_inc(ids_stored, 16)
                wait_apart(pool, ids_stored, 16 * 2 * TILES * (i + 1))
                G.tensor_scalar(tok[:], tok[:], float(N), None, ALU.add).then_inc(tok_step, 1)
                pool.wait_ge(tok_step, i + 2)

            pool.wait_ge(ids_cleared, 16)
            pool.wait_ge(loaded["attn"], 16 * 7)
            pool.wait_ge(loaded["tok"], 16)
            def image(i, first=False):
                rstds(i, 0)
                pool.wait_ge(norm_step, i * NORM_STEPS + LN1_STEP)
                G.tensor_tensor(t1[:], t1[:], bpB_s[:].unsqueeze(1).broadcast_to([P, TILES, C]), ALU.add).then_inc(bias_added, 1)
                if not first:
                    scatter_ids(i - 1)
                rstds(i, 1)

            image(0, first=True)
            with pool.Fori(1, IMAGES) as i:
                image(i)
            scatter_ids(IMAGES - 1)

            def gather(t, k):
                if not isinstance(t, int) or t >= SLOTS8:
                    pool.wait_ge(x_turned, t - (SLOTS8 - 1))
                wait_apart(pool, slot_ready, t + 1)
                G.indirect_dma_start(x_rows[k], None, ln2_dram, bass.IndirectOffsetOnAxis(ap=tok_slot[:, k:k + 1], axis=0)).then_inc(gathered[k], 16)

            def scatter(t, k):
                wait_apart(pool, y_kept, t + 1)
                G.indirect_dma_start(y_dram, bass.IndirectOffsetOnAxis(ap=id_slot[:, k:k + 1], axis=0), y_rows[k], None).then_inc(scattered[k], 16)

            def tile(t, k):
                if not isinstance(t, int) or t + AHEAD < FFN_TILES:
                    gather(t + AHEAD, (k + AHEAD) % SLOTS8)
                scatter(t, k)

            pool.wait_ge(ids_stored, 16 * 2 * TILES * IMAGES)
            pool.wait_ge(ln2_stored, 16 * IMAGES + 16)
            pool.wait_ge(rows_ready, 1)
            G.indirect_dma_start(ids_rows[:], None, ids_dram.rearrange("(a b) c -> a (b c)", b=P),
                                 bass.IndirectOffsetOnAxis(ap=tile_row[0:FFN_TILES, :], axis=0)).then_inc(ids_loaded, 16)
            for t in range(AHEAD):
                gather(t, t)
            experts_loop(pool, tile)

def host_layout(np, ml, d):
    f = {k: np.ascontiguousarray(np.asarray(v)) for k, v in d.items()}
    images, c, hh, ww = f["x"].shape
    n = hh * ww
    tiles = n // P
    tokens = images * n
    dim, r = f["L1_attn_lunchbox"].shape
    heads = f["L1_attn_proj_w"].shape[0] // dim
    experts, hid, _ = f["L1_ffn_w1"].shape
    chunk = -(-hid // 3)
    ident = np.eye(P, dtype=np.float32)
    dqk = f["L0_conv_Wq"].shape[0]
    low = np.zeros((P, 1), np.float32)
    for k in (2, 3, 5, 7):
        low[k * dqk:(k + 1) * dqk] = -1.0
    e = np.arange(experts, dtype=np.float32)
    cst = np.concatenate([ident, low, np.tile(experts - e, (P, 1)), np.tile(e * tokens, (P, 1)), np.tile(np.arange(FFN_MAX), (P, 1)),
                          np.arange(P)[:, None], np.tile(float(experts) ** (np.arange(FFN_MAX) % 8), (P, 1))], 1).astype(np.float32)
    tri = np.concatenate([np.triu(np.ones((P, P)), 1), np.ones((P, P))], 1).astype(ml.bfloat16)
    tok = np.arange(2)[:, None, None] * tokens + np.arange(tiles)[None, :, None] * P + np.arange(P)[None, None, :]
    tok = tok.reshape(2 * tiles, P).T.astype(np.int32)
    rows = np.arange(P)
    pad = [np.tile(2 * tokens + P * k + rows, tokens // P) for k in range(experts)]
    pad += [2 * tokens + P * (experts + k) + rows for k in range(experts)]
    pad = np.concatenate(pad).astype(np.int32).reshape(-1, (experts * (tokens + P)) // P)
    w = f["L1_attn_qkv_w"]
    bq, bv = f["L1_attn_qkv_b"][:heads * dim], f["L1_attn_qkv_b"][heads * dim:]
    w2 = np.transpose(f["L1_ffn_w2"], (2, 0, 1))
    w2p = np.zeros((3 * chunk, experts, c), np.float32)
    w2p[:hid] = w2
    return {
        "x": f["x"].reshape(images, c, n), "cst": cst, "tri": tri, "tokid": tok, "pad_ids": pad,
        "wqk": np.concatenate([f["L0_conv_Wq"].T] * 4 + [f["L0_conv_Wk"].T] * 4, 1),
        "bqk": np.concatenate([f["L0_conv_bq"]] * 4 + [f["L0_conv_bk"]] * 4)[:, None],
        "wvT": f["L0_conv_Wv"].T, "bvB": np.tile(f["L0_conv_bv"], (P, 1)), "gammaB": np.tile(f["L0_conv_gamma"], (P, 1)),
        "wq": w[:, :heads * dim], "bq": bq.reshape(heads, dim).T, "lunch": f["L1_attn_lunchbox"],
        "wvD": w[:, heads * dim:].T.reshape(heads, dim, c).transpose(1, 0, 2),
        "bvD": bv.reshape(heads, dim).T,
        "wp": f["L1_attn_proj_w"].reshape(heads, dim, c).transpose(1, 0, 2),
        "bpB": np.tile(f["L1_attn_proj_b"], (P, 1)), "routerT": f["L1_ffn_router_w"].T,
        "w13": np.concatenate([f["L1_ffn_w1"], f["L1_ffn_w3"]], 1).transpose(2, 0, 1),
        "w2T": w2p.reshape(3, chunk, experts, c).transpose(1, 0, 2, 3),
    }


_ORDER = ["x", "cst", "tri", "tokid", "pad_ids", "wqk", "bqk", "wvT", "bvB", "gammaB", "wq", "bq", "lunch", "wvD", "bvD", "wp",
          "bpB", "routerT", "w13", "w2T"]


def kernel(**inputs):
    import ml_dtypes
    import numpy as np
    import concourse.bacc as bacc
    from concourse.bass_utils import run_bass_kernel_spmd

    nc = bacc.Bacc("TRN2", target_bir_lowering=False, num_devices=1)
    layout = host_layout(np, ml_dtypes, inputs)
    arrays, args = {}, []
    for name in _ORDER:
        a = np.ascontiguousarray(layout[name])
        arrays[f"in_{name}_dram"] = a
        args.append(nc.dram_tensor(f"in_{name}_dram", a.shape, mybir.dt.from_np(a.dtype), kind="ExternalInput").ap())
    shape = inputs["x"].shape
    flat = (shape[0], shape[1], shape[2] * shape[3])
    args.append(nc.dram_tensor("out_0_dram", flat, F32, kind="ExternalOutput").ap())
    conv_attn_moe_kernel(nc, *args)
    r = run_bass_kernel_spmd(nc, [arrays], core_ids=[0])
    return r.results[0]["out_0_dram"].reshape(shape)
```

```python
from contextlib import ExitStack

import concourse.bass as bass
from concourse import mybir

ALU = mybir.AluOpType
ACT = mybir.ActivationFunctionType
AX_X = mybir.AxisListType.X
F32 = mybir.dt.float32
F32R = mybir.dt.float32r
BF16 = mybir.dt.bfloat16
I32 = mybir.dt.int32

P = 128

C_IDENT = 0
C_LOW = 128
C_RANK = 129
C_BASE = 137
C_TILE = 145
FFN_MAX = 72
C_ROW = C_TILE + FFN_MAX
C_DIGIT = C_ROW + 1
C_IOTA = C_DIGIT + FFN_MAX
C_HIGH = C_IOTA + P
C_COLS = C_HIGH + 16


class Uses:

    def __init__(self, filled, drained, total, **first):
        self.filled, self.drained, self.total, self.first = filled, drained, total, first

    def before(self, i, use, n=0):
        return i * self.total + (self.first[use] + n + 1)

    def after(self, i, use, n=0):
        return i * self.total + (self.first[use] + n + 2)

    def full(self, i, use, n=0):
        return i * self.total + (self.first[use] + n + 1)


def conv_attn_moe_kernel(nc, x, cst, tri, tokid, pad_ids, wqk, bqk, wvT, bvB, gammaB, wq, bq, lunch, wvD, bvD, wp, bpB,
                         routerT, w13, w2T, out):
    IMAGES, C, N = x.shape
    TILES = N // P
    TOKENS = IMAGES * N
    DQK = 16
    STACK = 4 * DQK
    HEADS = wp.shape[1]
    EXPERTS = routerT.shape[1]
    HID2 = w13.shape[2]
    HID = HID2 // 2
    CHUNK = -(-HID // 3)
    REGION = TOKENS
    FFN_TILES = 2 * TOKENS // P + EXPERTS
    assert FFN_TILES == FFN_MAX
    RESULTS = 2 * TOKENS + 2 * EXPERTS * P
    HALVES = 2 * IMAGES
    SLOTS8 = 8
    GROUPS = FFN_TILES // SLOTS8
    AHEAD = 6
    H13 = 170
    W_A = HID2 // 2 + 1
    SLOTS = pad_ids.shape[0] * pad_ids.shape[1]
    HALF = N // 2
    VCOLS = C + 1

    ids_dram = nc.dram_tensor("ids_dram", [SLOTS, 1], I32, kind="Internal").ap()
    ln2_dram = nc.dram_tensor("ln2_dram", [TOKENS, C], F32, kind="Internal").ap()

    y_dram = nc.dram_tensor("y_dram", [RESULTS, C], F32, kind="Internal").ap()

    with ExitStack() as ctx:
        def sb(name, shape, dt=F32):
            return ctx.enter_context(nc.sbuf_tensor(name + "_sb", shape, dt))

        def psum(name, shape):
            return ctx.enter_context(nc.psum_tensor(name, shape, F32))

        def sem(name):
            return ctx.enter_context(nc.semaphore(name))

        cst_s = sb("cst_s", [P, C_COLS])
        tri_s = sb("tri_s", [P, 2 * P], BF16)
        wqk_s = sb("wqk_s", [P, P])
        wvT_s = sb("wvT_s", [P, C])
        vec_s = sb("vec_s", [P, 2])
        bvB_s = sb("bvB_s", [P, C])
        wq_s = sb("wq_s", [P, HEADS * P])
        bq_s = sb("bq_s", [P, HEADS])
        lunch_s = sb("lunch_s", [P, lunch.shape[1]])
        wvD_s = sb("wvD_s", [P, HEADS, C])
        bvD_s = sb("bvD_s", [P, HEADS])
        wp_hi = sb("wp_hi", [P, HEADS, C], F32R)
        wp_lo = sb("wp_lo", [P, HEADS, C], F32R)
        bpB_s = sb("bpB_s", [P, C])
        routerT_s = sb("routerT_s", [P, EXPERTS])
        weights = sb("weights", [P, 2 * HEADS * HEADS * C])
        weff_hi, weff_lo = (weights[:, k * HEADS * HEADS * C:(k + 1) * HEADS * HEADS * C].bitcast(F32R)
                            .rearrange("p (k h c) -> p k h c", h=HEADS, c=C) for k in range(2))
        W13 = EXPERTS * HID2
        w13_hi, w13_lo = (weights[:, k * W13:(k + 1) * W13].bitcast(F32R) for k in range(2))

        xc = sb("xc", [P, N])
        qk_sum = sb("qk_sum", [P, N])
        qk_hi = sb("qk_hi", [P, N], F32R)
        q_stack = sb("q_stack", [STACK + 2, N], F32R)
        k_stack = sb("k_stack", [STACK + 2, N], F32R)
        gbv = sb("gbv", [P, C])
        v_ext = sb("v_ext", [P, TILES, VCOLS])
        xt = sb("xt", [P, TILES, C])
        row_max2 = sb("row_max2", [P, TILES, 2])
        neg_max = sb("neg_max", [P, TILES])
        neg_max_hi = sb("neg_max_hi", [P, TILES], F32R)
        max_cols = sb("max_cols", [P, TILES, STACK + 2])
        probs = sb("probs", [P, TILES, N])
        rden = sb("rden", [P, TILES])
        t1 = sb("t1", [P, TILES, C])
        stats = sb("stats", [P, TILES, 6])
        mean_var = sb("mean_var", [P, TILES, 2])
        var_eps = sb("var_eps", [P, TILES])
        minus_half = sb("minus_half", [P, TILES])
        rstd = sb("rstd", [P, TILES])
        ln1 = sb("ln1", [P, TILES, C])
        lnT = sb("lnT", [P, N])
        lnT_hi = sb("lnT_hi", [P, N], F32R)
        lnT_lo = sb("lnT_lo", [P, N], F32R)
        ln1_sum = sb("ln1_sum", [P, 2])
        nbq = sb("nbq", [P, HEADS])
        lunch_sum = sb("lunch_sum", [P, 1])
        qsum = sb("qsum", [P, HEADS])
        g_head = sb("g_head", [P, HEADS])
        g_wv = qk_hi[:].bitcast(F32).rearrange("p (h c) -> p h c", c=C)
        g_wv_hi = sb("g_wv_hi", [P, HEADS, C], F32R)
        g_wv_lo = sb("g_wv_lo", [P, HEADS, C], F32R)
        g_bv = sb("g_bv", [P, HEADS])
        wp_sum = sb("wp_sum", [P, C])
        t2 = sb("t2", [P, IMAGES * TILES, C])
        wp_raw = t2[:, (IMAGES - 1) * TILES:IMAGES * TILES, :]
        ln2 = sb("ln2", [P, TILES, C])
        small = sb("small", [P, 8, TILES])
        logit = sb("logit", [P, TILES, EXPERTS])
        prob = sb("prob", [P, TILES, EXPERTS])
        tie = sb("tie", [P, TILES, EXPERTS])
        others = sb("others", [P, TILES, EXPERTS])
        lesser = sb("lesser", [P, TILES])
        second = sb("second", [P, TILES])
        pick = sb("pick", [P, 2, TILES, EXPERTS])
        both = sb("both", [P, TILES, EXPERTS], BF16)
        gates = sb("gates", [P, 2, IMAGES * TILES])
        base = sb("base", [P, EXPERTS])
        slots = sb("slots", [P, 2 * TILES], I32)
        tok = sb("tok", [P, 2 * TILES], I32)

        counts_before = sb("counts_before", [P, EXPERTS])
        counts = sb("counts", [P, EXPERTS])
        packed = sb("packed", [P, EXPERTS])
        last_place = sb("last_place", [P, 2, 2 * TILES])
        last_int = sb("last_int", [P, 2, 2 * TILES], I32)
        ids_f = sb("ids_f", [P, FFN_TILES])
        counts_i = sb("counts_i", [P, EXPERTS], I32)
        n_tiles = sb("n_tiles", [P, EXPERTS])
        ends = sb("ends", [P, EXPERTS])
        past = sb("past", [1, FFN_TILES, EXPERTS])
        ended = sb("ended", [P, EXPERTS])
        tile_at = sb("tile_at", [P, 3])
        tile_row = sb("tile_row", [P, 1], I32)
        expert_f = sb("expert_f", [1, FFN_TILES])
        word_f = sb("word_f", [1, GROUPS])
        words = sb("words", [1, 1 + GROUPS], I32)
        table = sb("table", [1, GROUPS], I32)
        ids_rows = sb("ids_rows", [FFN_TILES, P], I32)
        ids_rows_f = sb("ids_rows_f", [FFN_TILES, P])
        ids = sb("ids", [P, FFN_TILES], I32)
        id_slot = sb("id_slot", [P, SLOTS8], I32)
        tok_slot = sb("tok_slot", [P, SLOTS8], I32)
        x_hi = [sb(f"x_hi{b}", [P, P], F32R) for b in range(2)]
        x_lo = [sb(f"x_lo{b}", [P, P], F32R) for b in range(2)]
        w2_s = [wq_s[0:CHUNK, :].rearrange("p (e c) -> p e c", c=C), wvD_s[0:CHUNK], xc[0:CHUNK, :].rearrange("p (e c) -> p e c", c=C)]
        spare, used = probs[:].rearrange("p m n -> p (m n)"), [0]

        def place(cols):
            used[0] += cols
            assert used[0] <= TILES * N
            return spare[:, used[0] - cols:used[0]]

        w13_raw = spare[:, 0:W13]
        of_place = xt[:].rearrange("p n c -> p (n c)").bitcast(BF16).rearrange("p (s q) -> p s q", q=P)
        of_tile = spare[:, W13:W13 + TILES * 3 * FFN_TILES].bitcast(BF16).rearrange("p (s k t) -> p s k t", k=3, t=FFN_TILES)
        x_rows = [place(C) for _ in range(SLOTS8)]
        y_rows = [place(C) for _ in range(SLOTS8)]
        silu1 = [place(HID) for _ in range(2)]
        hidden = [place(3 * CHUNK) for _ in range(2)]
        hiddenT = [place(3 * P).rearrange("p (k n) -> p k n", n=P) for _ in range(2)]
        y_in = probs[:].rearrange("p m n -> p (m n)").rearrange("p (h k n c) -> p h k n c", k=2, n=4, c=C)
        y_out = [place_of[:, 4 * h:4 * h + 4, :].rearrange("p n c -> p (n c)") for place_of in (t1, ln1, ln2, xt) for h in range(2)]

        bank_a = [psum(f"bank_a{h}", [P, 512]) for h in range(2)]
        bank_s = [psum(f"bank_s{h}", [P, N]) for h in range(2)]
        bank_c = [psum(f"bank_c{h}", [P, 512]) for h in range(2)]

        loaded = {n: sem(f"{n}_loaded") for n in ("cst", "wqk", "wv", "attn", "router", "w2", "tok")}
        x_loaded, w13_loaded, w13_parts = sem("x_loaded"), sem("w13_loaded"), sem("w13_parts")
        ids_cleared = sem("ids_cleared")
        consts_made, pool_made = sem("consts_made"), sem("pool_made")
        K = TILES // 2
        K = TILES // 2
        A = [Uses(sem("a_filled0"), sem("a_drained0"), 6 + TILES, qk=0, xt=1, v=2, scores=3, rows=3 + TILES, ln2=4 + TILES, route=5 + TILES),
             Uses(sem("a_filled1"), sem("a_drained1"), 5 + TILES, qk=0, xt=1, v=2, scores=3, rows=3 + TILES, ln2=4 + TILES)]
        S = [Uses(sem("s_filled0"), sem("s_drained0"), K + 1 + HEADS // 2, scores=0, rank=K, weff=K + 1),
             Uses(sem("s_filled1"), sem("s_drained1"), K + HEADS // 2, scores=0, weff=K)]
        Cb = [Uses(sem("c_filled0"), sem("c_drained0"), K + 3, pv=0, ln1=K, qsum=K + 1, attn=K + 2),
              Uses(sem("c_filled1"), sem("c_drained1"), K + 2, pv=0, ln1=K, attn=K + 1)]

        def routed(bank, i, use):
            past = isinstance(i, int) and i == IMAGES - 1
            first = bank.first["ln2" if "ln2" in bank.first else "rank"]
            return i + 1, use, -first if past else 0

        stack_step, max_step = sem("stack_step"), sem("max_step")
        norm_step, gate_step = sem("norm_step"), sem("gate_step")
        rstd_ready, exp_ready = sem("rstd_ready"), sem("exp_ready")
        ln2_stored, ids_stored = sem("ln2_stored"), sem("ids_stored")
        STACK_STEPS, MAX_STEPS, NORM_STEPS, GATE_STEPS = 3, 4, 24, 23
        LN1_STEP, SECOND_STEP, BOTH_STEP, SLOT_STEP = 8, 6, 11, 15
        LN2_STEP = (20, 24)
        G_STEP = (13, 16)
        setup, den_ready, tok_step, bias_added = sem("setup"), sem("den_ready"), sem("tok_step"), sem("bias_added")
        heads_made, weff_high, lnT_split = sem("heads_made"), sem("weff_high"), sem("lnT_split")
        MAX_BESIDE = [[0], [1], [2], [3], [4], [5], [6], [7]]

        table_ready, table_step = sem("table_ready"), sem("table_step")
        rows_ready, ids_loaded, ids_exact, ids_turned = sem("rows_ready"), sem("ids_loaded"), sem("ids_exact"), sem("ids_turned")
        ids_ready, placed = sem("ids_ready"), sem("placed")
        slot_ready = sem("slot_ready")
        gathered = [sem(f"gathered{k}") for k in range(SLOTS8)]
        scattered = [sem(f"scattered{k}") for k in range(SLOTS8)]
        x_turned, x_hi_ready, x_lo_ready = sem("x_turned"), sem("x_hi_ready"), sem("x_lo_ready")
        h13_ready, silu_ready, hidden_ready = sem("h13_ready"), sem("silu_ready"), sem("hidden_ready")
        hidden_turned, hiddenT_ready = sem("hidden_turned"), sem("hiddenT_ready")
        y_ready, y_kept, hidden_pad = sem("y_ready"), sem("y_kept"), sem("hidden_pad")
        y_loaded = [sem(f"y_loaded{h}") for h in range(HALVES)]
        y_added, y_scaled, y_turned, waits_passed = sem("y_added"), sem("y_scaled"), sem("y_turned"), sem("waits_passed")
        out_kept, out_stored = sem("out_kept"), sem("out_stored")

        def experts_loop(eng, tile, begin=lambda g: None):
            begin(0)
            for t in range(SLOTS8):
                tile(t, t)
            with eng.Fori(1, GROUPS - 1) as g:
                begin(g)
                for k in range(SLOTS8):
                    tile(g * SLOTS8 + k, k)
            begin(GROUPS - 1)
            for k in range(SLOTS8):
                tile((GROUPS - 1) * SLOTS8 + k, k)

        def wait_apart(eng, s, value):
            eng.wait_ge(s, value)
            eng.sem_inc(waits_passed, 1)

        def at_least(eng, s, value):
            if not isinstance(value, int) or value > 0:
                eng.wait_ge(s, value)

        def gathered_value(t, k):
            return (t - k) * (16 // SLOTS8) + 16

        scattered_value = gathered_value

        ident = cst_s[:, C_IDENT:C_IDENT + P]

        block = ctx.enter_context(nc.Block())

        @block.sync
        def _(sp):
            sp.dma_start(xc[:], x[0]).then_inc(x_loaded, 16)
            sp.dma_start(wqk_s[:], wqk).then_inc(loaded["wqk"], 16)
            sp.dma_start(vec_s[:, 0:1], bqk).then_inc(loaded["wqk"], 16)
            sp.dma_start(vec_s[:, 1:2], gammaB).then_inc(loaded["wqk"], 16)
            sp.dma_start(cst_s[:], cst).then_inc(loaded["cst"], 16)
            sp.dma_start(tri_s[:], tri).then_inc(loaded["cst"], 16)
            sp.dma_start(wvT_s[:], wvT).then_inc(loaded["wv"], 16)
            sp.dma_start(bvB_s[:], bvB).then_inc(loaded["wv"], 16)
            for dst, src in ((wq_s, wq), (bq_s, bq), (lunch_s, lunch), (wvD_s, wvD), (bvD_s, bvD), (wp_raw, wp), (bpB_s, bpB)):
                sp.dma_start(dst if dst is wp_raw else dst[:], src).then_inc(loaded["attn"], 16)
            sp.dma_start(routerT_s[:], routerT).then_inc(loaded["router"], 16)
            sp.dma_start(tok[:], tokid).then_inc(loaded["tok"], 16)
            sp.dma_start(ids_dram.rearrange("(a b) c -> a (b c)", b=pad_ids.shape[1]), pad_ids).then_inc(ids_cleared, 16)

            def store_ln2(i):
                sp.wait_ge(norm_step, i * NORM_STEPS + NORM_STEPS)
                sp.dma_start(ln2_dram[bass.ds(i * N, N), :].rearrange("(n p) c -> p n c", p=P), ln2[:]).then_inc(ln2_stored, 16)

            def load_x(i):
                sp.wait_ge(A[1].filled, A[1].full(i - 1, "v"))
                sp.dma_start(xc[:], x[bass.ds(i, 1)].rearrange("i c n -> c (i n)")).then_inc(x_loaded, 16)

            load_x(1)
            with sp.Fori(0, IMAGES - 2) as i:
                store_ln2(i)
                load_x(i + 2)
            store_ln2(IMAGES - 2)
            for c in Cb:
                sp.wait_ge(c.filled, c.full(IMAGES - 1, "pv", K - 1))
            sp.dma_start(w13_raw, w13.rearrange("p e h -> p (e h)")).then_inc(w13_loaded, 16)
            for c in Cb:
                sp.wait_ge(c.filled, c.full(IMAGES - 1, "attn"))
            for k in range(3):
                sp.dma_start(w2_s[k], w2T[:, k]).then_inc(loaded["w2"], 16)
            store_ln2(IMAGES - 1)
            sp.wait_ge(ln2_stored, 16 * IMAGES + 16)
            for k in range(SLOTS8):
                sp.wait_ge(scattered[k], 16 * GROUPS)
            for h in range(HALVES):
                for k in range(2):
                    rows = y_dram[k * TOKENS + h * HALF:k * TOKENS + (h + 1) * HALF, :]
                    sp.dma_start(y_in[:, h, k], rows.rearrange("(n p) c -> p n c", p=P)).then_inc(y_loaded[h], 16)
            for h in range(HALVES):
                sp.wait_ge(out_kept, h + 1)
                sp.dma_start(out[h // 2, :, h % 2 * HALF:(h % 2 + 1) * HALF], y_out[h]).then_inc(out_stored, 16)
            sp.wait_ge(out_stored, 16 * HALVES)

        @block.tensor
        def _(pe):
            def mm(bank, lhsT, rhs, start=True, stop=True):
                return nc.tensor.matmul(bank, lhsT, rhs, start=start, stop=stop)

            def project_qk(i):
                pe.wait_ge(x_loaded, i * 16 + 16)
                for h in range(2):
                    pe.wait_ge(A[h].drained, A[h].before(i, "qk"))
                    mm(bank_a[h][:, :], wqk_s[:], xc[:, h * HALF:(h + 1) * HALF]).then_inc(A[h].filled, 1)

            def project_xt(i):
                for h in range(2):
                    pe.wait_ge(A[h].drained, A[h].before(i, "xt"))
                    for j in range(4):
                        n = 4 * h + j
                        last = nc.tensor.transpose(bank_a[h][:, j * C:(j + 1) * C], xc[:, n * P:(n + 1) * P], ident)
                    last.then_inc(A[h].filled, 1)

            def project_v(i):
                for h in range(2):
                    pe.wait_ge(A[h].drained, A[h].before(i, "v"))
                    for j in range(4):
                        n = 4 * h + j
                        last = mm(bank_a[h][:, j * C:(j + 1) * C], xc[:, n * P:(n + 1) * P], wvT_s[:])
                    last.then_inc(A[h].filled, 1)

            def scores_by_query(i, n):
                if n == 0:
                    pe.wait_ge(stack_step, i * STACK_STEPS + (STACK_STEPS + 1))
                for h in range(2):
                    pe.wait_ge(A[h].drained, A[h].before(i, "scores", n))
                    mm(bank_a[h][:, :], q_stack[0:STACK, n * P:(n + 1) * P],
                       k_stack[0:STACK, h * HALF:(h + 1) * HALF]).then_inc(A[h].filled, 1)

            def max_rows(i):
                pe.wait_ge(max_step, i * MAX_STEPS + MAX_STEPS)
                for h in range(2):
                    pe.wait_ge(A[h].drained, A[h].before(i, "rows"))
                    for j in range(4):
                        last = nc.tensor.transpose(bank_a[h][0:STACK + 2, j * P:(j + 1) * P], max_cols[:, 4 * h + j, :], ident)
                    last.then_inc(A[h].filled, 1)

            def scores_by_key(i, m):
                if m == 0:
                    for h in range(2):
                        pe.wait_ge(A[h].drained, A[h].after(i, "rows"))
                s = S[m % 2]
                pe.wait_ge(s.drained, s.before(i, "scores", m // 2))
                for h in range(2):
                    last = mm(bank_s[m % 2][:, h * HALF:(h + 1) * HALF], k_stack[:, m * P:(m + 1) * P],
                              q_stack[:, h * HALF:(h + 1) * HALF])
                last.then_inc(s.filled, 1)

            def weigh_values(i, n):
                if n == 0:
                    for s in S:
                        pe.wait_ge(s.drained, s.after(i, "scores", TILES // 2 - 1))
                c = Cb[n % 2]
                pe.wait_ge(c.drained, c.before(i, "pv", n // 2))
                for m in range(TILES):
                    last = mm(bank_c[n % 2][:, 0:VCOLS], probs[:, m, n * P:(n + 1) * P], v_ext[:, m, :],
                              start=(m == 0), stop=(m == TILES - 1))
                last.then_inc(c.filled, 1)

            def turn_half(bank, src, h):
                for j in range(4):
                    last = nc.tensor.transpose(bank[:, j * C:(j + 1) * C], src[:, 4 * h + j, :], ident)
                return last

            def turn_ln1(i, h):
                pe.wait_ge(norm_step, i * NORM_STEPS + LN1_STEP // 2 * (h + 1))
                pe.wait_ge(Cb[h].drained, Cb[h].before(i, "ln1"))
                turn_half(bank_c[h], ln1, h).then_inc(Cb[h].filled, 1)

            def head_sums(i):
                for h in range(2):
                    pe.wait_ge(Cb[h].drained, Cb[h].after(i, "ln1"))
                for hd in range(HEADS):
                    last = mm(bank_c[0][:, 2 * hd:2 * hd + 2], wq_s[:, hd * P:(hd + 1) * P], ln1_sum[:, :])
                last.then_inc(Cb[0].filled, 1)

            def head_weight(i, hd):
                pe.wait_ge(norm_step, i * NORM_STEPS + G_STEP[hd // 4])
                s = S[hd % 2]
                pe.wait_ge(s.drained, s.before(i, "weff", hd // 2))
                for h in range(2):
                    for n, (g, w) in enumerate(((g_wv_hi, wp_hi), (g_wv_hi, wp_lo), (g_wv_lo, wp_hi))):
                        last = mm(bank_s[hd % 2][:, h * HALF:(h + 1) * HALF], g[:, hd, :],
                                  w[:, 4 * h:4 * h + 4, :].rearrange("p k c -> p (k c)"), start=(n == 0), stop=(n == 2))
                last.then_inc(s.filled, 1)

            def biases(i):
                for h in range(2):
                    pe.wait_ge(Cb[h].drained, Cb[h].before(i, "attn"))
                    for hd in range(4):
                        mm(bank_c[h][:, hd * C:(hd + 1) * C], g_bv[:, 4 * h + hd:4 * h + hd + 1].broadcast_to([P, P]),
                           wp_sum[:], start=(hd == 0), stop=False)

            def linear_attention(i, h, k):
                if k == 0:
                    pe.wait_ge(lnT_split, 2 * i + 2)
                    for s in S:
                        pe.wait_ge(s.drained, s.after(i, "weff", 2 * h + 1))
                for n, (t, w) in enumerate(((lnT_hi, weff_hi), (lnT_hi, weff_lo), (lnT_lo, weff_hi))):
                    last = mm(bank_c[h][:, :], t[:, k:N:HEADS], w[:, k, 4 * h:4 * h + 4, :].rearrange("p h c -> p (h c)"),
                              start=False, stop=(k == HEADS - 1 and n == 2))
                if k == HEADS - 1:
                    last.then_inc(Cb[h].filled, 1)

            def turn_ln2(i, h):
                pe.wait_ge(norm_step, i * NORM_STEPS + LN2_STEP[h])
                pe.wait_ge(A[h].drained, A[h].before(*routed(A[h], i, "ln2")))
                turn_half(bank_a[h], ln2, h).then_inc(A[h].filled, 1)

            def route(i, h):
                if h == 0:
                    pe.wait_ge(A[0].drained, A[0].before(*routed(A[0], i, "route")))
                pe.wait_ge(A[h].drained, A[h].after(*routed(A[h], i, "ln2")))
                for n in range(4 * h, 4 * h + 4):
                    last = mm(bank_a[0][:, n * EXPERTS:(n + 1) * EXPERTS], lnT[:, n * P:(n + 1) * P], routerT_s[:])
                if h == 1:
                    last.then_inc(A[0].filled, 1)

            def rank(i):
                pe.wait_ge(gate_step, i * GATE_STEPS + BOTH_STEP)
                pe.wait_ge(S[0].drained, S[0].before(*routed(S[0], i, "rank")))
                W = TILES * EXPERTS
                flat = both[:].rearrange("p n e -> p (n e)")
                mm(bank_s[0][:, 0:W], tri_s[:, 0:P], flat, stop=False)
                for n in range(1, TILES):
                    mm(bank_s[0][:, n * EXPERTS:W], tri_s[:, P:2 * P], flat[:, 0:W - n * EXPERTS], start=False, stop=False)
                for n in range(TILES):
                    last = mm(bank_s[0][:, W:W + EXPERTS], tri_s[:, P:2 * P], both[:, n, :], start=False, stop=(n == TILES - 1))
                last.then_inc(S[0].filled, 1)

            def pass_routing():
                for bank, uses in ((A[0], 2), (A[1], 1), (S[0], 1)):
                    pe.wait_ge(bank.drained, bank.before(0, "rank" if bank is S[0] else "ln2"))
                    pe.sem_inc(bank.filled, uses)
                    pe.sem_inc(bank.drained, uses)

            def image(i, first=False, last=False):
                for n in range(TILES):
                    weigh_values(i, n)
                    if first and n == 0:
                        pass_routing()
                    if not first and n == 3:
                        for h in range(2):
                            turn_ln2(i - 1, h)
                    if not first and n == 4:
                        for h in range(2):
                            route(i - 1, h)
                if not last:
                    project_qk(i + 1)
                    project_xt(i + 1)
                if first:
                    pe.wait_ge(loaded["attn"], 16 * 7)
                    pe.wait_ge(heads_made, 5)
                turn_ln1(i, 0)
                if not first:
                    rank(i - 1)
                turn_ln1(i, 1)
                head_sums(i)
                if not last:
                    project_v(i + 1)
                for hd in range(HEADS):
                    head_weight(i, hd)
                    if not last:
                        for n in MAX_BESIDE[hd]:
                            scores_by_query(i + 1, n)
                    if hd == 3:
                        biases(i)
                    if hd >= 4:
                        for k in (2 * (hd - 4), 2 * (hd - 4) + 1):
                            linear_attention(i, 0, k)
                if not last:
                    max_rows(i + 1)
                for k in range(HEADS):
                    linear_attention(i, 1, k)
                    if not last:
                        scores_by_key(i + 1, k)

            pe.wait_ge(loaded["wqk"], 48)
            project_qk(0)
            pe.wait_ge(loaded["cst"], 32)
            project_xt(0)
            pe.wait_ge(loaded["wv"], 32)
            project_v(0)
            pe.wait_ge(consts_made, 4)
            for n in range(TILES):
                scores_by_query(0, n)
            max_rows(0)
            for m in range(TILES):
                scores_by_key(0, m)
            pe.wait_ge(loaded["router"], 16)
            image(0, first=True)
            with pe.Fori(1, IMAGES - 1) as i:
                image(i)
            image(IMAGES - 1, last=True)
            for h in range(2):
                turn_ln2(IMAGES - 1, h)
                route(IMAGES - 1, h)
            rank(IMAGES - 1)

            def turn_x(t, k):
                at_least(pe, x_lo_ready, t - 1)
                pe.wait_ge(gathered[k], gathered_value(t, k))
                nc.tensor.transpose(bank_a[k % 2][:, 0:P], x_rows[k], ident).then_inc(x_turned, 1)

            def hidden13(t, k, e):
                pe.wait_ge(x_lo_ready, t + 1)
                at_least(pe, hidden_ready, t - 1)
                hi, lo = x_hi[k % 2], x_lo[k % 2]
                for h, cols in enumerate((slice(0, W_A), slice(W_A, HID2))):
                    dst = bank_s[k % 2][:, H13 + cols.start:H13 + cols.stop]
                    for n, (x_part, w_part) in enumerate(((hi, w13_hi), (hi, w13_lo), (lo, w13_hi))):
                        last = mm(dst, x_part[:], w_part.rearrange("p (e h) -> p e h", h=HID2)[:, bass.ds(e, 1), cols].rearrange("p a h -> p (a h)"), start=(n == 0), stop=(n == 2))
                last.then_inc(h13_ready, 1)

            def turn_hidden(t, k):
                pe.wait_ge(hidden_ready, t + 1)
                at_least(pe, hiddenT_ready, t)
                for c in range(3):
                    last = nc.tensor.transpose(bank_c[0][0:CHUNK, c * P:(c + 1) * P], hidden[k % 2][:, c * CHUNK:(c + 1) * CHUNK], ident)
                last.then_inc(hidden_turned, 1)

            def result(t, k, e):
                pe.wait_ge(hiddenT_ready, t + 1)
                at_least(pe, y_kept, t)
                for c in range(3):
                    rows = min(CHUNK, HID - c * CHUNK)
                    last = mm(bank_c[1][:, 0:C], hiddenT[k % 2][0:rows, c, :],
                              w2_s[c][0:rows, bass.ds(e, 1), :].rearrange("p a c -> p (a c)"), start=(c == 0), stop=(c == 2))
                last.then_inc(y_ready, 1)

            def tile(t, k):
                hidden13(t, k, experts[k + 2])
                if not isinstance(t, int) or t + 2 < FFN_TILES:
                    turn_x(t + 2, (k + 2) % SLOTS8)
                if not isinstance(t, int) or t >= 1:
                    turn_hidden(t - 1, (k - 1) % SLOTS8)
                if not isinstance(t, int) or t >= 2:
                    result(t - 2, (k - 2) % SLOTS8, experts[k])

            experts = []

            def load_experts(g):
                bits = (EXPERTS - 1).bit_length()
                word = pe.value_load(table[0:1, bass.ds(g, 1)], min_val=0, max_val=EXPERTS ** (SLOTS8 + 2) - 1)
                experts[:] = [(word >> (bits * j)) & (EXPERTS - 1) for j in range(SLOTS8 + 2)]

            pe.wait_ge(placed, 1)
            for c in range(2 * TILES):
                last = mm(bank_c[0][:, 0:3 * FFN_TILES], of_place[:, c, :], of_tile[:, c].rearrange("p k t -> p (k t)"),
                          start=(c == 0), stop=(c == 2 * TILES - 1))
            last.then_inc(ids_turned, 1)
            pe.wait_ge(ids_exact, 1)
            nc.tensor.transpose(bank_c[1][:, 0:FFN_TILES], ids_rows_f[:], cst_s[0:FFN_TILES, C_IDENT:C_IDENT + FFN_TILES]).then_inc(ids_turned, 1)
            pe.wait_ge(table_ready, 1)
            pe.wait_ge(w13_parts, 2)
            pe.wait_ge(loaded["w2"], 48)
            turn_x(0, 0)
            turn_x(1, 1)
            experts_loop(pe, tile, load_experts)
            turn_hidden(FFN_TILES - 1, SLOTS8 - 1)
            for t in (FFN_TILES - 2, FFN_TILES - 1):
                result(t, t % SLOTS8, experts[t - FFN_TILES])

            for h in range(HALVES):
                pe.wait_ge(y_added, h + 1)
                pe.wait_ge(y_scaled, h + 1)
                if h >= 2:
                    pe.wait_ge(out_kept, h - 1)
                for j in range(4):
                    for k in range(2):
                        last = mm(bank_a[h % 2][:, j * P:(j + 1) * P], y_in[:, h, k, j, :], ident, start=(k == 0), stop=(k == 1))
                last.then_inc(y_turned, 1)

        @block.scalar
        def _(act):
            def stack_sums(i):
                for h in range(2):
                    act.wait_ge(A[h].filled, A[h].full(i, "qk"))
                    act.wait_ge(stack_step, i * STACK_STEPS + 1)
                    nc.scalar.activation(qk_sum[:, h * HALF:(h + 1) * HALF], bank_a[h][:, :], ACT.Identity,
                                         bias=vec_s[:, 0:1]).then_inc(A[h].drained, 1)

            def keep_xt(i):
                for h in range(2):
                    if not isinstance(i, int) or i > 0:
                        act.wait_ge(Cb[h].drained, Cb[h].after(i - 1, "pv", K - 1))
                    act.wait_ge(A[h].filled, A[h].full(i, "xt"))
                    nc.scalar.copy(xt[:, 4 * h:4 * h + 4, :], bank_a[h][:, :].rearrange("p (n c) -> p n c", c=C)).then_inc(A[h].drained, 1)

            def max_rows(i):
                for h in range(2):
                    act.wait_ge(A[h].filled, A[h].full(i, "rows"))
                    nc.scalar.copy(q_stack[STACK:STACK + 2, h * HALF:(h + 1) * HALF],
                                   bank_a[h][STACK:STACK + 2, :]).then_inc(A[h].drained, 1)

            def exps(i, m):
                s = S[m % 2]
                act.wait_ge(s.filled, s.full(i, "scores", m // 2))
                nc.scalar.activation(probs[:, m, :], bank_s[m % 2][:, :], ACT.Exp, scale=DQK ** -0.5).then_inc(s.drained, 1)

            def split_w13():
                act.wait_ge(w13_loaded, 16)
                for c in Cb:
                    act.wait_ge(c.filled, c.full(IMAGES - 1, "attn"))
                nc.scalar.copy(w13_hi, w13_raw).then_inc(w13_parts, 1)

            def keep_ln1T(i):
                for h in range(2):
                    act.wait_ge(Cb[h].filled, Cb[h].full(i, "ln1"))
                    nc.scalar.activation(lnT[:, h * HALF:(h + 1) * HALF], bank_c[h][:, :], ACT.Identity,
                                         accum_out=ln1_sum[:, h:h + 1]).then_inc(Cb[h].drained, 1)

            def keep_weff(i):
                for hd in range(HEADS):
                    s = S[hd % 2]
                    act.wait_ge(s.filled, s.full(i, "weff", hd // 2))
                    nc.scalar.copy(weff_hi[:, :, hd, :], bank_s[hd % 2][:, :].rearrange("p (k c) -> p k c", c=C)).then_inc(weff_high, 1)

            def keep_ln2T(i, h):
                act.wait_ge(A[h].filled, A[h].full(*routed(A[h], i, "ln2")))
                nc.scalar.copy(lnT[:, h * HALF:(h + 1) * HALF], bank_a[h][:, :]).then_inc(A[h].drained, 1)

            def gate_exps(i):
                act.wait_ge(gate_step, i * GATE_STEPS + SECOND_STEP)
                nc.scalar.activation(prob[:].rearrange("p n e -> p (n e)"), logit[:].rearrange("p n e -> p (n e)"), ACT.Exp)
                nc.scalar.activation(second[:], lesser[:], ACT.Exp).then_inc(exp_ready, 1)

            def image(i, first=False, last=False):
                if not first:
                    for h in range(2):
                        keep_ln2T(i - 1, h)
                    gate_exps(i - 1)
                if not last:
                    stack_sums(i + 1)
                    keep_xt(i + 1)
                keep_ln1T(i)
                keep_weff(i)
                if not last:
                    max_rows(i + 1)
                    for m in range(TILES):
                        exps(i + 1, m)

            stack_sums(0)
            keep_xt(0)
            max_rows(0)
            for m in range(TILES):
                exps(0, m)
            image(0, first=True)
            with act.Fori(1, IMAGES - 1) as i:
                image(i)
            image(IMAGES - 1, last=True)
            keep_ln2T(IMAGES - 1, 0)
            split_w13()
            keep_ln2T(IMAGES - 1, 1)
            gate_exps(IMAGES - 1)

            def silu(t, k):
                act.wait_ge(h13_ready, t + 1)
                at_least(act, hidden_ready, t - 1)
                nc.scalar.activation(silu1[k % 2], bank_s[k % 2][:, H13:H13 + HID], ACT.Silu).then_inc(silu_ready, 1)

            def high_part(t, k):
                act.wait_ge(x_turned, t + 1)
                at_least(act, h13_ready, t - 1)
                nc.scalar.copy(x_hi[k % 2][:], bank_a[k % 2][:, 0:P]).then_inc(x_hi_ready, 1)

            def keep_y(t, k):
                act.wait_ge(y_ready, t + 1)
                if not isinstance(t, int) or t >= SLOTS8:
                    act.wait_ge(scattered[k], scattered_value(t, k) - 16)
                nc.scalar.copy(y_rows[k], bank_c[1][:, 0:C]).then_inc(y_kept, 1)

            def tile(t, k):
                silu(t, k)
                if not isinstance(t, int) or t + 2 < FFN_TILES:
                    high_part(t + 2, (k + 2) % SLOTS8)
                if not isinstance(t, int) or t >= 2:
                    keep_y(t - 2, (k - 2) % SLOTS8)

            high_part(0, 0)
            high_part(1, 1)
            experts_loop(act, tile)
            for t in (FFN_TILES - 2, FFN_TILES - 1):
                keep_y(t, t % SLOTS8)

            for h in range(HALVES):
                act.wait_ge(y_loaded[h], 32)
                for j in range(4):
                    last = nc.scalar.activation(y_in[:, h, 1, j, :], y_in[:, h, 1, j, :], ACT.Copy, scale=gates[:, 1, 4 * h + j:4 * h + j + 1])
                last.then_inc(y_scaled, 1)

        @block.vector
        def _(dve):
            V = nc.vector

            def step(ins, s, start, n):
                ins.then_inc(s, 1)
                dve.wait_ge(s, start + n)

            def bcast_e(ap):
                return ap.unsqueeze(2).broadcast_to([P, TILES, EXPERTS])

            def make_stacks(i):
                s0 = i * STACK_STEPS + 1
                for h in range(2):
                    dve.wait_ge(A[h].drained, A[h].after(i, "qk"))
                step(V.tensor_copy(qk_hi[:], qk_sum[:]), stack_step, s0, 1)
                for k, (dst, lo) in enumerate(((q_stack, 0), (k_stack, STACK))):
                    rows = slice(lo, lo + STACK)
                    V.scalar_tensor_tensor(out=dst[0:STACK, :], in0=qk_hi[rows, :].bitcast(F32), scalar=cst_s[rows, C_LOW:C_LOW + 1],
                                           in1=qk_sum[rows, :], op0=ALU.mult, op1=ALU.add).then_inc(stack_step, 1)

            def keep_v(i):
                for h in range(2):
                    dve.wait_ge(A[h].filled, A[h].full(i, "v"))
                    V.scalar_tensor_tensor(out=v_ext[:, 4 * h:4 * h + 4, 0:C], in0=bank_a[h][:, :].rearrange("p (n c) -> p n c", c=C),
                                           scalar=vec_s[:, 1:2], in1=gbv[:].unsqueeze(1).broadcast_to([P, 4, C]),
                                           op0=ALU.mult, op1=ALU.add).then_inc(A[h].drained, 1)

            def row_max(i, n):
                for h in range(2):
                    dve.wait_ge(A[h].filled, A[h].full(i, "scores", n))
                    V.reduce_max(row_max2[:, n, h:h + 1], bank_a[h][:, :], AX_X).then_inc(A[h].drained, 1)

            def negate_max(i):
                s0 = i * MAX_STEPS
                for h in range(2):
                    dve.wait_ge(A[h].drained, A[h].after(i, "scores", TILES - 1))
                step(V.tensor_reduce(neg_max[:], row_max2[:], AX_X, ALU.max, negate=True), max_step, s0, 1)
                step(V.tensor_copy(neg_max_hi[:], neg_max[:]), max_step, s0, 2)
                V.tensor_copy(max_cols[:, :, STACK], neg_max_hi[:].bitcast(F32)).then_inc(max_step, 1)
                V.tensor_tensor(max_cols[:, :, STACK + 1], neg_max[:], neg_max_hi[:].bitcast(F32), ALU.subtract).then_inc(max_step, 1)

            def attended(i, n):
                c = Cb[n % 2]
                dve.wait_ge(c.filled, c.full(i, "pv", n // 2))
                s0 = (i * TILES) + n
                V.reciprocal(rden[:, n:n + 1], bank_c[n % 2][:, C:VCOLS]).then_inc(den_ready, 1)
                dve.wait_ge(den_ready, s0 + 1)
                V.scalar_tensor_tensor(out=t1[:, n, :], in0=bank_c[n % 2][:, 0:C], scalar=rden[:, n:n + 1],
                                       in1=xt[:, n, :], op0=ALU.mult, op1=ALU.add).then_inc(c.drained, 1)

            def norm_vars(i, tiles, first, eps):
                wait_apart(dve, norm_step, i * NORM_STEPS + (first + 1))
                for n in range(tiles.start, tiles.stop):
                    last = V.bn_aggr(mean_var[:, n, :], stats[:, n, :])
                step(last, norm_step, i * NORM_STEPS, first + 2)
                V.tensor_scalar(var_eps[:, tiles], mean_var[:, tiles, 1], eps, None, ALU.add).then_inc(norm_step, 1)

            def normalise(i, src, dst, tiles, which):
                dve.wait_ge(rstd_ready, i * 4 + (which + 1))
                for n in range(tiles.start, tiles.stop):
                    last = V.tensor_scalar(dst[:, n, :], src(n), mean_var[:, n, 0:1], rstd[:, n:n + 1], ALU.subtract, ALU.mult)
                last.then_inc(norm_step, 1)

            def t1_stats(i, n):
                c = Cb[n % 2]
                dve.wait_ge(c.drained, c.after(i, "pv", n // 2))
                last = V.bn_stats(stats[:, n, :], t1[:, n, :])
                if n % 4 == 3:
                    last.then_inc(norm_step, 1)

            def head_weights(i):
                s0 = i * NORM_STEPS
                dve.wait_ge(Cb[0].filled, Cb[0].full(i, "qsum"))
                V.tensor_reduce(qsum[:], bank_c[0][:, 0:2 * HEADS].rearrange("p (h t) -> p h t", t=2), AX_X, ALU.add).then_inc(Cb[0].drained, 1)
                dve.wait_ge(Cb[0].drained, Cb[0].after(i, "qsum"))
                step(V.tensor_tensor(qsum[:], qsum[:], nbq[:], ALU.add), norm_step, s0, 9)
                step(V.tensor_scalar(g_head[:], qsum[:], lunch_sum[:, 0:1], None, ALU.mult), norm_step, s0, 10)
                V.tensor_tensor(g_bv[:], g_head[:], bvD_s[:], ALU.mult)
                for half in range(2):
                    hs = slice(4 * half, 4 * half + 4)
                    step(V.tensor_tensor(g_wv[:, hs], wvD_s[:, hs], g_head[:, hs].unsqueeze(2).broadcast_to([P, 4, C]), ALU.mult),
                         norm_step, s0, 11 + 3 * half)
                    step(V.tensor_copy(g_wv_hi[:, hs], g_wv[:, hs]), norm_step, s0, 12 + 3 * half)
                    V.tensor_tensor(g_wv_lo[:, hs], g_wv[:, hs], g_wv_hi[:, hs].bitcast(F32), ALU.subtract).then_inc(norm_step, 1)

            def low_weff(i, hd):
                s = S[hd % 2]
                dve.wait_ge(weff_high, i * HEADS + (hd + 1))
                V.tensor_tensor(weff_lo[:, :, hd, :], bank_s[hd % 2][:, :].rearrange("p (k c) -> p k c", c=C),
                                weff_hi[:, :, hd, :].bitcast(F32), ALU.subtract).then_inc(s.drained, 1)

            def linear_attended(i):
                dve.wait_ge(bias_added, i + 1)
                for h in range(2):
                    dve.wait_ge(Cb[h].filled, Cb[h].full(i, "attn"))
                    V.tensor_tensor(t2[:, bass.ds(i * TILES + 4 * h, 4), :], bank_c[h][:, :].rearrange("p (n c) -> p n c", c=C),
                                    t1[:, 4 * h:4 * h + 4, :], ALU.add).then_inc(Cb[h].drained, 1)
                    wait_apart(dve, Cb[h].drained, Cb[h].after(i, "attn"))
                    for n in range(4 * h, 4 * h + 4):
                        last = V.bn_stats(stats[:, n, :], t2[:, bass.ds(i * TILES + n, 1), :])
                    last.then_inc(norm_step, 1)
                    norm_vars(i, slice(4 * h, 4 * h + 4), 16 + 4 * h, 1e-5)
                    if h == 0:
                        norm2(i, 0)

            def norm2(i, h):
                if h == 0:
                    wait_apart(dve, ln2_stored, 16 * i + 16)
                normalise(i, lambda n: t2[:, bass.ds(i * TILES + n, 1), :], ln2, slice(4 * h, 4 * h + 4), 2 + h)

            mx, z, wmax, den = (small[:, k, :] for k in range(4))
            rev = cst_s[:, C_RANK:C_RANK + EXPERTS].unsqueeze(1).broadcast_to([P, TILES, EXPERTS])
            flat = "p n e -> p (n e)"

            def gate_chain(i, from_step):
                done = [from_step]

                def at(ins):
                    done[0] += 1
                    step(ins, gate_step, i * GATE_STEPS, done[0])

                return at

            def shift_logits(i):
                at = gate_chain(i, 0)
                psl = bank_a[0][:, 0:TILES * EXPERTS].rearrange("p (n e) -> p n e", e=EXPERTS)
                dve.wait_ge(A[0].filled, A[0].full(*routed(A[0], i, "route")))
                at(V.tensor_reduce(mx, psl, AX_X, ALU.max))
                V.tensor_tensor(logit[:], psl, bcast_e(mx), ALU.subtract).then_inc(A[0].drained, 1)
                dve.wait_ge(A[0].drained, A[0].after(*routed(A[0], i, "route")))

            def pick_equal_to_max(at, src, k):
                at(V.scalar_tensor_tensor(out=tie[:], in0=src, scalar=0.0, in1=rev, op0=ALU.is_equal, op1=ALU.mult))
                at(V.tensor_reduce(wmax, tie[:], AX_X, ALU.max))
                at(V.tensor_tensor(pick[:, k], tie[:], bcast_e(wmax), ALU.is_equal))

            def pick_first(i):
                at = gate_chain(i, 1)
                pick_equal_to_max(at, logit[:], 0)
                at(V.scalar_tensor_tensor(out=others[:].rearrange(flat), in0=pick[:, 0].rearrange(flat), scalar=-3.0e38,
                                          in1=logit[:].rearrange(flat), op0=ALU.mult, op1=ALU.add))

            def pick_second(i):
                at = gate_chain(i, 5)
                at(V.tensor_reduce(lesser[:], others[:], AX_X, ALU.max))
                at(V.tensor_tensor(others[:], others[:], bcast_e(lesser[:]), ALU.subtract))
                pick_equal_to_max(at, others[:], 1)
                at(V.tensor_tensor(both[:], pick[:, 0], pick[:, 1], ALU.add))

            def set_gates(i):
                at = gate_chain(i, SLOT_STEP)
                g = [gates[:, k, bass.ds(i * TILES, TILES)] for k in range(2)]
                at(V.tensor_reduce(z, prob[:], AX_X, ALU.add))
                at(V.reciprocal(z, z))
                at(V.tensor_tensor(second[:], second[:], z, ALU.mult))
                at(V.tensor_tensor(den, z, second[:], ALU.add))
                at(V.tensor_scalar(den, den, 1e-9, None, ALU.add))
                at(V.reciprocal(den, den))
                at(V.tensor_tensor(g[0], z, den, ALU.mult))
                at(V.tensor_tensor(g[1], second[:], den, ALU.mult))

            def set_slots(i):
                at = gate_chain(i, BOTH_STEP)
                W = TILES * EXPERTS
                dve.wait_ge(exp_ready, i + 1)
                dve.wait_ge(S[0].filled, S[0].full(*routed(S[0], i, "rank")))
                at(V.tensor_tensor(logit[:], bank_s[0][:, 0:W].rearrange("p (n e) -> p n e", e=EXPERTS),
                                   base[:].unsqueeze(1).broadcast_to([P, TILES, EXPERTS]), ALU.add))
                V.tensor_tensor(base[:], bank_s[0][:, W:W + EXPERTS], base[:], ALU.add).then_inc(S[0].drained, 1)
                at(V.tensor_tensor(pick[:], pick[:], logit[:].unsqueeze(1).broadcast_to([P, 2, TILES, EXPERTS]), ALU.mult))
                slot_f = small[:, 6:8, :].rearrange("p k n -> p (k n)")
                at(V.tensor_reduce(slot_f, pick[:].rearrange("p k n e -> p (k n) e"), AX_X, ALU.add))
                dve.wait_ge(tok_step, i + 1)
                at(V.tensor_copy(slots[:], slot_f))

            def image(i, first=False, last=False):
                half_a, half_b, t1_tile = slice(0, 4), slice(4, 8), lambda n: t1[:, n, :]
                for n in range(TILES):
                    attended(i, n)
                    if n >= 1:
                        t1_stats(i, n - 1)
                    if n == 1 and not first:
                        norm2(i - 1, 1)
                    if n == 4:
                        norm_vars(i, half_a, 0, 1e-5)
                    if n == 5:
                        if not first:
                            shift_logits(i - 1)
                        normalise(i, t1_tile, ln1, half_a, 0)
                    if n == 6 and not first:
                        pick_first(i - 1)
                t1_stats(i, TILES - 1)
                norm_vars(i, half_b, 4, 1e-5)
                if not first:
                    pick_second(i - 1)
                normalise(i, t1_tile, ln1, half_b, 1)
                if not last:
                    make_stacks(i + 1)
                if not first:
                    set_slots(i - 1)
                head_weights(i)
                if not last:
                    keep_v(i + 1)
                for hd in range(HEADS):
                    if not last:
                        for n in MAX_BESIDE[hd]:
                            row_max(i + 1, n)
                        if MAX_BESIDE[hd] and MAX_BESIDE[hd][-1] == TILES - 1:
                            negate_max(i + 1)
                    low_weff(i, hd)
                if not first:
                    set_gates(i - 1)
                linear_attended(i)

            V.memset(max_cols[:], 0.0).then_inc(consts_made, 1)
            V.memset(v_ext[:, :, C:VCOLS], 1.0).then_inc(consts_made, 1)
            V.memset(k_stack[STACK:STACK + 2, :].bitcast(F32), 1.0).then_inc(consts_made, 1)
            for bank in (*A, *S, *Cb):
                dve.sem_inc(bank.drained, 1)
            for s, by in ((stack_step, 1), (tok_step, 1), (ln2_stored, 16)):
                dve.sem_inc(s, by)
            dve.wait_ge(loaded["wqk"], 48)
            dve.wait_ge(loaded["cst"], 32)
            dve.wait_ge(loaded["wv"], 32)
            V.tensor_scalar(gbv[:], bvB_s[:], vec_s[:, 1:2], None, ALU.mult).then_inc(consts_made, 1)
            dve.wait_ge(consts_made, 4)
            make_stacks(0)
            keep_v(0)
            for n in range(TILES):
                row_max(0, n)
            negate_max(0)
            dve.wait_ge(loaded["attn"], 16 * 7)
            V.tensor_scalar(nbq[:], bq_s[:], float(N), None, ALU.mult).then_inc(heads_made, 1)
            V.tensor_reduce(lunch_sum[:], lunch_s[:], AX_X, ALU.add).then_inc(setup, 1)
            V.tensor_copy(base[:], cst_s[:, C_BASE:C_BASE + EXPERTS]).then_inc(setup, 1)
            dve.wait_ge(setup, 2)
            V.tensor_scalar(lunch_sum[:], lunch_sum[:], float(max(P, lunch.shape[1])) ** -0.5, None, ALU.mult).then_inc(heads_made, 1)
            V.tensor_reduce(wp_sum[:], wp_raw.rearrange("p k c -> p c k"), AX_X, ALU.add).then_inc(heads_made, 1)
            V.tensor_copy(wp_hi[:], wp_raw).then_inc(heads_made, 1)
            dve.wait_ge(heads_made, 4)
            V.tensor_tensor(wp_lo[:], wp_raw, wp_hi[:].bitcast(F32), ALU.subtract).then_inc(heads_made, 1)
            image(0, first=True)
            with dve.Fori(1, IMAGES - 1) as i:
                image(i)
            image(IMAGES - 1, last=True)
            norm2(IMAGES - 1, 1)
            shift_logits(IMAGES - 1)
            pick_first(IMAGES - 1)
            pick_second(IMAGES - 1)

            def ready_token(t, k):
                V.tensor_scalar(tok_slot[:, k:k + 1], ids[:, bass.ds(t, 1)], TOKENS - 1, None, ALU.bitwise_and).then_inc(slot_ready, 1)

            def ready_result(t, k):
                if not isinstance(t, int) or t >= SLOTS8:
                    dve.wait_ge(scattered[k], scattered_value(t, k) - 16)
                V.tensor_scalar(id_slot[:, k:k + 1], ids[:, bass.ds(t, 1)], 0, None, ALU.bitwise_or)

            marks = [0]

            def then(ins):
                marks[0] += 1
                step(ins, table_step, 0, marks[0])

            then(V.tensor_tensor(counts_before[:], base[:], cst_s[:, C_BASE:C_BASE + EXPERTS], ALU.subtract))
            W = TILES * EXPERTS
            dve.wait_ge(S[0].filled, S[0].full(*routed(S[0], IMAGES - 1, "rank")))
            then(V.tensor_tensor(counts[:], bank_s[0][:, W:W + EXPERTS], counts_before[:], ALU.add))
            then(V.tensor_scalar(counts_i[:], counts[:], float(P - 1), None, ALU.add))
            then(V.tensor_scalar(counts_i[:], counts_i[:], P.bit_length() - 1, None, ALU.arith_shift_right))
            then(V.tensor_copy(n_tiles[:], counts_i[:]))
            then(V.tensor_copy(ends[:], n_tiles[:]))
            for e in range(1, EXPERTS):
                then(V.tensor_tensor(ends[:, e:e + 1], ends[:, e - 1:e], ends[:, e:e + 1], ALU.add))
            at_row = cst_s[:, C_ROW:C_ROW + 1]
            expert, before, row = (tile_at[:, k:k + 1] for k in range(3))
            then(V.tensor_scalar(ended[:], ends[:], at_row, None, ALU.is_le))
            then(V.tensor_reduce(expert, ended[:], AX_X, ALU.add))
            then(V.tensor_tensor(ended[:], ended[:], n_tiles[:], ALU.mult))
            then(V.tensor_reduce(before, ended[:], AX_X, ALU.add))
            then(V.tensor_tensor(row, at_row, before, ALU.subtract))
            then(V.scalar_tensor_tensor(out=row, in0=expert, scalar=float(REGION // P), in1=row, op0=ALU.mult, op1=ALU.add))
            V.tensor_copy(tile_row[:], row).then_inc(rows_ready, 1)
            then(V.tensor_tensor(packed[:], ends[:], n_tiles[:], ALU.subtract))
            then(V.scalar_tensor_tensor(out=packed[:], in0=packed[:], scalar=float(P), in1=counts_before[:], op0=ALU.mult, op1=ALU.add))
            at = gate_chain(IMAGES - 1, BOTH_STEP)
            V.tensor_tensor(others[:], bank_s[0][:, 0:W].rearrange("p (n e) -> p n e", e=EXPERTS),
                            packed[:].unsqueeze(1).broadcast_to([P, TILES, EXPERTS]), ALU.add).then_inc(S[0].drained, 1)
            dve.wait_ge(S[0].drained, S[0].after(*routed(S[0], IMAGES - 1, "rank")))
            at(V.tensor_tensor(pick[:], pick[:], others[:].unsqueeze(1).broadcast_to([P, 2, TILES, EXPERTS]), ALU.mult))
            at(V.tensor_reduce(last_place[:, 0, :], pick[:].rearrange("p k n e -> p (k n) e"), AX_X, ALU.add))
            at(V.tensor_copy(last_int[:, 0, :], last_place[:, 0, :]))
            then(V.tensor_scalar(last_int[:, 1, :], last_int[:, 0, :], P.bit_length() - 1, None, ALU.arith_shift_right))
            at(V.tensor_scalar(last_int[:, 0, :], last_int[:, 0, :], P - 1, None, ALU.bitwise_and))
            then(V.tensor_copy(last_place[:], last_int[:]))
            V.tensor_tensor(of_place, cst_s[:, C_IOTA:C_IOTA + P].unsqueeze(1).broadcast_to([P, 2 * TILES, P]),
                            last_place[:, 0, :].unsqueeze(2).broadcast_to([P, 2 * TILES, P]), ALU.is_equal)
            then(V.tensor_tensor(of_tile[:, :, 0, :], cst_s[:, C_TILE:C_TILE + FFN_TILES].unsqueeze(1).broadcast_to([P, 2 * TILES, FFN_TILES]),
                                 last_place[:, 1, :].unsqueeze(2).broadcast_to([P, 2 * TILES, FFN_TILES]), ALU.is_equal))
            V.tensor_scalar(of_tile[:, :, 1, :], of_tile[:, :, 0, :], cst_s[:, C_ROW:C_ROW + 1], None, ALU.mult)
            V.tensor_tensor(of_tile[:, :, 2, :], of_tile[:, :, 0, :],
                            cst_s[:, C_HIGH:C_HIGH + 2 * TILES].unsqueeze(2).broadcast_to([P, 2 * TILES, FFN_TILES]), ALU.mult).then_inc(placed, 1)
            dve.wait_ge(exp_ready, IMAGES)
            set_gates(IMAGES - 1)
            dve.wait_ge(ids_loaded, 16)
            V.tensor_copy(ids_rows_f[:], ids_rows[:]).then_inc(ids_exact, 1)
            dve.wait_ge(ids_turned, 2)
            F = FFN_TILES
            then(V.tensor_scalar(ids_f[:], bank_c[0][:, 0:F], -1.0, 1.0, ALU.mult, ALU.add))
            then(V.tensor_tensor(ids_f[:], ids_f[:], bank_c[1][:, 0:F], ALU.mult))
            then(V.tensor_tensor(ids_f[:], ids_f[:], bank_c[0][:, F:2 * F], ALU.add))
            V.scalar_tensor_tensor(out=ids[:], in0=bank_c[0][:, 2 * F:3 * F], scalar=float(P), in1=ids_f[:], op0=ALU.mult, op1=ALU.add).then_inc(ids_ready, 1)
            dve.wait_ge(ids_ready, 1)
            for t in range(AHEAD + 1):
                ready_token(t, t)
            ready_result(0, 0)
            tiles = cst_s[0:1, C_TILE:C_TILE + FFN_TILES]
            wide = [1, FFN_TILES, EXPERTS]
            then(V.tensor_tensor(past[:], tiles.unsqueeze(2).broadcast_to(wide), ends[0:1, :].unsqueeze(1).broadcast_to(wide), ALU.is_ge))
            then(V.tensor_reduce(expert_f[:], past[:], AX_X, ALU.add))
            then(V.scalar_tensor_tensor(out=expert_f[:], in0=expert_f[:], scalar=float(EXPERTS - 1), in1=cst_s[0:1, C_DIGIT:C_DIGIT + FFN_TILES],
                                        op0=ALU.min, op1=ALU.mult))
            then(V.memset(words[:, 0:1], 0))
            then(V.tensor_reduce(word_f[:], expert_f[:].rearrange("p (g k) -> p g k", k=SLOTS8), AX_X, ALU.add))
            then(V.tensor_copy(words[:, 1:1 + GROUPS], word_f[:]))
            bits = (EXPERTS - 1).bit_length()
            then(V.tensor_scalar(table[:], words[:, 0:GROUPS], bits * (SLOTS8 - 2), None, ALU.logical_shift_right))
            then(V.tensor_scalar(words[:, 1:1 + GROUPS], words[:, 1:1 + GROUPS], 2 * bits, None, ALU.logical_shift_left))
            then(V.tensor_tensor(table[:], table[:], words[:, 1:1 + GROUPS], ALU.bitwise_or))
            dve.wait_ge(w13_parts, 2)
            V.memset(hidden[0][:, HID:3 * CHUNK], 0.0).then_inc(hidden_pad, 1)
            V.memset(hidden[1][:, HID:3 * CHUNK], 0.0).then_inc(table_ready, 1)

            def low_part(t, k):
                dve.wait_ge(x_hi_ready, t + 1)
                V.tensor_tensor(x_lo[k % 2][:], bank_a[k % 2][:, 0:P], x_hi[k % 2][:].bitcast(F32), ALU.subtract).then_inc(x_lo_ready, 1)

            def multiply(t, k):
                dve.wait_ge(silu_ready, t + 1)
                at_least(dve, hidden_turned, t - 1)
                V.tensor_tensor(hidden[k % 2][:, 0:HID], silu1[k % 2], bank_s[k % 2][:, H13 + HID:H13 + HID2], ALU.mult).then_inc(hidden_ready, 1)

            def keep_hiddenT(t, k):
                dve.wait_ge(hidden_turned, t + 1)
                at_least(dve, y_ready, t - 1)
                V.tensor_copy(hiddenT[k % 2][0:CHUNK], bank_c[0][0:CHUNK, 0:3 * P].rearrange("p (k n) -> p k n", n=P)).then_inc(hiddenT_ready, 1)

            def tile(t, k):
                multiply(t, k)
                if not isinstance(t, int) or t + 2 < FFN_TILES:
                    low_part(t + 2, (k + 2) % SLOTS8)
                if not isinstance(t, int) or t >= 1:
                    keep_hiddenT(t - 1, (k - 1) % SLOTS8)
                if not isinstance(t, int) or t + AHEAD + 1 < FFN_TILES:
                    ready_token(t + AHEAD + 1, (k + AHEAD + 1) % SLOTS8)
                if not isinstance(t, int) or t + 1 < FFN_TILES:
                    ready_result(t + 1, (k + 1) % SLOTS8)

            low_part(0, 0)
            low_part(1, 1)
            experts_loop(dve, tile)
            keep_hiddenT(FFN_TILES - 1, SLOTS8 - 1)

            def add_first(h):
                dve.wait_ge(y_loaded[h], 32)
                for j in range(4):
                    n = 4 * h + j
                    last = V.scalar_tensor_tensor(out=y_in[:, h, 0, j, :], in0=y_in[:, h, 0, j, :], scalar=gates[:, 0, n:n + 1],
                                                  in1=t2[:, n, :], op0=ALU.mult, op1=ALU.add)
                last.then_inc(y_added, 1)

            def keep_out(h):
                dve.wait_ge(y_turned, h + 1)
                V.tensor_copy(y_out[h], bank_a[h % 2][:, :]).then_inc(out_kept, 1)

            for h in range(HALVES):
                add_first(h)
                if h >= 1:
                    keep_out(h - 1)
            keep_out(HALVES - 1)

        @block.gpsimd
        def _(pool):
            G = nc.gpsimd
            G.memset(minus_half[:], -0.5).then_inc(pool_made, 1)
            pool.wait_ge(pool_made, 1)
            def rstds(i, which):
                tiles, step_ready = slice(4 * (which % 2), 4 * (which % 2) + 4), (3, 7, 19, 23)[which]
                pool.wait_ge(norm_step, i * NORM_STEPS + step_ready)
                G.tensor_tensor(rstd[:, tiles], var_eps[:, tiles], minus_half[:, tiles], ALU.pow).then_inc(rstd_ready, 1)

            def scatter_ids(i):
                wait_apart(pool, gate_step, i * GATE_STEPS + SLOT_STEP)
                for k in range(2 * TILES):
                    G.indirect_dma_start(ids_dram, bass.IndirectOffsetOnAxis(ap=slots[:, k:k + 1], axis=0),
                                         tok[:, k:k + 1], None).then_inc(ids_stored, 16)
                wait_apart(pool, ids_stored, 16 * 2 * TILES * (i + 1))
                G.tensor_scalar(tok[:], tok[:], float(N), None, ALU.add).then_inc(tok_step, 1)
                pool.wait_ge(tok_step, i + 2)

            pool.wait_ge(ids_cleared, 16)
            pool.wait_ge(loaded["attn"], 16 * 7)
            pool.wait_ge(loaded["tok"], 16)
            def image(i, first=False):
                for which in range(2):
                    rstds(i, which)
                for h in range(2):
                    wait_apart(pool, Cb[h].drained, Cb[h].after(i, "ln1"))
                G.tensor_copy(lnT_hi[:], lnT[:]).then_inc(lnT_split, 1)
                pool.wait_ge(lnT_split, 2 * i + 1)
                G.tensor_tensor(lnT_lo[:], lnT[:], lnT_hi[:].bitcast(F32), ALU.subtract).then_inc(lnT_split, 1)
                G.tensor_tensor(t1[:], t1[:], bpB_s[:].unsqueeze(1).broadcast_to([P, TILES, C]), ALU.add).then_inc(bias_added, 1)
                if not first:
                    scatter_ids(i - 1)
                for which in range(2, 4):
                    rstds(i, which)

            image(0, first=True)
            with pool.Fori(1, IMAGES) as i:
                image(i)
            pool.wait_ge(w13_parts, 1)
            G.tensor_tensor(w13_lo, w13_raw, w13_hi.bitcast(F32), ALU.subtract).then_inc(w13_parts, 1)

            def gather(t, k):
                if not isinstance(t, int) or t >= SLOTS8:
                    pool.wait_ge(x_turned, t - (SLOTS8 - 1))
                wait_apart(pool, slot_ready, t + 1)
                G.indirect_dma_start(x_rows[k], None, ln2_dram, bass.IndirectOffsetOnAxis(ap=tok_slot[:, k:k + 1], axis=0)).then_inc(gathered[k], 16)

            def scatter(t, k):
                wait_apart(pool, y_kept, t + 1)
                G.indirect_dma_start(y_dram, bass.IndirectOffsetOnAxis(ap=id_slot[:, k:k + 1], axis=0), y_rows[k], None).then_inc(scattered[k], 16)

            def tile(t, k):
                if not isinstance(t, int) or t + AHEAD < FFN_TILES:
                    gather(t + AHEAD, (k + AHEAD) % SLOTS8)
                scatter(t, k)

            pool.wait_ge(ids_stored, 16 * 2 * TILES * (IMAGES - 1))
            pool.wait_ge(ln2_stored, 16 * IMAGES + 16)
            pool.wait_ge(rows_ready, 1)
            G.indirect_dma_start(ids_rows[:], None, ids_dram.rearrange("(a b) c -> a (b c)", b=P),
                                 bass.IndirectOffsetOnAxis(ap=tile_row[0:FFN_TILES, :], axis=0)).then_inc(ids_loaded, 16)
            pool.wait_ge(w13_parts, 2)
            for t in range(AHEAD):
                gather(t, t)
            experts_loop(pool, tile)

def host_layout(np, ml, d):
    f = {k: np.ascontiguousarray(np.asarray(v)) for k, v in d.items()}
    images, c, hh, ww = f["x"].shape
    n = hh * ww
    tiles = n // P
    tokens = images * n
    dim, r = f["L1_attn_lunchbox"].shape
    heads = f["L1_attn_proj_w"].shape[0] // dim
    experts, hid, _ = f["L1_ffn_w1"].shape
    chunk = -(-hid // 3)
    ident = np.eye(P, dtype=np.float32)
    dqk = f["L0_conv_Wq"].shape[0]
    low = np.zeros((P, 1), np.float32)
    for k in (2, 3, 5, 7):
        low[k * dqk:(k + 1) * dqk] = -1.0
    e = np.arange(experts, dtype=np.float32)
    tri = np.concatenate([np.triu(np.ones((P, P)), 1), np.ones((P, P))], 1).astype(ml.bfloat16)
    tok = np.arange(2)[:, None, None] * tokens + np.arange(tiles)[None, :, None] * P + np.arange(P)[None, None, :]
    tok = tok.reshape(2 * tiles, P).T.astype(np.int32)
    cst = np.concatenate([ident, low, np.tile(experts - e, (P, 1)), np.tile(e * tokens, (P, 1)), np.tile(np.arange(FFN_MAX), (P, 1)),
                          np.arange(P)[:, None], np.tile(float(experts) ** (np.arange(FFN_MAX) % 8), (P, 1)),
                          np.tile(np.arange(P), (P, 1)), np.tile(tok[0] // P + (images - 1) * n // P, (P, 1))], 1).astype(np.float32)
    rows = np.arange(P)
    pad = [np.tile(2 * tokens + P * k + rows, tokens // P) for k in range(experts)]
    pad += [2 * tokens + P * (experts + k) + rows for k in range(experts)]
    pad = np.concatenate(pad).astype(np.int32).reshape(-1, (experts * (tokens + P)) // P)
    w = f["L1_attn_qkv_w"]
    bq, bv = f["L1_attn_qkv_b"][:heads * dim], f["L1_attn_qkv_b"][heads * dim:]
    w2 = np.transpose(f["L1_ffn_w2"], (2, 0, 1))
    w2p = np.zeros((3 * chunk, experts, c), np.float32)
    w2p[:hid] = w2
    return {
        "x": f["x"].reshape(images, c, n), "cst": cst, "tri": tri, "tokid": tok, "pad_ids": pad,
        "wqk": np.concatenate([f["L0_conv_Wq"].T] * 4 + [f["L0_conv_Wk"].T] * 4, 1),
        "bqk": np.concatenate([f["L0_conv_bq"]] * 4 + [f["L0_conv_bk"]] * 4)[:, None],
        "wvT": f["L0_conv_Wv"].T, "bvB": np.tile(f["L0_conv_bv"], (P, 1)), "gammaB": np.tile(f["L0_conv_gamma"], (P, 1)),
        "wq": w[:, :heads * dim], "bq": bq.reshape(heads, dim).T, "lunch": f["L1_attn_lunchbox"],
        "wvD": w[:, heads * dim:].T.reshape(heads, dim, c).transpose(1, 0, 2),
        "bvD": bv.reshape(heads, dim).T,
        "wp": f["L1_attn_proj_w"].reshape(heads, dim, c).transpose(1, 0, 2),
        "bpB": np.tile(f["L1_attn_proj_b"], (P, 1)), "routerT": f["L1_ffn_router_w"].T,
        "w13": np.concatenate([f["L1_ffn_w1"], f["L1_ffn_w3"]], 1).transpose(2, 0, 1),
        "w2T": w2p.reshape(3, chunk, experts, c).transpose(1, 0, 2, 3),
    }


_ORDER = ["x", "cst", "tri", "tokid", "pad_ids", "wqk", "bqk", "wvT", "bvB", "gammaB", "wq", "bq", "lunch", "wvD", "bvD", "wp",
          "bpB", "routerT", "w13", "w2T"]


def kernel(**inputs):
    import ml_dtypes
    import numpy as np
    import concourse.bacc as bacc
    from concourse.bass_utils import run_bass_kernel_spmd

    nc = bacc.Bacc("TRN2", target_bir_lowering=False, num_devices=1)
    layout = host_layout(np, ml_dtypes, inputs)
    arrays, args = {}, []
    for name in _ORDER:
        a = np.ascontiguousarray(layout[name])
        arrays[f"in_{name}_dram"] = a
        args.append(nc.dram_tensor(f"in_{name}_dram", a.shape, mybir.dt.from_np(a.dtype), kind="ExternalInput").ap())
    shape = inputs["x"].shape
    flat = (shape[0], shape[1], shape[2] * shape[3])
    args.append(nc.dram_tensor("out_0_dram", flat, F32, kind="ExternalOutput").ap())
    conv_attn_moe_kernel(nc, *args)
    r = run_bass_kernel_spmd(nc, [arrays], core_ids=[0])
    return r.results[0]["out_0_dram"].reshape(shape)
```
